# Optimizing a Trainium2 kernel written in Bass

```python
import numpy as np
import jax
import jax.numpy as jnp

def _softmax(x, axis=-1):
    return jax.nn.softmax(x, axis=axis)

def _gelu(x):
    return jax.nn.gelu(x, approximate=True)

def _silu(x):
    return jax.nn.silu(x)

def _sigmoid(x):
    return jax.nn.sigmoid(x)

def _layernorm(x, axis=-1, eps=1e-05):
    m = jnp.mean(x, axis=axis, keepdims=True)
    v = jnp.var(x, axis=axis, keepdims=True)
    return (x - m) / jnp.sqrt(v + eps)

def _scatter_add(tgt, idx, src, axis=0):
    return tgt.at[idx].add(src)

def _segment_sum(src, seg, n):
    return jax.ops.segment_sum(src, seg, n)
kernel_name = 'mk_conv_seq_d4_conv_nchw512_r4_b485a4'

def setup_inputs(seed: int=0):
    np.random.seed(seed)
    _w = jnp.asarray

    def _rec_inputs():
        import jax
        import jax.numpy as jnp
        _gk = jax.random.key(seed)
        x = -0.0002928 + 1 * jax.random.normal(jax.random.fold_in(_gk, 1), (2, 128, 16, 16), jnp.float32)
        return x
    x = _rec_inputs()

    def _L0_conv_setup():
        import jax, jax.numpy as jnp
        import numpy as np
        C = 128
        B, H, W = (2, 16, 16)
        G = 32
        EPS = 1e-06

        def _group_norm(x, gamma, beta):
            b, c, h, w = x.shape
            xr = x.reshape(b, G, c // G * h * w)
            mu = jnp.mean(xr, axis=-1, keepdims=True)
            var = jnp.var(xr, axis=-1, keepdims=True)
            xn = ((xr - mu) * jax.lax.rsqrt(var + EPS)).reshape(b, c, h, w)
            return xn * gamma[None, :, None, None] + beta[None, :, None, None]
        key = jax.random.key(seed)
        ks = jax.random.split(key, 6)
        s = 1.0 / np.sqrt(C)
        return {'x': jax.random.normal(ks[0], (B, C, H, W), dtype=jnp.float32), 'gamma': jnp.ones((C,), jnp.float32), 'beta': jnp.zeros((C,), jnp.float32), 'wq': jax.random.normal(ks[1], (C, C), jnp.float32) * s, 'bq': jnp.zeros((C,), jnp.float32), 'wk': jax.random.normal(ks[2], (C, C), jnp.float32) * s, 'bk': jnp.zeros((C,), jnp.float32), 'wv': jax.random.normal(ks[3], (C, C), jnp.float32) * s, 'bv': jnp.zeros((C,), jnp.float32), 'wp': jax.random.normal(ks[4], (C, C), jnp.float32) * s, 'bp': jnp.zeros((C,), jnp.float32)}
    _L0_conv_all = _L0_conv_setup()
    _L0_conv_in = {k: v for k, v in _L0_conv_all.items() if k in ('gamma', 'beta', 'wq', 'bq', 'wk', 'bk', 'wv', 'bv', 'wp', 'bp')}
    del _L0_conv_all

    def _L1_conv_setup():
        import jax, jax.numpy as jnp
        import numpy as np
        B, C, H, W = (4, 128, 16, 16)
        CQ = C // 8
        key = jax.random.key(seed)
        ks = jax.random.split(key, 9)
        s = 0.02
        return {'x': jax.random.normal(ks[0], (B, C, H, W), jnp.float32), 'Wq': jax.random.normal(ks[1], (CQ, C), jnp.float32) * s, 'bq': jax.random.normal(ks[2], (CQ,), jnp.float32) * s, 'Wk': jax.random.normal(ks[3], (CQ, C), jnp.float32) * s, 'bk': jax.random.normal(ks[4], (CQ,), jnp.float32) * s, 'Wv': jax.random.normal(ks[5], (C, C), jnp.float32) * s, 'bv': jax.random.normal(ks[6], (C,), jnp.float32) * s, 'gamma_pam': jax.random.normal(ks[7], (1,), jnp.float32) * 0.1, 'gamma_cam': jax.random.normal(ks[8], (1,), jnp.float32) * 0.1}
    _L1_conv_all = _L1_conv_setup()
    _L1_conv_in = {k: v for k, v in _L1_conv_all.items() if k in ('Wq', 'bq', 'Wk', 'bk', 'Wv', 'bv', 'gamma_pam', 'gamma_cam')}
    del _L1_conv_all

    def _L2_conv_setup():
        import jax, jax.numpy as jnp
        import numpy as np
        FREQ_DIM = 32
        TIME_DIM = 32
        HEADS = 8
        TWO_PI = 6.283185307179586

        def get_embeddings(B, H, W, freq_dim, time_dim, dtype):
            nf = freq_dim // 2
            ln_x = jnp.log2(jnp.arange(0, H * nf, dtype=jnp.float32))
            ln_x = ln_x.at[0].set(-2.0)
            ln_x = ln_x.reshape(H, nf).T
            ln_x = ln_x * jnp.arange(1, nf + 1, dtype=jnp.float32)[:, None]
            freq = jnp.stack([jnp.cos(ln_x), jnp.sin(ln_x)], axis=1).reshape(freq_dim, H)
            freq = jnp.broadcast_to(freq[None, :, :, None], (B, freq_dim, H, W))
            nt = time_dim // 2
            k = jnp.arange(0, nt, dtype=jnp.float32) + 0.5
            x = jnp.arange(0, nt * W, dtype=jnp.float32).reshape(W, nt).T
            theta = k[:, None] * x / (W * nt) * TWO_PI
            time = jnp.stack([jnp.cos(theta), jnp.sin(theta)], axis=1).reshape(time_dim, W)
            time = jnp.broadcast_to(time[None, :, None, :], (B, time_dim, H, W))
            return jnp.concatenate([freq, time], axis=1).astype(dtype)
        key = jax.random.key(seed)
        ks = jax.random.split(key, 6)
        B, C, H, W = (2, 128, 16, 32)
        qkC = C + FREQ_DIM + TIME_DIM
        inner = HEADS * 16
        return {'hidden_states': jax.random.normal(ks[0], (B, C, H, W), dtype=jnp.float32), 'Wq': jax.random.normal(ks[1], (qkC, inner), dtype=jnp.float32) * 0.02, 'Wk': jax.random.normal(ks[2], (qkC, inner), dtype=jnp.float32) * 0.02, 'Wv': jax.random.normal(ks[3], (C, inner), dtype=jnp.float32) * 0.02, 'Wout': jax.random.normal(ks[4], (inner, C), dtype=jnp.float32) * 0.02, 'bout': jnp.zeros((C,), dtype=jnp.float32)}
    _L2_conv_all = _L2_conv_setup()
    _L2_conv_in = {k: v for k, v in _L2_conv_all.items() if k in ('Wq', 'Wk', 'Wv', 'Wout', 'bout')}
    del _L2_conv_all

    def _L3_conv_setup():
        import jax, jax.numpy as jnp
        import numpy as np
        from jax import lax
        HEADS = 8
        DIM_HEAD = 16
        EPS = 1e-05

        def chan_ln(x, g):
            mean = jnp.mean(x, axis=1, keepdims=True)
            var = jnp.var(x, axis=1, keepdims=True)
            return (x - mean) * lax.rsqrt(var + EPS) * g[None]

        def conv1x1(x, w):
            return jnp.einsum('bchw,oc->bohw', x, w)

        def dwconv3x3(x, w):
            return lax.conv_general_dilated(x, w, window_strides=(1, 1), padding='SAME', feature_group_count=x.shape[1], dimension_numbers=('NCHW', 'OIHW', 'NCHW'))

        def linear_attn_block(x, norm_g, q_w, q_dw, k_w, k_dw, v_w, v_dw, out_w, out_norm_g, ff_g1, ff_w1, ff_g2, ff_w2):
            B, C, H, W = x.shape
            h, d = (HEADS, DIM_HEAD)
            scale = d ** (-0.5)
            f = chan_ln(x, norm_g)
            q = dwconv3x3(conv1x1(f, q_w), q_dw)
            k = dwconv3x3(conv1x1(f, k_w), k_dw)
            v = dwconv3x3(conv1x1(f, v_w), v_dw)

            def to_heads(t):
                return t.reshape(B, h, d, H * W).transpose(0, 1, 3, 2).reshape(B * h, H * W, d)
            q, k, v = map(to_heads, (q, k, v))
            q = jax.nn.softmax(q, axis=-1) * scale
            k = jax.nn.softmax(k, axis=-2)
            ctx = jnp.einsum('bnd,bne->bde', k, v)
            out = jnp.einsum('bnd,bde->bne', q, ctx)
            out = out.reshape(B, h, H * W, d).transpose(0, 1, 3, 2).reshape(B, h * d, H, W)
            out = jax.nn.silu(out)
            out = chan_ln(conv1x1(out, out_w), out_norm_g)
            x = out + x
            hdn = conv1x1(chan_ln(x, ff_g1), ff_w1)
            hdn = jax.nn.gelu(hdn, approximate=False)
            ff_out = conv1x1(chan_ln(hdn, ff_g2), ff_w2)
            return ff_out + x
        key = jax.random.key(seed)
        ks = jax.random.split(key, 10)
        B, C, H, W = (8, 128, 16, 16)
        inner = HEADS * DIM_HEAD
        hidden = 2 * C
        s_c = 1.0 / np.sqrt(C)
        s_i = 1.0 / np.sqrt(inner)
        s_h = 1.0 / np.sqrt(hidden)
        return {'x': jax.random.normal(ks[0], (B, C, H, W), jnp.float32), 'norm_g': jnp.ones((C, 1, 1), jnp.float32), 'q_w': jax.random.normal(ks[1], (inner, C), jnp.float32) * s_c, 'q_dw': jax.random.normal(ks[2], (inner, 1, 3, 3), jnp.float32) * (1.0 / 3.0), 'k_w': jax.random.normal(ks[3], (inner, C), jnp.float32) * s_c, 'k_dw': jax.random.normal(ks[4], (inner, 1, 3, 3), jnp.float32) * (1.0 / 3.0), 'v_w': jax.random.normal(ks[5], (inner, C), jnp.float32) * s_c, 'v_dw': jax.random.normal(ks[6], (inner, 1, 3, 3), jnp.float32) * (1.0 / 3.0), 'out_w': jax.random.normal(ks[7], (C, inner), jnp.float32) * s_i, 'out_norm_g': jnp.ones((C, 1, 1), jnp.float32), 'ff_g1': jnp.ones((C, 1, 1), jnp.float32), 'ff_w1': jax.random.normal(ks[8], (hidden, C), jnp.float32) * s_c, 'ff_g2': jnp.ones((hidden, 1, 1), jnp.float32), 'ff_w2': jax.random.normal(ks[9], (C, hidden), jnp.float32) * s_h}
    _L3_conv_all = _L3_conv_setup()
    _L3_conv_in = {k: v for k, v in _L3_conv_all.items() if k in ('norm_g', 'q_w', 'q_dw', 'k_w', 'k_dw', 'v_w', 'v_dw', 'out_w', 'out_norm_g', 'ff_g1', 'ff_w1', 'ff_g2', 'ff_w2')}
    del _L3_conv_all
    return {'x': x, 'L0_conv_gamma': _L0_conv_in['gamma'], 'L0_conv_beta': _L0_conv_in['beta'], 'L0_conv_wq': _L0_conv_in['wq'], 'L0_conv_bq': _L0_conv_in['bq'], 'L0_conv_wk': _L0_conv_in['wk'], 'L0_conv_bk': _L0_conv_in['bk'], 'L0_conv_wv': _L0_conv_in['wv'], 'L0_conv_bv': _L0_conv_in['bv'], 'L0_conv_wp': _L0_conv_in['wp'], 'L0_conv_bp': _L0_conv_in['bp'], 'L1_conv_Wq': _L1_conv_in['Wq'], 'L1_conv_bq': _L1_conv_in['bq'], 'L1_conv_Wk': _L1_conv_in['Wk'], 'L1_conv_bk': _L1_conv_in['bk'], 'L1_conv_Wv': _L1_conv_in['Wv'], 'L1_conv_bv': _L1_conv_in['bv'], 'L1_conv_gamma_pam': _L1_conv_in['gamma_pam'], 'L1_conv_gamma_cam': _L1_conv_in['gamma_cam'], 'L2_conv_Wq': _L2_conv_in['Wq'], 'L2_conv_Wk': _L2_conv_in['Wk'], 'L2_conv_Wv': _L2_conv_in['Wv'], 'L2_conv_Wout': _L2_conv_in['Wout'], 'L2_conv_bout': _L2_conv_in['bout'], 'L3_conv_norm_g': _L3_conv_in['norm_g'], 'L3_conv_q_w': _L3_conv_in['q_w'], 'L3_conv_q_dw': _L3_conv_in['q_dw'], 'L3_conv_k_w': _L3_conv_in['k_w'], 'L3_conv_k_dw': _L3_conv_in['k_dw'], 'L3_conv_v_w': _L3_conv_in['v_w'], 'L3_conv_v_dw': _L3_conv_in['v_dw'], 'L3_conv_out_w': _L3_conv_in['out_w'], 'L3_conv_out_norm_g': _L3_conv_in['out_norm_g'], 'L3_conv_ff_g1': _L3_conv_in['ff_g1'], 'L3_conv_ff_w1': _L3_conv_in['ff_w1'], 'L3_conv_ff_g2': _L3_conv_in['ff_g2'], 'L3_conv_ff_w2': _L3_conv_in['ff_w2']}

def reference(x, L0_conv_gamma, L0_conv_beta, L0_conv_wq, L0_conv_bq, L0_conv_wk, L0_conv_bk, L0_conv_wv, L0_conv_bv, L0_conv_wp, L0_conv_bp, L1_conv_Wq, L1_conv_bq, L1_conv_Wk, L1_conv_bk, L1_conv_Wv, L1_conv_bv, L1_conv_gamma_pam, L1_conv_gamma_cam, L2_conv_Wq, L2_conv_Wk, L2_conv_Wv, L2_conv_Wout, L2_conv_bout, L3_conv_norm_g, L3_conv_q_w, L3_conv_q_dw, L3_conv_k_w, L3_conv_k_dw, L3_conv_v_w, L3_conv_v_dw, L3_conv_out_w, L3_conv_out_norm_g, L3_conv_ff_g1, L3_conv_ff_w1, L3_conv_ff_g2, L3_conv_ff_w2):
    import jax
    import jax.numpy as jnp

    def _L0_conv_ref(x, gamma, beta, wq, bq, wk, bk, wv, bv, wp, bp):
        import jax, jax.numpy as jnp
        import numpy as np
        C = 128
        B, H, W = (2, 16, 16)
        G = 32
        EPS = 1e-06

        def _group_norm(x, gamma, beta):
            b, c, h, w = x.shape
            xr = x.reshape(b, G, c // G * h * w)
            mu = jnp.mean(xr, axis=-1, keepdims=True)
            var = jnp.var(xr, axis=-1, keepdims=True)
            xn = ((xr - mu) * jax.lax.rsqrt(var + EPS)).reshape(b, c, h, w)
            return xn * gamma[None, :, None, None] + beta[None, :, None, None]
        b, c, h, w = x.shape
        hw = h * w
        hn = _group_norm(x, gamma, beta).reshape(b, c, hw)
        q = jnp.einsum('oc,bcn->bon', wq, hn) + bq[None, :, None]
        k = jnp.einsum('oc,bcn->bon', wk, hn) + bk[None, :, None]
        v = jnp.einsum('oc,bcn->bon', wv, hn) + bv[None, :, None]
        scale = jnp.float32(c) ** (-0.5)
        attn = jax.nn.softmax(jnp.einsum('bci,bcj->bij', q, k) * scale, axis=-1)
        hattn = jnp.einsum('bcj,bij->bci', v, attn)
        out = jnp.einsum('oc,bcn->bon', wp, hattn) + bp[None, :, None]
        return out.reshape(b, c, h, w) + x

    def _L1_conv_ref(x, Wq, bq, Wk, bk, Wv, bv, gamma_pam, gamma_cam):
        import jax, jax.numpy as jnp
        import numpy as np
        B, C, H, W = (4, 128, 16, 16)
        CQ = C // 8
        b, c, h, w = x.shape
        n = h * w
        xf = x.reshape(b, c, n)
        q = jnp.einsum('oc,bcn->bon', Wq, xf) + bq[None, :, None]
        k = jnp.einsum('oc,bcn->bon', Wk, xf) + bk[None, :, None]
        v = jnp.einsum('oc,bcn->bon', Wv, xf) + bv[None, :, None]
        energy = jnp.einsum('bdi,bdj->bij', q, k)
        att = jax.nn.softmax(energy, axis=-1)
        pout = jnp.einsum('bcj,bij->bci', v, att)
        pam = gamma_pam[0] * pout.reshape(b, c, h, w) + x
        pf = pam.reshape(b, c, n)
        cen = jnp.einsum('bci,bdi->bcd', pf, pf)
        cen_new = jnp.max(cen, axis=-1, keepdims=True) - cen
        catt = jax.nn.softmax(cen_new, axis=-1)
        cout = jnp.einsum('bcd,bdn->bcn', catt, pf)
        out = gamma_cam[0] * cout.reshape(b, c, h, w) + pam
        return out

    def _L2_conv_ref(hidden_states, Wq, Wk, Wv, Wout, bout):
        import jax, jax.numpy as jnp
        import numpy as np
        FREQ_DIM = 32
        TIME_DIM = 32
        HEADS = 8
        TWO_PI = 6.283185307179586

        def get_embeddings(B, H, W, freq_dim, time_dim, dtype):
            nf = freq_dim // 2
            ln_x = jnp.log2(jnp.arange(0, H * nf, dtype=jnp.float32))
            ln_x = ln_x.at[0].set(-2.0)
            ln_x = ln_x.reshape(H, nf).T
            ln_x = ln_x * jnp.arange(1, nf + 1, dtype=jnp.float32)[:, None]
            freq = jnp.stack([jnp.cos(ln_x), jnp.sin(ln_x)], axis=1).reshape(freq_dim, H)
            freq = jnp.broadcast_to(freq[None, :, :, None], (B, freq_dim, H, W))
            nt = time_dim // 2
            k = jnp.arange(0, nt, dtype=jnp.float32) + 0.5
            x = jnp.arange(0, nt * W, dtype=jnp.float32).reshape(W, nt).T
            theta = k[:, None] * x / (W * nt) * TWO_PI
            time = jnp.stack([jnp.cos(theta), jnp.sin(theta)], axis=1).reshape(time_dim, W)
            time = jnp.broadcast_to(time[None, :, None, :], (B, time_dim, H, W))
            return jnp.concatenate([freq, time], axis=1).astype(dtype)
        B, C, H, W = hidden_states.shape
        emb = get_embeddings(B, H, W, FREQ_DIM, TIME_DIM, hidden_states.dtype)
        qk_hs = jnp.concatenate([hidden_states, emb], axis=1)
        S = H * W
        qk_hs = qk_hs.reshape(B, -1, S).transpose(0, 2, 1)
        v_hs = hidden_states.reshape(B, C, S).transpose(0, 2, 1)
        q = qk_hs @ Wq
        k = qk_hs @ Wk
        v = v_hs @ Wv
        hd_qk = q.shape[-1] // HEADS
        hd_v = v.shape[-1] // HEADS
        q = q.reshape(B, S, HEADS, hd_qk).transpose(0, 2, 1, 3)
        k = k.reshape(B, S, HEADS, hd_qk).transpose(0, 2, 1, 3)
        v = v.reshape(B, S, HEADS, hd_v).transpose(0, 2, 1, 3)
        scale = 1.0 / jnp.sqrt(jnp.asarray(hd_qk, dtype=q.dtype))
        scores = jnp.einsum('bhqd,bhkd->bhqk', q, k) * scale
        attn = jax.nn.softmax(scores, axis=-1)
        o = jnp.einsum('bhqk,bhkd->bhqd', attn, v)
        o = o.transpose(0, 2, 1, 3).reshape(B, S, HEADS * hd_v)
        o = o @ Wout + bout
        o = o.transpose(0, 2, 1).reshape(B, C, H, W)
        return o + hidden_states

    def _L3_conv_ref(x, norm_g, q_w, q_dw, k_w, k_dw, v_w, v_dw, out_w, out_norm_g, ff_g1, ff_w1, ff_g2, ff_w2):
        import jax, jax.numpy as jnp
        import numpy as np
        from jax import lax
        HEADS = 8
        DIM_HEAD = 16
        EPS = 1e-05

        def chan_ln(x, g):
            mean = jnp.mean(x, axis=1, keepdims=True)
            var = jnp.var(x, axis=1, keepdims=True)
            return (x - mean) * lax.rsqrt(var + EPS) * g[None]

        def conv1x1(x, w):
            return jnp.einsum('bchw,oc->bohw', x, w)

        def dwconv3x3(x, w):
            return lax.conv_general_dilated(x, w, window_strides=(1, 1), padding='SAME', feature_group_count=x.shape[1], dimension_numbers=('NCHW', 'OIHW', 'NCHW'))

        def linear_attn_block(x, norm_g, q_w, q_dw, k_w, k_dw, v_w, v_dw, out_w, out_norm_g, ff_g1, ff_w1, ff_g2, ff_w2):
            B, C, H, W = x.shape
            h, d = (HEADS, DIM_HEAD)
            scale = d ** (-0.5)
            f = chan_ln(x, norm_g)
            q = dwconv3x3(conv1x1(f, q_w), q_dw)
            k = dwconv3x3(conv1x1(f, k_w), k_dw)
            v = dwconv3x3(conv1x1(f, v_w), v_dw)

            def to_heads(t):
                return t.reshape(B, h, d, H * W).transpose(0, 1, 3, 2).reshape(B * h, H * W, d)
            q, k, v = map(to_heads, (q, k, v))
            q = jax.nn.softmax(q, axis=-1) * scale
            k = jax.nn.softmax(k, axis=-2)
            ctx = jnp.einsum('bnd,bne->bde', k, v)
            out = jnp.einsum('bnd,bde->bne', q, ctx)
            out = out.reshape(B, h, H * W, d).transpose(0, 1, 3, 2).reshape(B, h * d, H, W)
            out = jax.nn.silu(out)
            out = chan_ln(conv1x1(out, out_w), out_norm_g)
            x = out + x
            hdn = conv1x1(chan_ln(x, ff_g1), ff_w1)
            hdn = jax.nn.gelu(hdn, approximate=False)
            ff_out = conv1x1(chan_ln(hdn, ff_g2), ff_w2)
            return ff_out + x
        return linear_attn_block(x, norm_g, q_w, q_dw, k_w, k_dw, v_w, v_dw, out_w, out_norm_g, ff_g1, ff_w1, ff_g2, ff_w2)

    def _gn(v, G=32, eps=1e-05):
        B_, C_, H_, W_ = v.shape
        g = v.reshape(B_, G, C_ // G, H_, W_)
        m = jnp.mean(g, axis=(2, 3, 4), keepdims=True)
        s = jnp.var(g, axis=(2, 3, 4), keepdims=True)
        return ((g - m) / jnp.sqrt(s + eps)).reshape(v.shape)

    def _ln_c(v, eps=1e-06):
        m = jnp.mean(v, axis=1, keepdims=True)
        s = jnp.var(v, axis=1, keepdims=True)
        return (v - m) / jnp.sqrt(s + eps)

    def _ln_t(v, eps=1e-05):
        m = jnp.mean(v, axis=-1, keepdims=True)
        s = jnp.var(v, axis=-1, keepdims=True)
        return (v - m) / jnp.sqrt(s + eps)

    def _to_tokens(v):
        B_, C_, H_, W_ = v.shape
        return v.reshape(B_, C_, H_ * W_).transpose(0, 2, 1)

    def _from_tokens(t, like):
        B_, C_, H_, W_ = like.shape
        return t.transpose(0, 2, 1).reshape(B_, C_, H_, W_)
    x = _L0_conv_ref(x, L0_conv_gamma, L0_conv_beta, L0_conv_wq, L0_conv_bq, L0_conv_wk, L0_conv_bk, L0_conv_wv, L0_conv_bv, L0_conv_wp, L0_conv_bp)
    x = _L1_conv_ref(x, L1_conv_Wq, L1_conv_bq, L1_conv_Wk, L1_conv_bk, L1_conv_Wv, L1_conv_bv, L1_conv_gamma_pam, L1_conv_gamma_cam)
    x = _L2_conv_ref(x, L2_conv_Wq, L2_conv_Wk, L2_conv_Wv, L2_conv_Wout, L2_conv_bout)
    x = _L3_conv_ref(x, L3_conv_norm_g, L3_conv_q_w, L3_conv_q_dw, L3_conv_k_w, L3_conv_k_dw, L3_conv_v_w, L3_conv_v_dw, L3_conv_out_w, L3_conv_out_norm_g, L3_conv_ff_g1, L3_conv_ff_w1, L3_conv_ff_g2, L3_conv_ff_w2)
    return x

_drawn_inputs = setup_inputs


def setup_inputs(seed=0):
    import zlib

    import numpy as np

    out = dict(_drawn_inputs(seed))
    spreads = {'L0_conv_gamma': (1.0, 0.2),
     'L0_conv_beta': (0.0, 0.1),
     'L0_conv_bq': (0.0, 0.1),
     'L0_conv_bk': (0.0, 2.0),
     'L0_conv_bv': (0.0, 0.1),
     'L0_conv_bp': (0.0, 0.1),
     'L2_conv_bout': (0.0, 0.1),
     'L3_conv_norm_g': (1.0, 0.2),
     'L3_conv_out_norm_g': (1.0, 0.2),
     'L3_conv_ff_g1': (1.0, 0.2),
     'L3_conv_ff_g2': (1.0, 0.2)}
    factors = {'L1_conv_Wq': 48.346,
     'L1_conv_bq': 64.0,
     'L1_conv_Wk': 47.886,
     'L1_conv_bk': 64.0,
     'L1_conv_Wv': 36.704,
     'L1_conv_bv': 64.0,
     'L2_conv_Wq': 8.0,
     'L2_conv_Wk': 8.0}
    for name, (base, spread) in spreads.items():
        noise = np.random.default_rng([zlib.crc32(name.encode()), seed]).standard_normal(out[name].shape)
        drawn = base * np.exp(spread * noise) if base else spread * noise
        out[name] = jnp.asarray(drawn.astype(out[name].dtype))
    for name, factor in factors.items():
        out[name] = (out[name] * factor).astype(out[name].dtype)
    return out
```

```python
import concourse.bass as bass
from concourse import mybir
from contextlib import ExitStack

NB = 2
C = 128
H = W = 16
N = H * W
NT = N // 128
CQ = C // 8
HEADS, D = 8, 16
QUAD = 32
HG = C // QUAD
NG = HEADS // HG
EMB = 64
HID = 2 * C
TAPS = 9
GN_GROUP = 4
EPS_GN, EPS_LN = 1e-6, 1e-5

PACK_A = [("ident", C), ("gmean", C), ("wqT0", C), ("wkT0", C), ("wv0", C), ("wpT0", C),
          ("gamma", 1), ("beta", 1), ("bq0", 1), ("bk0", 1), ("bv0", 1), ("bp0", 1),
          ("bq1", 1), ("bk1", 1), ("bv1", 1), ("gpam", 1), ("gcam", 1), ("bout", 1),
          ("norm_g", 1), ("out_norm_g", 1), ("ff_g1", 1), ("ff_g2", 2)]
PACK_B = [("wqT1", CQ), ("wkT1", CQ), ("wvT1", C),
          ("wqx", NG * C), ("wkx", NG * C), ("wqe", NG * C), ("wke", NG * C), ("emb", N),
          ("wvx", NG * C), ("woutp", NG * C)]
PACK_C = [("w1x1T", 3 * C), ("cmean", C), ("headmask", C), ("outwT", C), ("w1T", HID), ("w2T", HID)]


def places(pack):
    at, out = 0, {}
    for name, width in pack:
        out[name] = (at, at + width)
        at += width
    return out, at


def build(nc, x, pack_a, pack_b, pack_c, taps, out):
    fp32 = mybir.dt.float32
    ALU = mybir.AluOpType
    ACT = mybir.ActivationFunctionType
    AX = mybir.AxisListType

    with ExitStack() as ctx:
        def sb(name, shape):
            return ctx.enter_context(nc.sbuf_tensor(name, shape, fp32))

        def sem(name):
            return ctx.enter_context(nc.semaphore(name))

        at_a, width_a = places(PACK_A)
        at_b, width_b = places(PACK_B)
        at_c, width_c = places(PACK_C)
        wa, wb, wc = sb("wa", [128, width_a]), sb("wb", [128, width_b]), sb("wc", [128, width_c])

        def A(name):
            return wa[:, at_a[name][0]:at_a[name][1]]

        def B(name):
            return wb[:, at_b[name][0]:at_b[name][1]]

        def K(name):
            return wc[:, at_c[name][0]:at_c[name][1]]

        ident = A("ident")
        tapw = sb("tapw", [128, TAPS * 3 * C])
        convw = sb("convw", [128, TAPS, 3, C])
        wg = sb("wg", [128, 3 * C])
        wpvT = sb("wpvT", [128, C])
        bias0 = sb("bias0", [128, 1])
        gbv = sb("gbv", [128, 1])
        outwc = sb("outwc", [128, C])
        outws = sb("outws", [128, 2])
        w1c = sb("w1c", [128, HID])
        w1g = sb("w1g", [128, HID])
        w2c = sb("w2c", [128, 2, C])
        w2g = sb("w2g", [128, 2, C])
        mhalf = sb("mhalf", [128, 4])

        def per_batch(name, shape):
            return [sb(f"{name}_{b}", shape) for b in range(NB)]

        x0 = per_batch("x0", [128, N])
        st0 = per_batch("st0", [128, 6])
        mv0 = per_batch("mv0", [128, 2])
        gs0 = per_batch("gs0", [128, 2])
        sm0 = per_batch("sm0", [128, 8])
        hn0 = per_batch("hn0", [128, N])
        xb0 = per_batch("xb0", [128, N])
        q0, k0 = per_batch("q0", [128, N]), per_batch("k0", [128, N])
        v0 = per_batch("v0", [128, NT, C])
        nmax = per_batch("nmax", [128, 2 * NT])
        psum_ = per_batch("sums", [128, 2 * NT])
        rsum = per_batch("rsum", [128, 2 * NT])
        p0, pT0 = per_batch("p0", [128, NT, N]), per_batch("pT0", [128, NT, N])
        rb0, t0, x1 = per_batch("rb0", [128, N]), per_batch("t0", [128, N]), per_batch("x1", [128, N])
        xb1 = per_batch("xb1", [128, N])
        q1, k1 = per_batch("q1", [CQ, N]), per_batch("k1", [CQ, N])
        v1 = per_batch("v1", [128, NT, C])
        p1, pT1 = per_batch("p1", [128, NT, N]), per_batch("pT1", [128, NT, N])
        rb1, t1, pam = per_batch("rb1", [128, N]), per_batch("t1", [128, N]), per_batch("pam", [128, N])
        pamT = per_batch("pamT", [128, NT, C])
        cmin, csum, cscale = per_batch("cmin", [128, 1]), per_batch("csum", [128, 1]), per_batch("cscale", [128, 2])
        ce, ceT = per_batch("ce", [128, C]), per_batch("ceT", [128, C])
        x2, xb2 = per_batch("x2", [128, N]), per_batch("xb2", [128, N])
        q2, k2 = per_batch("q2", [128, NG, N]), per_batch("k2", [128, NG, N])
        v2 = per_batch("v2", [128, NT, NG * C])
        nmax2 = per_batch("nmax2", [128, HEADS, 2 * NT])
        sum2, rsum2 = per_batch("sum2", [128, NT, HEADS]), per_batch("rsum2", [128, NT, HEADS])
        rsx2 = per_batch("rsx2", [128, NT, HEADS, QUAD])
        P2_RING, PT2_RING = 3, 2 * HG
        p2 = [sb(f"p2_{i}", [128, NT, N]) for i in range(P2_RING)]
        pT2 = [sb(f"pT2_{i}", [128, NT, N]) for i in range(PT2_RING)]
        rb2, o2 = per_batch("rb2", [128, NG, N]), per_batch("o2", [128, NG, N])
        x3, xc3 = per_batch("x3", [128, N]), per_batch("xc3", [128, N])
        st3 = per_batch("st3", [128, 4, NT, 6])
        mv3 = per_batch("mv3", [128, 4, NT, 2])
        ve3 = per_batch("ve3", [128, 4, NT])
        rs3 = per_batch("rs3", [128, 4, NT])
        fsh = [per_batch(f"fsh{dx}", [128, H + 2, W]) for dx in range(3)]
        nmk, sumk, rsk = per_batch("nmk", [128, 1]), per_batch("sumk", [128, 1]), per_batch("rsk", [128, 2])
        ek, ekT = per_batch("ek", [128, N]), per_batch("ekT", [128, NT, C])
        v3 = per_batch("v3", [128, NT, C])
        mq, sq, rq = (per_batch(n, [128, NT, HEADS]) for n in ("mq", "sq", "rq"))
        qs, eq, qn = (per_batch(n, [128, NT, HEADS, D]) for n in ("qs", "eq", "qn"))
        qT, cm = per_batch("qT", [128, N]), per_batch("cm", [128, C])
        th, s3 = per_batch("th", [128, N]), per_batch("s3", [128, N])
        ycg, x4a, x4 = per_batch("ycg", [128, N]), per_batch("x4a", [128, N]), per_batch("x4", [128, N])
        h3, hT3 = per_batch("h3", [128, NT, HID]), per_batch("hT3", [128, 2, N])
        rb4, fo, y = per_batch("rb4", [128, N]), per_batch("fo", [128, N]), per_batch("y", [128, N])

        bank = [ctx.enter_context(nc.psum_tensor(f"bank{i}", [128, 512], fp32)) for i in range(8)]

        def tiles(t, n=NT):
            return t[:, :].rearrange("p (t c) -> p t c", t=n)

        NAMES = """vec a_in x_in b_in c_in tap_in zeroed mhalf_set wg_done conv_w wpv_p wpv_w bias0_w gbv_w outw_c w1g_w             w1c_w w2g_w w2m_p w2c_w  gin0_d g0_p ve0_d rstd0_d hn0_d q0_p k0_p v0_p q0_d k0_d v0_d s0_p
            max0_d e0_d rs0_d t0_p pT0_d rb0_p rb0_d pv0_p x1_d q1_p k1_p v1_p q1_d k1_d v1_d s1_p max1_d e1_d
            rsg1_d t1_p pT1_d rb1_p rb1_d pv1_p pam_d pamT_p pamT_d cen_p min_d ce_d ceT_p ceT_d co_p x2_d q2_p
            k2_p v2_p q2_d k2_d v2_d s2_p nb2_d e2_d t2_p pT2e_d pT2o_d pv2_p rs2_d rsx2_d f0_d f2_d rb2_p rb2_d o2_d w2_p x3_d
            x3T_p ve3_d rs3_d mean3_p xc3_d rb3_p f_d k3_p k3m_d ek_d ekT_p ekT_d qv_p v3_d qs_d eq_d qn_d qT_p
            qT_d ctx_p cm_d o3_p th_d s3_d yc_p yT_p ycg_d ve4_d rs4_d rb4_p x4_d x4T_p ve5_d rs5_d h_p h_d
            ve6_d rs6_d rb6_p rb6_d hT_p hT_d ff_p y_d stored""".split()
        s = {n: sem(n) for n in NAMES}
        block = ctx.enter_context(nc.Block())

        @block.sync
        def _(sp):
            sp.dma_start(x0[0][:, :], x[0].rearrange("c h w -> c (h w)")).then_inc(s["x_in"], 16)
            sp.dma_start(wa[:, :], pack_a).then_inc(s["a_in"], 16)
            sp.dma_start(wb[:, :], pack_b).then_inc(s["b_in"], 16)
            sp.dma_start(wc[:, :], pack_c).then_inc(s["c_in"], 16)
            for b in range(NB):
                sp.wait_ge(s["y_d"], b + 1)
                sp.dma_start(out[b].rearrange("c h w -> c (h w)"), y[b][:, :]).then_inc(s["stored"], 16)
            sp.wait_ge(s["stored"], 16 * NB)

        @block.gpsimd
        def _(pool):
            nc.gpsimd.memset(mhalf[:, :], -0.5).then_inc(s["mhalf_set"], 1)
            for b in range(NB):
                for dx in range(3):
                    nc.gpsimd.memset(fsh[dx][b][:, :, :], 0.0).then_inc(s["zeroed"], 1)
            pool.wait_ge(s["mhalf_set"], 1)

            def inverse_root(dst, src, ready, done, b, width):
                pool.wait_ge(ready, b + 1)
                nc.gpsimd.tensor_tensor(dst, src, mhalf[:, 0:width], ALU.pow).then_inc(done, 1)

            for b in range(NB):
                inverse_root(sm0[b][:, 2:3], sm0[b][:, 1:2], s["ve0_d"], s["rstd0_d"], b, 1)
            pool.wait_ge(s["wg_done"], 1)
            pool.wait_ge(s["tap_in"], 16)
            for t in range(TAPS):
                nc.gpsimd.tensor_tensor(convw[:, t, :, :].rearrange("p a o -> p (a o)"), wg[:, :],
                                        tapw[:, t * 3 * C:(t + 1) * 3 * C], ALU.mult).then_inc(s["conv_w"], 1)
            for b in range(NB):
                pool.wait_ge(s["rs2_d"], b + 1)
                nc.gpsimd.tensor_copy(rsx2[b][:, :, :, :], rsum2[b][:, :, :].unsqueeze(3).broadcast_to([128, NT, HEADS, QUAD])).then_inc(s["rsx2_d"], 1)
            for n, (ready, done) in enumerate(((s["ve3_d"], s["rs3_d"]), (s["ve4_d"], s["rs4_d"]), (s["ve5_d"], s["rs5_d"]), (s["ve6_d"], s["rs6_d"]))):
                for b in range(NB):
                    inverse_root(rs3[b][:, n, :], ve3[b][:, n, :], ready, done, b, NT)
                if n == 0:
                    for b in range(NB):
                        pool.wait_ge(s["f_d"], b + 1)
                        nc.gpsimd.tensor_copy(fsh[2][b][:, 1:H + 1, 0:W - 1], fsh[1][b][:, 1:H + 1, 1:W]).then_inc(s["f2_d"], 1)

        @block.scalar
        def _(act):
            act.dma_start(x0[1][:, :], x[1].rearrange("c h w -> c (h w)")).then_inc(s["x_in"], 16)
            act.dma_start(tapw[:, :], taps.partition_broadcast(128)).then_inc(s["tap_in"], 16)

            def exps(b, src, dst, nm, sums, max_d, e_d):
                act.wait_ge(max_d, b + 1)
                for t in range(NT):
                    nc.scalar.activation(dst[b][:, t, :], tiles(src)[:, t, :], ACT.Exp, bias=nm[:, t:t + 1],
                                         accum_out=sums[:, t:t + 1]).then_inc(e_d, 1)

            for b in range(NB):
                act.wait_ge(s["k0_p"], b + 1)
                nc.scalar.activation(k0[b][:, :], bank[4 * b + 1][:, 0:N], ACT.Identity, bias=A("bk0")).then_inc(s["k0_d"], 1)
                act.wait_ge(s["v0_p"], b + 1)
                nc.scalar.activation(v0[b][:, :, :], tiles(bank[4 * b + 2], 4)[:, 0:NT, :], ACT.Copy).then_inc(s["v0_d"], 1)
            for b in range(NB):
                exps(b, bank[4 * b + 3], p0, nmax[b][:, 0:NT], psum_[b][:, 0:NT], s["max0_d"], s["e0_d"])
            for b in range(NB):
                act.wait_ge(s["rb0_p"], b + 1)
                nc.scalar.activation(rb0[b][:, :], bank[4 * b + 1][:, 0:N], ACT.Copy).then_inc(s["rb0_d"], 1)
            for b in range(NB):
                act.wait_ge(s["k1_p"], b + 1)
                nc.scalar.activation(k1[b][:, :], bank[4 * b + 1][0:CQ, 0:N], ACT.Identity, bias=A("bk1")[0:CQ, :]).then_inc(s["k1_d"], 1)
                act.wait_ge(s["v1_p"], b + 1)
                nc.scalar.activation(v1[b][:, :, :], tiles(bank[4 * b + 3], 4)[:, 0:NT, :], ACT.Copy).then_inc(s["v1_d"], 1)
            for b in range(NB):
                exps(b, bank[4 * b + 2], p1, nmax[b][:, NT:2 * NT], psum_[b][:, NT:2 * NT], s["max1_d"], s["e1_d"])
            for b in range(NB):
                act.wait_ge(s["rb1_p"], b + 1)
                nc.scalar.activation(rb1[b][:, :], bank[4 * b + 1][:, 0:N], ACT.Copy).then_inc(s["rb1_d"], 1)
            for b in range(NB):
                act.wait_ge(s["min_d"], b + 1)
                nc.scalar.activation(ce[b][:, :], bank[4 * b + 1][:, 0:C], ACT.Exp, bias=cmin[b][:, :], scale=-1.0,
                                     accum_out=csum[b][:, :]).then_inc(s["ce_d"], 1)
            for b in range(NB):
                act.wait_ge(s["k2_p"], b + 1)
                nc.scalar.activation(k2[b][:, :, :], tiles(bank[4 * b + 1], NG), ACT.Copy).then_inc(s["k2_d"], 1)
                act.wait_ge(s["v2_p"], b + 1)
                nc.scalar.activation(v2[b][:, :, :], tiles(bank[4 * b + 2]), ACT.Copy).then_inc(s["v2_d"], 1)
            for u in range(NB * HEADS + 2):
                if u < NB * HEADS:
                    b, h = divmod(u, HEADS)
                    act.wait_ge(s["nb2_d"], u + 1)
                    if u >= P2_RING:
                        act.wait_ge(s["t2_p"], u - P2_RING + 1)
                    for t in range(NT):
                        nc.scalar.activation(p2[u % P2_RING][:, t, :], tiles(bank[u % 3])[:, t, :], ACT.Exp, scale=D ** -0.5,
                                             bias=nmax2[b][:, h, NT + t:NT + t + 1],
                                             accum_out=sum2[b][:, t, h:h + 1]).then_inc(s["e2_d"], 1)
                v = u - 2
                if v >= 0 and v % 2:
                    act.wait_ge(s["t2_p"], v + 1)
                    if v >= PT2_RING:
                        act.wait_ge(s["pv2_p"], (v - PT2_RING) // HG + 1)
                    nc.scalar.activation(pT2[v % PT2_RING][:, :, :], tiles(bank[4 + v % 3]), ACT.Copy).then_inc(s["pT2o_d"], 1)
            for b in range(NB):
                act.wait_ge(s["rb2_p"], b + 1)
                nc.scalar.activation(rb2[b][:, :, :], tiles(bank[4 * b], NG), ACT.Copy).then_inc(s["rb2_d"], 1)
            for b in range(NB):
                act.wait_ge(s["f_d"], b + 1)
                act.wait_ge(s["zeroed"], 3 * NB)
                nc.scalar.activation(fsh[0][b][:, 1:H + 1, 1:W], fsh[1][b][:, 1:H + 1, 0:W - 1], ACT.Copy).then_inc(s["f0_d"], 1)
            for b in range(NB):
                act.wait_ge(s["k3m_d"], b + 1)
                nc.scalar.activation(ek[b][:, :], bank[4 * b + 3][:, 0:N], ACT.Exp, bias=nmk[b][:, :],
                                     accum_out=sumk[b][:, :]).then_inc(s["ek_d"], 1)
                act.wait_ge(s["qv_p"], b + 1)
                nc.scalar.activation(v3[b][:, :, :], tiles(bank[4 * b])[:, :, C:2 * C], ACT.Copy).then_inc(s["v3_d"], 1)
                act.wait_ge(s["qs_d"], b + 1)
                nc.scalar.activation(eq[b][:, :, :, :], qs[b][:, :, :, :], ACT.Exp).then_inc(s["eq_d"], 1)
                act.wait_ge(s["ekT_p"], b + 1)
                nc.scalar.activation(ekT[b][:, :, :], tiles(bank[4 * b + 1], 4)[:, 0:NT, :], ACT.Copy).then_inc(s["ekT_d"], 1)
            for b in range(NB):
                act.wait_ge(s["qT_p"], b + 1)
                nc.scalar.activation(qT[b][:, :], bank[4 * b + 2][:, 0:N], ACT.Copy).then_inc(s["qT_d"], 1)
            for b in range(NB):
                act.wait_ge(s["o3_p"], b + 1)
                nc.scalar.activation(th[b][:, :], bank[4 * b][:, 0:N], ACT.Tanh, scale=0.5).then_inc(s["th_d"], 1)
            for b in range(NB):
                act.wait_ge(s["yc_p"], b + 1)
                nc.scalar.activation(ycg[b][:, :], bank[4 * b + 1][:, 0:N], ACT.Copy, scale=A("out_norm_g")).then_inc(s["ycg_d"], 1)
            for b in range(NB):
                act.wait_ge(s["rs5_d"], b + 1)
                act.wait_ge(s["h_p"], b + 1)
                for t in range(NT):
                    nc.scalar.activation(h3[b][:, t, :], tiles(bank[4 * b + 1])[:, t, :], ACT.Gelu,
                                         scale=rs3[b][:, 2, t:t + 1]).then_inc(s["h_d"], 1)
            for b in range(NB):
                act.wait_ge(s["hT_p"], b + 1)
                nc.scalar.activation(hT3[b][:, :, :], tiles(bank[4 * b + 2]), ACT.Copy).then_inc(s["hT_d"], 1)
                act.wait_ge(s["rb6_p"], b + 1)
                nc.scalar.activation(rb4[b][:, :], bank[4 * b + 3][:, 0:N], ACT.Copy).then_inc(s["rb6_d"], 1)

        @block.vector
        def _(dve):
            counts = {}

            def vec_done(name):
                counts.setdefault(name, []).append(sum(len(c) for c in counts.values()) + 1)

            def vec_at(name, nth):
                return counts[name][nth - 1]

            def norm_stats(b, n, src, ready, ve_d, count):
                dve.wait_ge(ready, count)
                for t in range(NT):
                    nc.vector.bn_stats(st3[b][:, n, t, :], src(t)).then_inc(s["vec"], 1)
                    vec_done("st")
                dve.wait_ge(s["vec"], vec_at("st", NT * (NB * n + b + 1)))
                for t in range(NT):
                    nc.vector.bn_aggr(mv3[b][:, n, t, :], st3[b][:, n, t, :]).then_inc(s["vec"], 1)
                    vec_done("mv")
                dve.wait_ge(s["vec"], vec_at("mv", NT * (NB * n + b + 1)))
                nc.vector.tensor_scalar_add(ve3[b][:, n, :], mv3[b][:, n, :, 1], EPS_LN).then_inc(ve_d, 1)

            def row_max(b, scores, ready, nm, max_d):
                dve.wait_ge(ready, b + 1)
                nc.vector.tensor_reduce(nm, tiles(scores), AX.X, ALU.max, negate=True).then_inc(max_d, 1)

            for b in range(NB):
                dve.wait_ge(s["x_in"], 32)
                nc.vector.bn_stats(st0[b][:, :], x0[b][:, :]).then_inc(s["vec"], 1)
                vec_done("st0")
            for b in range(NB):
                dve.wait_ge(s["vec"], vec_at("st0", b + 1))
                nc.vector.bn_aggr(mv0[b][:, :], st0[b][:, :]).then_inc(s["vec"], 1)
                vec_done("mv0")
            for b in range(NB):
                dve.wait_ge(s["vec"], vec_at("mv0", b + 1))
                nc.vector.scalar_tensor_tensor(mv0[b][:, 1:2], mv0[b][:, 0:1], mv0[b][:, 0:1], mv0[b][:, 1:2],
                                               ALU.mult, ALU.add).then_inc(s["gin0_d"], 1)
            for b in range(NB):
                dve.wait_ge(s["g0_p"], b + 1)
                nc.vector.tensor_copy(gs0[b][:, :], bank[4 * b][:, 0:2]).then_inc(s["vec"], 1)
                vec_done("g0")
            for b in range(NB):
                dve.wait_ge(s["vec"], vec_at("g0", b + 1))
                nc.vector.scalar_tensor_tensor(sm0[b][:, 0:1], gs0[b][:, 0:1], -1.0, gs0[b][:, 0:1],
                                               ALU.mult, ALU.mult).then_inc(s["vec"], 1)
                vec_done("nm0")
            for b in range(NB):
                dve.wait_ge(s["vec"], vec_at("nm0", b + 1))
                nc.vector.scalar_tensor_tensor(sm0[b][:, 1:2], gs0[b][:, 1:2], EPS_GN, sm0[b][:, 0:1],
                                               ALU.add, ALU.add).then_inc(s["ve0_d"], 1)
            dve.wait_ge(s["wpv_p"], 1)
            nc.vector.tensor_copy(wpvT[:, :], bank[3][:, 0:C]).then_inc(s["wpv_w"], 1)
            nc.vector.tensor_add(bias0[:, :], bank[3][:, C:C + 1], A("bp0")).then_inc(s["bias0_w"], 1)
            for b in range(NB):
                dve.wait_ge(s["rstd0_d"], b + 1)
                nc.vector.tensor_mul(sm0[b][:, 3:4], sm0[b][:, 2:3], A("gamma")).then_inc(s["vec"], 1)
                vec_done("a0")
                dve.wait_ge(s["vec"], vec_at("a0", b + 1))
                nc.vector.tensor_mul(sm0[b][:, 4:5], sm0[b][:, 3:4], gs0[b][:, 0:1]).then_inc(s["vec"], 1)
                vec_done("ma0")
                dve.wait_ge(s["vec"], vec_at("ma0", b + 1))
                nc.vector.tensor_sub(sm0[b][:, 5:6], A("beta"), sm0[b][:, 4:5]).then_inc(s["vec"], 1)
                vec_done("b0")
                dve.wait_ge(s["vec"], vec_at("b0", b + 1))
                nc.vector.tensor_scalar(hn0[b][:, :], x0[b][:, :], sm0[b][:, 3:4], sm0[b][:, 5:6],
                                        ALU.mult, ALU.add).then_inc(s["hn0_d"], 1)
            for b in range(NB):
                dve.wait_ge(s["q0_p"], b + 1)
                nc.vector.tensor_scalar(q0[b][:, :], bank[4 * b][:, 0:N], A("bq0"), float(C) ** -0.5,
                                        ALU.add, ALU.mult).then_inc(s["q0_d"], 1)
            dve.wait_ge(s["bias0_w"], 1)
            for b in range(NB):
                nc.vector.tensor_scalar_add(xb0[b][:, :], x0[b][:, :], bias0[:, :]).then_inc(s["vec"], 1)
                vec_done("xb0")
            for b in range(NB):
                row_max(b, bank[4 * b + 3], s["s0_p"], nmax[b][:, 0:NT], s["max0_d"])
            dve.wait_ge(s["c_in"], 16)
            nc.vector.tensor_scalar_mul(wg[:, :], K("w1x1T"), A("norm_g")).then_inc(s["wg_done"], 1)
            for b in range(NB):
                dve.wait_ge(s["e0_d"], NT * (b + 1))
                nc.vector.reciprocal(rsum[b][:, 0:NT], psum_[b][:, 0:NT]).then_inc(s["rs0_d"], 1)
                dve.wait_ge(s["t0_p"], b + 1)
                nc.vector.tensor_copy(pT0[b][:, :, :], tiles(bank[4 * b])).then_inc(s["pT0_d"], 1)
            nc.vector.tensor_mul(gbv[:, :], A("gpam"), A("bv1")).then_inc(s["gbv_w"], 1)
            for b in range(NB):
                dve.wait_ge(s["pv0_p"], b + 1)
                dve.wait_ge(s["rb0_d"], b + 1)
                nc.vector.tensor_mul(t0[b][:, :], bank[4 * b + 2][:, 0:N], rb0[b][:, :]).then_inc(s["vec"], 1)
                vec_done("n0")
                dve.wait_ge(s["vec"], vec_at("n0", b + 1))
                dve.wait_ge(s["vec"], vec_at("xb0", b + 1))
                nc.vector.tensor_add(x1[b][:, :], t0[b][:, :], xb0[b][:, :]).then_inc(s["x1_d"], 1)

            for b in range(NB):
                dve.wait_ge(s["q1_p"], b + 1)
                nc.vector.tensor_scalar_add(q1[b][:, :], bank[4 * b][0:CQ, 0:N], A("bq1")[0:CQ, :]).then_inc(s["q1_d"], 1)
            dve.wait_ge(s["gbv_w"], 1)
            for b in range(NB):
                dve.wait_ge(s["x1_d"], b + 1)
                nc.vector.tensor_scalar_add(xb1[b][:, :], x1[b][:, :], gbv[:, :]).then_inc(s["vec"], 1)
                vec_done("xb1")
            for b in range(NB):
                row_max(b, bank[4 * b + 2], s["s1_p"], nmax[b][:, NT:2 * NT], s["max1_d"])
            nc.vector.tensor_scalar_mul(w1g[:, :], K("w1T"), A("ff_g1")).then_inc(s["w1g_w"], 1)
            for j in range(2):
                nc.vector.tensor_scalar_mul(w2g[:, j, :], tiles(K("w2T"))[:, j, :], A("ff_g2")[:, j:j + 1]).then_inc(s["w2g_w"], 1)
            for b in range(NB):
                dve.wait_ge(s["e1_d"], NT * (b + 1))
                nc.vector.reciprocal(rsum[b][:, NT:2 * NT], psum_[b][:, NT:2 * NT]).then_inc(s["vec"], 1)
                vec_done("rs1")
                dve.wait_ge(s["vec"], vec_at("rs1", b + 1))
                nc.vector.tensor_scalar_mul(rsum[b][:, NT:2 * NT], rsum[b][:, NT:2 * NT], A("gpam")).then_inc(s["rsg1_d"], 1)
                dve.wait_ge(s["t1_p"], b + 1)
                nc.vector.tensor_copy(pT1[b][:, :, :], tiles(bank[4 * b])).then_inc(s["pT1_d"], 1)
            for b in range(NB):
                dve.wait_ge(s["pv1_p"], b + 1)
                dve.wait_ge(s["rb1_d"], b + 1)
                nc.vector.tensor_mul(t1[b][:, :], bank[4 * b + 3][:, 0:N], rb1[b][:, :]).then_inc(s["vec"], 1)
                vec_done("n1")
                dve.wait_ge(s["vec"], vec_at("n1", b + 1))
                dve.wait_ge(s["vec"], vec_at("xb1", b + 1))
                nc.vector.tensor_add(pam[b][:, :], t1[b][:, :], xb1[b][:, :]).then_inc(s["pam_d"], 1)
            for b in range(NB):
                dve.wait_ge(s["pamT_p"], b + 1)
                nc.vector.tensor_copy(pamT[b][:, :, :], tiles(bank[4 * b], 4)[:, 0:NT, :]).then_inc(s["pamT_d"], 1)
            for b in range(NB):
                dve.wait_ge(s["cen_p"], b + 1)
                nc.vector.tensor_reduce(cmin[b][:, :], bank[4 * b + 1][:, 0:C], AX.X, ALU.min).then_inc(s["min_d"], 1)
            for b in range(NB):
                dve.wait_ge(s["ceT_p"], b + 1)
                nc.vector.tensor_copy(ceT[b][:, :], bank[4 * b + 2][:, 0:C]).then_inc(s["ceT_d"], 1)
                nc.vector.reciprocal(cscale[b][:, 0:1], csum[b][:, :]).then_inc(s["vec"], 1)
                vec_done("cr")
                dve.wait_ge(s["vec"], vec_at("cr", b + 1))
                nc.vector.tensor_mul(cscale[b][:, 1:2], cscale[b][:, 0:1], A("gcam")).then_inc(s["vec"], 1)
                vec_done("cs")
            for b in range(NB):
                dve.wait_ge(s["co_p"], b + 1)
                dve.wait_ge(s["vec"], vec_at("cs", b + 1))
                nc.vector.scalar_tensor_tensor(x2[b][:, :], bank[4 * b + 3][:, 0:N], cscale[b][:, 1:2], pam[b][:, :],
                                               ALU.mult, ALU.add).then_inc(s["x2_d"], 1)

            for b in range(NB):
                dve.wait_ge(s["q2_p"], b + 1)
                nc.vector.tensor_copy(q2[b][:, :, :], tiles(bank[4 * b], NG)).then_inc(s["q2_d"], 1)
            for b in range(NB):
                dve.wait_ge(s["x2_d"], b + 1)
                nc.vector.tensor_scalar_add(xb2[b][:, :], x2[b][:, :], A("bout")).then_inc(s["vec"], 1)
                vec_done("xb2")
            nc.vector.tensor_scalar(outwc[:, :], K("outwT"), 0.5, None, ALU.mult).then_inc(s["vec"], 1)
            vec_done("outw_half")
            dve.wait_ge(s["vec"], vec_at("outw_half", 1))
            nc.vector.reduce_sum(outws[:, 0:1], outwc[:, :], AX.X).then_inc(s["vec"], 1)
            vec_done("outw_sum")
            dve.wait_ge(s["vec"], vec_at("outw_sum", 1))
            nc.vector.tensor_scalar(outws[:, 1:2], outws[:, 0:1], -1.0 / C, None, ALU.mult).then_inc(s["vec"], 1)
            vec_done("outw_neg")
            dve.wait_ge(s["vec"], vec_at("outw_neg", 1))
            nc.vector.tensor_scalar_add(outwc[:, :], outwc[:, :], outws[:, 1:2]).then_inc(s["outw_c"], 1)
            for u in range(NB * HEADS + 2):
                if u < NB * HEADS:
                    b, h = divmod(u, HEADS)
                    dve.wait_ge(s["s2_p"], u + 1)
                    nc.vector.tensor_reduce(nmax2[b][:, h, 0:NT], tiles(bank[u % 3]), AX.X, ALU.max, negate=True).then_inc(s["vec"], 1)
                    vec_done("max2")
                    dve.wait_ge(s["vec"], vec_at("max2", u + 1))
                    nc.vector.tensor_scalar(nmax2[b][:, h, NT:2 * NT], nmax2[b][:, h, 0:NT], D ** -0.5, None,
                                            ALU.mult).then_inc(s["nb2_d"], 1)
                v = u - 2
                if v >= 0 and v % 2 == 0:
                    dve.wait_ge(s["t2_p"], v + 1)
                    if v >= PT2_RING:
                        dve.wait_ge(s["pv2_p"], (v - PT2_RING) // HG + 1)
                    nc.vector.tensor_copy(pT2[v % PT2_RING][:, :, :], tiles(bank[4 + v % 3])).then_inc(s["pT2e_d"], 1)
            for b in range(NB):
                dve.wait_ge(s["e2_d"], NT * HEADS * (b + 1))
                nc.vector.reciprocal(rsum2[b][:, :, :], sum2[b][:, :, :]).then_inc(s["rs2_d"], 1)
            for b in range(NB):
                dve.wait_ge(s["rb2_d"], b + 1)
                dve.wait_ge(s["pv2_p"], NG * (b + 1))
                nc.vector.tensor_mul(o2[b][:, :, :], tiles(bank[4 * b + 3], NG), rb2[b][:, :, :]).then_inc(s["o2_d"], 1)
            for b in range(NB):
                dve.wait_ge(s["w2_p"], b + 1)
                dve.wait_ge(s["vec"], vec_at("xb2", b + 1))
                nc.vector.tensor_add(x3[b][:, :], bank[4 * b + 1][:, 0:N], xb2[b][:, :]).then_inc(s["x3_d"], 1)

            for b in range(NB):
                norm_stats(b, 0, lambda t: tiles(bank[4 * b], 4)[:, t, :], s["x3T_p"], s["ve3_d"], b + 1)
                dve.wait_ge(s["mean3_p"], b + 1)
                nc.vector.tensor_sub(xc3[b][:, :], x3[b][:, :], bank[4 * b + 1][:, 0:N]).then_inc(s["xc3_d"], 1)
            for b in range(NB):
                dve.wait_ge(s["rb3_p"], b + 1)
                dve.wait_ge(s["xc3_d"], b + 1)
                dve.wait_ge(s["zeroed"], 3 * (b + 1))
                nc.vector.tensor_mul(fsh[1][b][:, 1:H + 1, :], xc3[b][:, :].rearrange("p (h w) -> p h w", h=H),
                                     bank[4 * b + 2][:, 0:N].rearrange("p (h w) -> p h w", h=H)).then_inc(s["f_d"], 1)
            dve.wait_ge(s["w2m_p"], 1)
            nc.vector.tensor_sub(w1c[:, :], w1g[:, :], bank[1][:, 0:HID]).then_inc(s["w1c_w"], 1)
            for j in range(2):
                nc.vector.scalar_tensor_tensor(w2c[:, j, :], bank[1][:, HID:HID + C], -0.5, w2g[:, j, :],
                                               ALU.mult, ALU.add).then_inc(s["w2c_w"], 1)
            for b in range(NB):
                dve.wait_ge(s["k3_p"], b + 1)
                nc.vector.tensor_reduce(nmk[b][:, :], bank[4 * b + 3][:, 0:N], AX.X, ALU.max, negate=True).then_inc(s["k3m_d"], 1)
                dve.wait_ge(s["v3_d"], b + 1)
                qv = tiles(bank[4 * b])[:, :, 0:C].rearrange("p t (h d) -> p t h d", h=HEADS)

                def heads(t):
                    return t[b][:, :, :].unsqueeze(3).broadcast_to([128, NT, HEADS, D])

                nc.vector.tensor_reduce(mq[b][:, :, :], qv, AX.X, ALU.max).then_inc(s["vec"], 1)
                vec_done("mq")
                dve.wait_ge(s["vec"], vec_at("mq", b + 1))
                nc.vector.tensor_tensor(qs[b][:, :, :, :], qv, heads(mq), ALU.subtract).then_inc(s["qs_d"], 1)
                dve.wait_ge(s["eq_d"], b + 1)
                nc.vector.reduce_sum(sq[b][:, :, :], eq[b][:, :, :, :], AX.X).then_inc(s["vec"], 1)
                vec_done("sq")
                dve.wait_ge(s["vec"], vec_at("sq", b + 1))
                nc.vector.reciprocal(rq[b][:, :, :], sq[b][:, :, :]).then_inc(s["vec"], 1)
                vec_done("rq")
                dve.wait_ge(s["vec"], vec_at("rq", b + 1))
                nc.vector.tensor_tensor(qn[b][:, :, :, :], eq[b][:, :, :, :], heads(rq), ALU.mult).then_inc(s["qn_d"], 1)
                dve.wait_ge(s["ek_d"], b + 1)
                nc.vector.reciprocal(rsk[b][:, 0:1], sumk[b][:, :]).then_inc(s["vec"], 1)
                vec_done("rkr")
                dve.wait_ge(s["vec"], vec_at("rkr", b + 1))
                nc.vector.tensor_scalar(rsk[b][:, 1:2], rsk[b][:, 0:1], D ** -0.5, None, ALU.mult).then_inc(s["vec"], 1)
                vec_done("rk")
            for b in range(NB):
                dve.wait_ge(s["ctx_p"], b + 1)
                dve.wait_ge(s["vec"], vec_at("rk", b + 1))
                nc.vector.scalar_tensor_tensor(cm[b][:, :], bank[4 * b + 3][:, 0:C], rsk[b][:, 1:2], K("headmask"),
                                               ALU.mult, ALU.mult).then_inc(s["cm_d"], 1)
            for b in range(NB):
                dve.wait_ge(s["th_d"], b + 1)
                nc.vector.scalar_tensor_tensor(s3[b][:, :], th[b][:, :], 1.0, bank[4 * b][:, 0:N],
                                               ALU.add, ALU.mult).then_inc(s["s3_d"], 1)
            for b in range(NB):
                norm_stats(b, 1, lambda t: tiles(bank[4 * b + 2], 4)[:, t, :], s["yT_p"], s["ve4_d"], b + 1)
            for b in range(NB):
                dve.wait_ge(s["rb4_p"], b + 1)
                dve.wait_ge(s["ycg_d"], b + 1)
                nc.vector.tensor_mul(x4a[b][:, :], bank[4 * b + 3][:, 0:N], ycg[b][:, :]).then_inc(s["vec"], 1)
                vec_done("x4a")
                dve.wait_ge(s["vec"], vec_at("x4a", b + 1))
                nc.vector.tensor_add(x4[b][:, :], x4a[b][:, :], x3[b][:, :]).then_inc(s["x4_d"], 1)
            for b in range(NB):
                norm_stats(b, 2, lambda t: tiles(bank[4 * b], 4)[:, t, :], s["x4T_p"], s["ve5_d"], b + 1)
            for b in range(NB):
                norm_stats(b, 3, lambda t: h3[b][:, t, :], s["h_d"], s["ve6_d"], NT * (b + 1))
            for b in range(NB):
                dve.wait_ge(s["ff_p"], b + 1)
                dve.wait_ge(s["rb6_d"], b + 1)
                nc.vector.tensor_mul(fo[b][:, :], bank[4 * b][:, 0:N], rb4[b][:, :]).then_inc(s["vec"], 1)
                vec_done("fo")
                dve.wait_ge(s["vec"], vec_at("fo", b + 1))
                nc.vector.tensor_add(y[b][:, :], fo[b][:, :], x4[b][:, :]).then_inc(s["y_d"], 1)

        @block.tensor
        def _(pe):
            def spread(dst, rows, width=128):
                return nc.tensor.matmul(dst, rows, ident, start=True, stop=True)

            def transposes(dst, src, done):
                for i in range(NT):
                    for t in range(NT):
                        last = nc.tensor.transpose(tiles(dst)[:, i, t * 128:(t + 1) * 128],
                                                   src[:, t, i * 128:(i + 1) * 128], ident)
                last.then_inc(done, 1)

            pe.wait_ge(s["a_in"], 16)
            nc.tensor.matmul(bank[3][:, 0:C], A("wv0"), A("wpT0"), start=True, stop=True)
            nc.tensor.matmul(bank[3][:, C:C + 1], A("wpT0"), A("bv0"), start=True, stop=True).then_inc(s["wpv_p"], 1)
            for b in range(NB):
                pe.wait_ge(s["gin0_d"], b + 1)
                nc.tensor.matmul(bank[4 * b][:, 0:2], A("gmean"), mv0[b][:, :], start=True, stop=True).then_inc(s["g0_p"], 1)
            for b in range(NB):
                pe.wait_ge(s["hn0_d"], b + 1)
                nc.tensor.matmul(bank[4 * b][:, 0:N], A("wqT0"), hn0[b][:, :], start=True, stop=True).then_inc(s["q0_p"], 1)
                nc.tensor.matmul(bank[4 * b + 1][:, 0:N], A("wkT0"), hn0[b][:, :], start=True, stop=True).then_inc(s["k0_p"], 1)
                pe.wait_ge(s["wpv_w"], 1)
                for t in range(NT):
                    last = nc.tensor.matmul(bank[4 * b + 2][:, t * C:(t + 1) * C], hn0[b][:, t * 128:(t + 1) * 128], wpvT[:, :],
                                            start=True, stop=True)
                last.then_inc(s["v0_p"], 1)
            for b in range(NB):
                pe.wait_ge(s["q0_d"], b + 1)
                pe.wait_ge(s["k0_d"], b + 1)
                pe.wait_ge(s["bias0_w"], 1)
                for t in range(NT):
                    last = nc.tensor.matmul(tiles(bank[4 * b + 3])[:, t, :], q0[b][:, t * 128:(t + 1) * 128], k0[b][:, :],
                                            start=True, stop=True)
                last.then_inc(s["s0_p"], 1)

            def weigh(b, p, e_d, t_p, rs, rs_d, rb_p):
                pe.wait_ge(e_d, NT * (b + 1))
                transposes(bank[4 * b], p[b], t_p)
                pe.wait_ge(rs_d, b + 1)
                for t in range(NT):
                    last = spread(bank[4 * b + 1][:, t * 128:(t + 1) * 128], rs[:, t:t + 1].broadcast_to([128, 128]))
                last.then_inc(rb_p, 1)

            def mix(b, dst, v, pT, v_d, pT_d, done):
                pe.wait_ge(v_d, b + 1)
                pe.wait_ge(pT_d, b + 1)
                for i in range(NT):
                    last = nc.tensor.matmul(dst, v[b][:, i, :], pT[b][:, i, :], start=(i == 0), stop=(i == NT - 1))
                last.then_inc(done, 1)

            for b in range(NB):
                weigh(b, p0, s["e0_d"], s["t0_p"], rsum[b][:, 0:NT], s["rs0_d"], s["rb0_p"])
            for b in range(NB):
                mix(b, bank[4 * b + 2][:, 0:N], v0, pT0, s["v0_d"], s["pT0_d"], s["pv0_p"])

            pe.wait_ge(s["b_in"], 16)
            for b in range(NB):
                pe.wait_ge(s["x1_d"], b + 1)
                nc.tensor.matmul(bank[4 * b][0:CQ, 0:N], B("wqT1"), x1[b][:, :], start=True, stop=True).then_inc(s["q1_p"], 1)
                nc.tensor.matmul(bank[4 * b + 1][0:CQ, 0:N], B("wkT1"), x1[b][:, :], start=True, stop=True).then_inc(s["k1_p"], 1)
                for t in range(NT):
                    last = nc.tensor.matmul(bank[4 * b + 3][:, t * C:(t + 1) * C], x1[b][:, t * 128:(t + 1) * 128], B("wvT1"),
                                            start=True, stop=True)
                last.then_inc(s["v1_p"], 1)
            for b in range(NB):
                pe.wait_ge(s["q1_d"], b + 1)
                pe.wait_ge(s["k1_d"], b + 1)
                for t in range(NT):
                    last = nc.tensor.matmul(tiles(bank[4 * b + 2])[:, t, :], q1[b][:, t * 128:(t + 1) * 128], k1[b][:, :],
                                            start=True, stop=True)
                last.then_inc(s["s1_p"], 1)
            for b in range(NB):
                weigh(b, p1, s["e1_d"], s["t1_p"], rsum[b][:, NT:2 * NT], s["rsg1_d"], s["rb1_p"])
            for b in range(NB):
                mix(b, bank[4 * b + 3][:, 0:N], v1, pT1, s["v1_d"], s["pT1_d"], s["pv1_p"])
            for b in range(NB):
                pe.wait_ge(s["pam_d"], b + 1)
                for t in range(NT):
                    last = nc.tensor.transpose(bank[4 * b][:, t * C:(t + 1) * C], pam[b][:, t * 128:(t + 1) * 128], ident)
                last.then_inc(s["pamT_p"], 1)
            for b in range(NB):
                pe.wait_ge(s["pamT_d"], b + 1)
                for t in range(NT):
                    last = nc.tensor.matmul(bank[4 * b + 1][:, 0:C], pamT[b][:, t, :], pamT[b][:, t, :],
                                            start=(t == 0), stop=(t == NT - 1))
                last.then_inc(s["cen_p"], 1)
            for b in range(NB):
                pe.wait_ge(s["ce_d"], b + 1)
                nc.tensor.transpose(bank[4 * b + 2][:, 0:C], ce[b][:, :], ident).then_inc(s["ceT_p"], 1)
            for b in range(NB):
                pe.wait_ge(s["ceT_d"], b + 1)
                nc.tensor.matmul(bank[4 * b + 3][:, 0:N], ceT[b][:, :], pam[b][:, :], start=True, stop=True).then_inc(s["co_p"], 1)

            for b in range(NB):
                for n, (we, wx) in enumerate((("wqe", "wqx"), ("wke", "wkx"))):
                    for g in range(NG):
                        nc.tensor.matmul(tiles(bank[4 * b + n])[:, g, :], B(we)[0:EMB, g * C:(g + 1) * C], B("emb")[0:EMB, :],
                                         start=(g == 0), stop=False, skip_group_check=True)
            for b in range(NB):
                pe.wait_ge(s["x2_d"], b + 1)
                for n, (wx, done) in enumerate((("wqx", s["q2_p"]), ("wkx", s["k2_p"]))):
                    for g in range(NG):
                        last = nc.tensor.matmul(tiles(bank[4 * b + n])[:, g, :], B(wx)[:, g * C:(g + 1) * C], x2[b][:, :],
                                                start=False, stop=True, skip_group_check=True)
                    last.then_inc(done, 1)
                for t in range(NT):
                    last = nc.tensor.matmul(tiles(bank[4 * b + 2])[:, t, :], x2[b][:, t * 128:(t + 1) * 128], B("wvx"),
                                            start=True, stop=True)
                last.then_inc(s["v2_p"], 1)
            pe.wait_ge(s["q2_d"], NB)
            pe.wait_ge(s["k2_d"], NB)
            pe.wait_ge(s["v2_d"], NB)
            for u in range(NB * HEADS + 3):
                if u < NB * HEADS:
                    b, h = divmod(u, HEADS)
                    g, i = divmod(h, HG)
                    if u >= 3:
                        pe.wait_ge(s["e2_d"], NT * (u - 2))
                    rows = slice(QUAD * i, QUAD * i + D)
                    for t in range(NT):
                        last = nc.tensor.matmul(tiles(bank[u % 3])[:, t, :], q2[b][rows, g, t * 128:(t + 1) * 128],
                                                k2[b][rows, g, :], start=True, stop=True, tile_position=(QUAD * i, 0))
                    last.then_inc(s["s2_p"], 1)
                v = u - 1
                if 0 <= v < NB * HEADS:
                    pe.wait_ge(s["e2_d"], NT * (v + 1))
                    if v >= 3:
                        pe.wait_ge(s["pT2e_d"] if (v - 3) % 2 == 0 else s["pT2o_d"], (v - 3) // 2 + 1)
                    transposes(bank[4 + v % 3], p2[v % P2_RING], s["t2_p"])
                if u >= 3 and (u - 3) % HG == HG - 1:
                    grp = (u - 3) // HG
                    b, g = divmod(grp, NG)
                    pe.wait_ge(s["pT2e_d"], 2 * (grp + 1))
                    pe.wait_ge(s["pT2o_d"], 2 * (grp + 1))
                    for kt in range(NT):
                        for i in range(HG):
                            last = nc.tensor.matmul(tiles(bank[4 * b + 3], NG)[QUAD * i:QUAD * (i + 1), g, :],
                                                    v2[b][:, kt, g * C + QUAD * i:g * C + QUAD * (i + 1)],
                                                    pT2[(grp * HG + i) % PT2_RING][:, kt, :], start=(kt == 0), stop=(kt == NT - 1),
                                                    tile_position=(0, QUAD * i), skip_group_check=True)
                    last.then_inc(s["pv2_p"], 1)
            for b in range(NB):
                pe.wait_ge(s["rsx2_d"], b + 1)
                for g in range(NG):
                    for t in range(NT):
                        rows = rsx2[b][:, t, g * HG:(g + 1) * HG, :].rearrange("p h q -> p (h q)")
                        last = spread(tiles(bank[4 * b], NG)[:, g, t * 128:(t + 1) * 128], rows)
                last.then_inc(s["rb2_p"], 1)
            for b in range(NB):
                pe.wait_ge(s["o2_d"], b + 1)
                for g in range(NG):
                    last = nc.tensor.matmul(bank[4 * b + 1][:, 0:N], B("woutp")[:, g * C:(g + 1) * C], o2[b][:, g, :],
                                            start=(g == 0), stop=(g == NG - 1))
                last.then_inc(s["w2_p"], 1)

            pe.wait_ge(s["c_in"], 16)
            for b in range(NB):
                pe.wait_ge(s["x3_d"], b + 1)
                for t in range(NT):
                    last = nc.tensor.transpose(bank[4 * b][:, t * C:(t + 1) * C], x3[b][:, t * 128:(t + 1) * 128], ident)
                last.then_inc(s["x3T_p"], 1)
                nc.tensor.matmul(bank[4 * b + 1][:, 0:N], K("cmean"), x3[b][:, :], start=True, stop=True).then_inc(s["mean3_p"], 1)
            for b in range(NB):
                pe.wait_ge(s["rs3_d"], b + 1)
                for t in range(NT):
                    last = spread(bank[4 * b + 2][:, t * 128:(t + 1) * 128], rs3[b][:, 0, t:t + 1].broadcast_to([128, 128]))
                last.then_inc(s["rb3_p"], 1)
            pe.wait_ge(s["w1g_w"], 1)
            pe.wait_ge(s["w2g_w"], 2)
            pe.wait_ge(s["xc3_d"], 1)
            nc.tensor.matmul(bank[1][:, 0:HID], K("cmean"), w1g[:, :], start=True, stop=True)
            for j in range(2):
                last = nc.tensor.matmul(bank[1][:, HID:HID + C], K("cmean"), w2g[:, j, :], start=(j == 0), stop=(j == 1))
            last.then_inc(s["w2m_p"], 1)
            pe.wait_ge(s["conv_w"], TAPS)
            for b in range(NB):
                pe.wait_ge(s["f_d"], b + 1)
                for n, (dx, dy) in enumerate((dx, dy) for dx in (1, 0, 2) for dy in range(3)):
                    if dx == 0 and dy == 0:
                        pe.wait_ge(s["f0_d"], b + 1)
                    if dx == 2 and dy == 0:
                        pe.wait_ge(s["f2_d"], b + 1)
                    last = nc.tensor.matmul(bank[4 * b + 3][:, 0:N], convw[:, 3 * dy + dx, 0, :],
                                            fsh[dx][b][:, dy:dy + H, :].rearrange("p h w -> p (h w)"),
                                            start=(n == 0), stop=(n == TAPS - 1))
                last.then_inc(s["k3_p"], 1)
                for j in range(NT):
                    for n, (dx, dy) in enumerate((dx, dy) for dx in (1, 0, 2) for dy in range(3)):
                        row = dy + j * (H // NT)
                        last = nc.tensor.matmul(tiles(bank[4 * b])[:, j, :],
                                                fsh[dx][b][:, row:row + H // NT, :].rearrange("p h w -> p (h w)"),
                                                convw[:, 3 * dy + dx, 1:3, :].rearrange("p a o -> p (a o)"),
                                                start=(n == 0), stop=(n == TAPS - 1))
                last.then_inc(s["qv_p"], 1)
            for b in range(NB):
                pe.wait_ge(s["ek_d"], b + 1)
                pe.wait_ge(s["w2c_w"], 2)
                for t in range(NT):
                    last = nc.tensor.transpose(bank[4 * b + 1][:, t * C:(t + 1) * C], ek[b][:, t * 128:(t + 1) * 128], ident)
                last.then_inc(s["ekT_p"], 1)
            for b in range(NB):
                pe.wait_ge(s["ekT_d"], b + 1)
                pe.wait_ge(s["v3_d"], b + 1)
                for t in range(NT):
                    last = nc.tensor.matmul(bank[4 * b + 3][:, 0:C], ekT[b][:, t, :], v3[b][:, t, :],
                                            start=(t == 0), stop=(t == NT - 1))
                last.then_inc(s["ctx_p"], 1)
                pe.wait_ge(s["qn_d"], b + 1)
                for t in range(NT):
                    last = nc.tensor.transpose(bank[4 * b + 2][:, t * 128:(t + 1) * 128],
                                               qn[b][:, t, :, :].rearrange("p h d -> p (h d)"), ident)
                last.then_inc(s["qT_p"], 1)
            for b in range(NB):
                pe.wait_ge(s["cm_d"], b + 1)
                pe.wait_ge(s["qT_d"], b + 1)
                nc.tensor.matmul(bank[4 * b][:, 0:N], cm[b][:, :], qT[b][:, :], start=True, stop=True).then_inc(s["o3_p"], 1)
            pe.wait_ge(s["outw_c"], 1)
            for b in range(NB):
                pe.wait_ge(s["s3_d"], b + 1)
                for t in range(NT):
                    last = nc.tensor.matmul(bank[4 * b + 2][:, t * C:(t + 1) * C], s3[b][:, t * 128:(t + 1) * 128], outwc[:, :],
                                            start=True, stop=True)
                last.then_inc(s["yT_p"], 1)
                nc.tensor.matmul(bank[4 * b + 1][:, 0:N], outwc[:, :], s3[b][:, :], start=True, stop=True).then_inc(s["yc_p"], 1)
            for b in range(NB):
                pe.wait_ge(s["rs4_d"], b + 1)
                for t in range(NT):
                    last = spread(bank[4 * b + 3][:, t * 128:(t + 1) * 128], rs3[b][:, 1, t:t + 1].broadcast_to([128, 128]))
                last.then_inc(s["rb4_p"], 1)
            pe.wait_ge(s["w1c_w"], 1)
            for b in range(NB):
                pe.wait_ge(s["x4_d"], b + 1)
                for t in range(NT):
                    last = nc.tensor.transpose(bank[4 * b][:, t * C:(t + 1) * C], x4[b][:, t * 128:(t + 1) * 128], ident)
                last.then_inc(s["x4T_p"], 1)
                for t in range(NT):
                    last = nc.tensor.matmul(tiles(bank[4 * b + 1])[:, t, :], x4[b][:, t * 128:(t + 1) * 128], w1c[:, :],
                                            start=True, stop=True)
                last.then_inc(s["h_p"], 1)
            for b in range(NB):
                pe.wait_ge(s["h_d"], NT * (b + 1))
                transposes(bank[4 * b + 2], h3[b], s["hT_p"])
            for b in range(NB):
                pe.wait_ge(s["hT_d"], b + 1)
                pe.wait_ge(s["ve5_d"], b + 1)
                for j in range(2):
                    last = nc.tensor.matmul(bank[4 * b][:, 0:N], w2c[:, j, :], hT3[b][:, j, :], start=(j == 0), stop=(j == 1))
                last.then_inc(s["ff_p"], 1)
                pe.wait_ge(s["rs6_d"], b + 1)
                for t in range(NT):
                    last = spread(bank[4 * b + 3][:, t * 128:(t + 1) * 128], rs3[b][:, 3, t:t + 1].broadcast_to([128, 128]))
                last.then_inc(s["rb6_p"], 1)



def _embedding():
    import numpy as np
    f = np.float32
    nf = nt = EMB // 4
    ln_x = np.concatenate([np.array([-2.0], f), np.log2(np.arange(1, H * nf, dtype=f))])
    ln_x = ln_x.reshape(H, nf).T * np.arange(1, nf + 1, dtype=f)[:, None]
    freq = np.stack([np.cos(ln_x), np.sin(ln_x)], axis=1).reshape(2 * nf, H).astype(f)
    k = np.arange(0, nt, dtype=f) + f(0.5)
    xs = np.arange(0, nt * W, dtype=f).reshape(W, nt).T
    theta = (k[:, None] * xs / f(W * nt) * f(6.283185307179586)).astype(f)
    time = np.stack([np.cos(theta), np.sin(theta)], axis=1).reshape(2 * nt, W).astype(f)
    freq = np.broadcast_to(freq[:, :, None], (2 * nf, H, W))
    time = np.broadcast_to(time[:, None, :], (2 * nt, H, W))
    return np.concatenate([freq, time], axis=0).reshape(EMB, N)


def _layout(inputs):
    import numpy as np
    g = {k: np.asarray(v) for k, v in inputs.items()}
    f = np.float32

    def pad_heads(w):
        r = w.shape[0]
        o = np.zeros((r, HEADS, QUAD), f)
        o[:, :, :D] = w.reshape(r, HEADS, D)
        return o.reshape(r, HEADS * QUAD)

    cols = {
        "ident": np.eye(C, dtype=f),
        "gmean": np.kron(np.eye(C // GN_GROUP, dtype=f), np.full((GN_GROUP, GN_GROUP), 1.0 / GN_GROUP, f)),
        "wqT0": g["L0_conv_wq"].T, "wkT0": g["L0_conv_wk"].T, "wv0": g["L0_conv_wv"], "wpT0": g["L0_conv_wp"].T,
        "gamma": g["L0_conv_gamma"], "beta": g["L0_conv_beta"], "bq0": g["L0_conv_bq"], "bk0": g["L0_conv_bk"],
        "bv0": g["L0_conv_bv"], "bp0": g["L0_conv_bp"], "bq1": g["L1_conv_bq"], "bk1": g["L1_conv_bk"],
        "bv1": g["L1_conv_bv"], "gpam": np.broadcast_to(g["L1_conv_gamma_pam"], (C,)),
        "gcam": np.broadcast_to(g["L1_conv_gamma_cam"], (C,)), "bout": g["L2_conv_bout"],
        "norm_g": g["L3_conv_norm_g"].reshape(C), "out_norm_g": g["L3_conv_out_norm_g"].reshape(C),
        "ff_g1": g["L3_conv_ff_g1"].reshape(C), "ff_g2": g["L3_conv_ff_g2"].reshape(2, C).T,
        "wqT1": g["L1_conv_Wq"].T, "wkT1": g["L1_conv_Wk"].T, "wvT1": g["L1_conv_Wv"].T,
        "wqx": pad_heads(g["L2_conv_Wq"][:C]), "wkx": pad_heads(g["L2_conv_Wk"][:C]),
        "wqe": pad_heads(g["L2_conv_Wq"][C:]), "wke": pad_heads(g["L2_conv_Wk"][C:]), "emb": _embedding(),
        "wvx": pad_heads(g["L2_conv_Wv"]),
        "woutp": pad_heads(g["L2_conv_Wout"].T).T.reshape(NG, C, C).transpose(1, 0, 2).reshape(C, NG * C),
        "w1x1T": np.concatenate([g["L3_conv_k_w"].T, g["L3_conv_q_w"].T, g["L3_conv_v_w"].T], axis=1),
        "cmean": np.full((C, C), 1.0 / C, f),
        "headmask": np.kron(np.eye(HEADS, dtype=f), np.ones((D, D), f)),
        "outwT": g["L3_conv_out_w"].T, "w1T": g["L3_conv_ff_w1"].T,
        "w2T": g["L3_conv_ff_w2"].T.reshape(2, C, C).transpose(1, 0, 2).reshape(C, 2 * C),
    }

    def pack(names):
        at, width = places(names)
        o = np.zeros((128, width), f)
        for name, (lo, hi) in at.items():
            a = cols[name].reshape(cols[name].shape[0], hi - lo)
            o[:a.shape[0], lo:hi] = a
        return o

    taps = np.stack([g[f"L3_conv_{n}_dw"].reshape(C, TAPS).T for n in "kqv"], axis=1)
    return {"x": g["x"], "pack_a": pack(PACK_A), "pack_b": pack(PACK_B), "pack_c": pack(PACK_C),
            "taps": np.ascontiguousarray(taps.reshape(TAPS * 3 * C))}


def kernel(**inputs):
    import numpy as _np
    import concourse.bacc as _bacc
    from concourse import mybir as _mybir
    from concourse.bass_utils import run_bass_kernel_spmd as _run

    nc = _bacc.Bacc("TRN2", target_bir_lowering=False, num_devices=1)
    arrays, args = {}, []
    for name, a in _layout(inputs).items():
        a = _np.ascontiguousarray(a)
        arrays[f"in_{name}"] = a
        args.append(nc.dram_tensor(f"in_{name}", a.shape, _mybir.dt.from_np(a.dtype), kind="ExternalInput").ap())
    args.append(nc.dram_tensor("out_0", (NB, C, H, W), _mybir.dt.float32, kind="ExternalOutput").ap())
    build(nc, *args)
    return _run(nc, [arrays], core_ids=[0]).results[0]["out_0"]
```

```python
import concourse.bass as bass
from concourse import mybir
from contextlib import ExitStack

NB = 2
C = 128
H = W = 16
N = H * W
NT = N // 128
CQ = C // 8
HEADS, D = 8, 16
QUAD = 32
HG = C // QUAD
NG = HEADS // HG
EMB = 64
HID = 2 * C
TAPS = 9
GN_GROUP = 4
EPS_GN, EPS_LN = 1e-6, 1e-5

PACK_A = [("gmean", C),
          ("gamma", 1), ("beta", 1), ("bq0", 1), ("bk0", 1), ("bv0", 1), ("bp0", 1),
          ("bq1", 1), ("bk1", 1), ("bv1", 1), ("gpam", 1), ("gcam", 1), ("bout", 1),
          ("norm_g", 1), ("out_norm_g", 1), ("ff_g1", 1), ("ff_g2", 2),
          ("wqT0", C), ("wkT0", C), ("wv0", C), ("wpT0", C), ("ident", C)]
FIRST_A = PACK_A[:-5]
PACK_B = [("wqT1", C), ("wkT1", C), ("wvT1", C),
          ("wqx", C), ("wkx", C), ("wqe", C), ("wke", C), ("emb", N), ("headcol", HEADS),
          ("wvx", NG * C), ("wout", C)]
PACK_C = [("w1x1T", 3 * C), ("cmean", C), ("headmask", C), ("outwT", C), ("w1T", HID), ("w2T", HID), ("kdw", TAPS)]


def places(pack):
    at, out = 0, {}
    for name, width in pack:
        out[name] = (at, at + width)
        at += width
    return out, at


def build(nc, x, pack_a, pack_b, pack_c, taps, out):
    fp32 = mybir.dt.float32
    ALU = mybir.AluOpType
    ACT = mybir.ActivationFunctionType
    AX = mybir.AxisListType

    with ExitStack() as ctx:
        def sb(name, shape):
            return ctx.enter_context(nc.sbuf_tensor(name, shape, fp32))

        def sem(name):
            return ctx.enter_context(nc.semaphore(name))

        at_a, width_a = places(PACK_A)
        at_b, width_b = places(PACK_B)
        at_c, width_c = places(PACK_C)
        wa, wb, wc = sb("wa", [128, width_a]), sb("wb", [128, width_b]), sb("wc", [128, width_c])

        def A(name):
            return wa[:, at_a[name][0]:at_a[name][1]]

        def B(name):
            return wb[:, at_b[name][0]:at_b[name][1]]

        def K(name):
            return wc[:, at_c[name][0]:at_c[name][1]]

        ident = A("ident")
        tapw = sb("tapw", [128, TAPS * 2 * C])
        convw = sb("convw", [128, TAPS, 2, C])
        wg = sb("wg", [128, 3 * C])
        wpvT = sb("wpvT", [128, C])
        bias0 = sb("bias0", [128, 1])
        gbv = sb("gbv", [128, 1])
        outwc = sb("outwc", [128, C])
        outws = sb("outws", [128, 2])
        w1c = sb("w1c", [128, HID])
        w1g = sb("w1g", [128, HID])
        w2c = sb("w2c", [128, 2, C])
        w2g = sb("w2g", [128, 2, C])
        warm = ctx.enter_context(nc.sbuf_tensor("warm", [128, 512], mybir.dt.bfloat16))
        mhalf = sb("mhalf", [128, 4])

        def per_batch(name, shape):
            return [sb(f"{name}_{b}", shape) for b in range(NB)]

        x0 = per_batch("x0", [128, N])
        st0 = per_batch("st0", [128, 6])
        mv0 = per_batch("mv0", [128, 2])
        gs0 = per_batch("gs0", [128, 2])
        sm0 = per_batch("sm0", [128, 8])
        hn0 = per_batch("hn0", [128, N])
        xb0 = per_batch("xb0", [128, N])
        q0, k0 = per_batch("q0", [128, N]), per_batch("k0", [128, N])
        v0 = per_batch("v0", [128, NT, C])
        nmax = per_batch("nmax", [128, 2 * NT])
        psum_ = per_batch("sums", [128, 2 * NT])
        rsum = per_batch("rsum", [128, 2 * NT])
        p0, pT0 = per_batch("p0", [128, NT, N]), per_batch("pT0", [128, NT, N])
        rb0, t0, x1 = per_batch("rb0", [128, N]), per_batch("t0", [128, N]), per_batch("x1", [128, N])
        xb1 = per_batch("xb1", [128, N])
        q1, k1 = per_batch("q1", [128, N]), per_batch("k1", [128, N])
        v1 = per_batch("v1", [128, NT, C])
        p1, pT1 = per_batch("p1", [128, NT, N]), per_batch("pT1", [128, NT, N])
        rb1, t1, pam = per_batch("rb1", [128, N]), per_batch("t1", [128, N]), per_batch("pam", [128, N])
        pamT = per_batch("pamT", [128, NT, C])
        cmin, csum, cscale = per_batch("cmin", [128, 1]), per_batch("csum", [128, 1]), per_batch("cscale", [128, 2])
        ce, ceT = per_batch("ce", [128, C]), per_batch("ceT", [128, C])
        x2, xb2 = per_batch("x2", [128, N]), per_batch("xb2", [128, N])
        q2, k2 = per_batch("q2", [128, N]), per_batch("k2", [128, N])
        qh2 = per_batch("qh2", [128, HEADS, N])
        v2 = per_batch("v2", [128, NT, NG * C])
        nmax2 = per_batch("nmax2", [128, HEADS, NT])
        sum2, rsum2 = per_batch("sum2", [128, NT, HEADS]), per_batch("rsum2", [128, NT, HEADS])
        rsx2 = per_batch("rsx2", [128, NT, HEADS, D])
        S2_BANKS, T2_BANKS, P2_RING, PT2_RING = 2, 2, 3, 2 * HG
        p2 = [sb(f"p2_{i}", [128, NT, N]) for i in range(P2_RING)]
        pT2 = [sb(f"pT2_{i}", [128, NT, N]) for i in range(PT2_RING)]
        rb2, o2 = per_batch("rb2", [128, N]), per_batch("o2", [128, N])
        x3, xc3 = per_batch("x3", [128, N]), per_batch("xc3", [128, N])
        st3 = per_batch("st3", [128, 4, NT, 6])
        mv3 = per_batch("mv3", [128, 4, NT, 2])
        ve3 = per_batch("ve3", [128, 4, NT])
        rs3 = per_batch("rs3", [128, 4, NT])
        fsh = [per_batch(f"fsh{dx}", [128, H + 2, W]) for dx in range(3)]
        k1x1 = per_batch("k1x1", [128, H, W])
        kacc = per_batch("kacc", [128, 2, H, W])
        kc = per_batch("kc", [128, N])
        nmk, sumk, rsk = per_batch("nmk", [128, 1]), per_batch("sumk", [128, 1]), per_batch("rsk", [128, 2])
        ek, ekT = per_batch("ek", [128, N]), per_batch("ekT", [128, NT, C])
        v3 = per_batch("v3", [128, NT, C])
        mq, sq, rq = (per_batch(n, [128, NT, HEADS]) for n in ("mq", "sq", "rq"))
        qs, eq, qn = (per_batch(n, [128, NT, HEADS, D]) for n in ("qs", "eq", "qn"))
        qT, cm = per_batch("qT", [128, N]), per_batch("cm", [128, C])
        th, s3 = per_batch("th", [128, N]), per_batch("s3", [128, N])
        ycg, x4a, x4 = per_batch("ycg", [128, N]), per_batch("x4a", [128, N]), per_batch("x4", [128, N])
        h3, hT3 = per_batch("h3", [128, NT, HID]), per_batch("hT3", [128, 2, N])
        rb4, fo, y = per_batch("rb4", [128, N]), per_batch("fo", [128, N]), per_batch("y", [128, N])

        bank = [ctx.enter_context(nc.psum_tensor(f"bank{i}", [128, 512], fp32)) for i in range(8)]

        def tiles(t, n=NT):
            return t[:, :].rearrange("p (t c) -> p t c", t=n)

        LA, LB, LC, LD = (bank[6], bank[4]), (bank[3], bank[7]), (bank[2], bank[0]), (bank[5], bank[1])
        STEPS = NB * HEADS

        def head_of(u):
            b, n = divmod(u, HEADS)
            g, i = divmod(n, HG)
            return b, NG * i + g

        NAMES = """a2_in warm_set vec a_in x_in b_in c_in tap_in zeroed mhalf_set wg_done conv_w wpv_p wpv_w bias0_w gbv_w outw_c w1g_w w1c_w
            w2g_w w2m_p w2c_w gin0_d g0_p ve0_d rstd0_d hn0_d q0_p k0_p v0_p q0_d k0_d v0_d s0_p max0_d e0_d
            rs0_d t0_p pT0_d rb0_p rb0_d pv0_p x1_d q1_p k1_p v1_p q1_d k1_d v1_d s1_p max1_d e1_d rsg1_d t1_p
            pT1_d rb1_p rb1_d pv1_p pam_d pamT_p pamT_d cen_p min_d ce_d ceT_p ceT_d co_p x2_d q2_p k2_p v2_p
            q2_d k2_d v2_d s2_p e2_d t2_p pT2e_d pT2o_d pv2_p rs2_d qh2_d rsx2_d f0_d f2_d rb2_p rb2_d o2_d w2_p
            x3_d x3T_p ve3_d rs3_d mean3_p xc3_d rb3_p f_d k3m_d ek_d ekT_p ekT_d v3_d qs_d eq_d qn_d qT_p qT_d
            ctx_p cm_d o3_p th_d s3_d yc_p yT_p ycg_d ve4_d rs4_d rb4_p x4_d x4T_p ve5_d rs5_d h_p h_d ve6_d
            rs6_d rb6_p rb6_d hT_p hT_d ff_p y_d stored max2_d k1x1_p k1x1_d v3_p q3_p""".split()
        s = {n: sem(n) for n in NAMES}
        block = ctx.enter_context(nc.Block())

        @block.sync
        def _(sp):
            sp.dma_start(x0[0][:, :], x[0].rearrange("c h w -> c (h w)")).then_inc(s["x_in"], 16)
            first = at_a[FIRST_A[-1][0]][1]
            sp.dma_start(wa[:, 0:first], pack_a[:, 0:first]).then_inc(s["a_in"], 16)
            sp.dma_start(wa[:, first:width_a], pack_a[:, first:width_a]).then_inc(s["a2_in"], 16)
            sp.dma_start(wb[:, :], pack_b).then_inc(s["b_in"], 16)
            sp.dma_start(wc[:, :], pack_c).then_inc(s["c_in"], 16)
            for b in range(NB):
                sp.wait_ge(s["y_d"], b + 1)
                sp.dma_start(out[b].rearrange("c h w -> c (h w)"), y[b][:, :]).then_inc(s["stored"], 16)
            sp.wait_ge(s["stored"], 16 * NB)

        @block.gpsimd
        def _(pool):
            nc.gpsimd.memset(mhalf[:, :], -0.5).then_inc(s["mhalf_set"], 1)
            for b in range(NB):
                for dx in range(3):
                    nc.gpsimd.memset(fsh[dx][b][:, :, :], 0.0).then_inc(s["zeroed"], 1)
            pool.wait_ge(s["mhalf_set"], 1)

            def inverse_root(dst, src, ready, done, b, width):
                pool.wait_ge(ready, b + 1)
                nc.gpsimd.tensor_tensor(dst, src, mhalf[:, 0:width], ALU.pow).then_inc(done, 1)

            for b in range(NB):
                inverse_root(sm0[b][:, 2:3], sm0[b][:, 1:2], s["ve0_d"], s["rstd0_d"], b, 1)
            pool.wait_ge(s["wg_done"], 1)
            pool.wait_ge(s["tap_in"], 16)
            for t in range(TAPS):
                nc.gpsimd.tensor_tensor(convw[:, t, :, :].rearrange("p a o -> p (a o)"), wg[:, C:3 * C],
                                        tapw[:, t * 2 * C:(t + 1) * 2 * C], ALU.mult).then_inc(s["conv_w"], 1)
            for u in range(NB * HEADS):
                b, h = head_of(u)
                pool.wait_ge(s["q2_d"], b + 1)
                nc.gpsimd.tensor_scalar(qh2[b][:, h, :], q2[b][:, :], B("headcol")[:, h:h + 1], 1.0,
                                        ALU.mult, ALU.mult).then_inc(s["qh2_d"], 1)
            for b in range(NB):
                nc.gpsimd.memset(kacc[b][:, 1, :, :], 0.0).then_inc(s["zeroed"], 1)

            def rs2_widen(b):
                pool.wait_ge(s["rs2_d"], b + 1)
                nc.gpsimd.tensor_copy(rsx2[b][:, :, :, :], rsum2[b][:, :, :].unsqueeze(3).broadcast_to([128, NT, HEADS, D])).then_inc(s["rsx2_d"], 1)
            def root(n, ready, done):
                return lambda b: inverse_root(rs3[b][:, n, :], ve3[b][:, n, :], ready, done, b, NT)

            root3, root4 = root(0, s["ve3_d"], s["rs3_d"]), root(1, s["ve4_d"], s["rs4_d"])
            root5, root6 = root(2, s["ve5_d"], s["rs5_d"]), root(3, s["ve6_d"], s["rs6_d"])

            def shift_right_edge(b):
                pool.wait_ge(s["f_d"], b + 1)
                nc.gpsimd.tensor_copy(fsh[2][b][:, 1:H + 1, 0:W - 1], fsh[1][b][:, 1:H + 1, 1:W]).then_inc(s["f2_d"], 1)

            for stage, b in ((rs2_widen, 0), (root3, 0), (shift_right_edge, 0), (rs2_widen, 1), (root3, 1), (shift_right_edge, 1),
                             (root4, 0), (root5, 0), (root4, 1), (root6, 0), (root5, 1), (root6, 1)):
                stage(b)

        @block.scalar
        def _(act):
            act.dma_start(x0[1][:, :], x[1].rearrange("c h w -> c (h w)")).then_inc(s["x_in"], 16)
            act.dma_start(tapw[:, :], taps.partition_broadcast(128)).then_inc(s["tap_in"], 16)

            def exps(b, src, dst, nm, sums, max_d, e_d):
                act.wait_ge(max_d, b + 1)
                for t in range(NT):
                    nc.scalar.activation(dst[b][:, t, :], tiles(src)[:, t, :], ACT.Exp, bias=nm[:, t:t + 1],
                                         accum_out=sums[:, t:t + 1]).then_inc(e_d, 1)

            for b in range(NB):
                act.wait_ge(s["k0_p"], b + 1)
                nc.scalar.activation(k0[b][:, :], bank[4 * b + 1][:, 0:N], ACT.Identity, bias=A("bk0")).then_inc(s["k0_d"], 1)
                act.wait_ge(s["v0_p"], b + 1)
                nc.scalar.activation(v0[b][:, :, :], tiles(bank[4 * b + 2], 4)[:, 0:NT, :], ACT.Copy).then_inc(s["v0_d"], 1)
            for b in range(NB):
                exps(b, bank[4 * b + 3], p0, nmax[b][:, 0:NT], psum_[b][:, 0:NT], s["max0_d"], s["e0_d"])
            for b in range(NB):
                act.wait_ge(s["rb0_p"], b + 1)
                nc.scalar.activation(rb0[b][:, :], bank[4 * b + 1][:, 0:N], ACT.Copy).then_inc(s["rb0_d"], 1)
            for b in range(NB):
                act.wait_ge(s["k1_p"], b + 1)
                nc.scalar.activation(k1[b][:, :], bank[4 * b + 1][:, 0:N], ACT.Identity, bias=A("bk1")).then_inc(s["k1_d"], 1)
                act.wait_ge(s["v1_p"], b + 1)
                nc.scalar.activation(v1[b][:, :, :], tiles(bank[4 * b + 3], 4)[:, 0:NT, :], ACT.Copy).then_inc(s["v1_d"], 1)
            for b in range(NB):
                exps(b, bank[4 * b + 2], p1, nmax[b][:, NT:2 * NT], psum_[b][:, NT:2 * NT], s["max1_d"], s["e1_d"])
            for b in range(NB):
                act.wait_ge(s["rb1_p"], b + 1)
                nc.scalar.activation(rb1[b][:, :], bank[4 * b + 1][:, 0:N], ACT.Copy).then_inc(s["rb1_d"], 1)
            for b in range(NB):
                act.wait_ge(s["min_d"], b + 1)
                nc.scalar.activation(ce[b][:, :], bank[4 * b + 1][:, 0:C], ACT.Exp, bias=cmin[b][:, :], scale=-1.0,
                                     accum_out=csum[b][:, :]).then_inc(s["ce_d"], 1)
            for b in range(NB):
                act.wait_ge(s["k2_p"], b + 1)
                nc.scalar.activation(k2[b][:, :], bank[4 * b + 1][:, 0:N], ACT.Copy).then_inc(s["k2_d"], 1)
                act.wait_ge(s["v2_p"], b + 1)
                nc.scalar.activation(v2[b][:, :, :], tiles(bank[4 * b + 2]), ACT.Copy).then_inc(s["v2_d"], 1)
            def head_exps(u):
                b, h = head_of(u)
                act.wait_ge(s["max2_d"], u + 1)
                if u >= P2_RING:
                    act.wait_ge(s["t2_p"], u - P2_RING + 1)
                for t in range(NT):
                    nc.scalar.activation(p2[u % P2_RING][:, t, :], tiles(bank[u % S2_BANKS])[:, t, :], ACT.Exp,
                                         bias=nmax2[b][:, h, t:t + 1], accum_out=sum2[b][:, t, h:h + 1]).then_inc(s["e2_d"], 1)

            def head_evac(u):
                act.wait_ge(s["t2_p"], u + 1)
                if u >= PT2_RING:
                    act.wait_ge(s["pv2_p"], (u - PT2_RING) // HG + 1)
                nc.scalar.activation(pT2[u % PT2_RING][:, :, :], tiles(bank[4 + u % T2_BANKS]), ACT.Copy).then_inc(s["pT2o_d"], 1)

            def rb2_evac(b):
                act.wait_ge(s["rb2_p"], b + 1)
                nc.scalar.activation(rb2[b][:, :], LA[b][:, 0:N], ACT.Copy).then_inc(s["rb2_d"], 1)

            def shift_left_edge(b):
                act.wait_ge(s["f_d"], b + 1)
                act.wait_ge(s["zeroed"], 3 * NB)
                nc.scalar.activation(fsh[0][b][:, 1:H + 1, 1:W], fsh[1][b][:, 1:H + 1, 0:W - 1], ACT.Copy).then_inc(s["f0_d"], 1)

            def k1x1_evac(b):
                act.wait_ge(s["k1x1_p"], b + 1)
                nc.scalar.activation(k1x1[b][:, :, :].rearrange("p h w -> p (h w)"), LB[b][:, 0:N], ACT.Copy).then_inc(s["k1x1_d"], 1)

            def q_exp(b):
                act.wait_ge(s["qs_d"], b + 1)
                nc.scalar.activation(eq[b][:, :, :, :], qs[b][:, :, :, :], ACT.Exp).then_inc(s["eq_d"], 1)

            def k_exp(b):
                act.wait_ge(s["k3m_d"], b + 1)
                nc.scalar.activation(ek[b][:, :], kc[b][:, :], ACT.Exp, bias=nmk[b][:, :],
                                     accum_out=sumk[b][:, :]).then_inc(s["ek_d"], 1)

            def ekT_evac(b):
                act.wait_ge(s["ekT_p"], b + 1)
                nc.scalar.activation(ekT[b][:, :, :], tiles(LB[b], 4)[:, 0:NT, :], ACT.Copy).then_inc(s["ekT_d"], 1)

            def v3_evac(b):
                act.wait_ge(s["v3_p"], b + 1)
                nc.scalar.activation(v3[b][:, :, :], tiles(LD[b], 4)[:, 0:NT, :], ACT.Copy).then_inc(s["v3_d"], 1)

            def qT_evac(b):
                act.wait_ge(s["qT_p"], b + 1)
                nc.scalar.activation(qT[b][:, :], LB[b][:, 0:N], ACT.Copy).then_inc(s["qT_d"], 1)

            def o3_tanh(b):
                act.wait_ge(s["o3_p"], b + 1)
                nc.scalar.activation(th[b][:, :], LA[b][:, 0:N], ACT.Tanh, scale=0.5).then_inc(s["th_d"], 1)

            def yc_evac(b):
                act.wait_ge(s["yc_p"], b + 1)
                nc.scalar.activation(ycg[b][:, :], LC[b][:, 0:N], ACT.Copy, scale=A("out_norm_g")).then_inc(s["ycg_d"], 1)

            def gelu(b):
                act.wait_ge(s["rs5_d"], b + 1)
                act.wait_ge(s["h_p"], b + 1)
                for t in range(NT):
                    nc.scalar.activation(h3[b][:, t, :], tiles(LD[b])[:, t, :], ACT.Gelu,
                                         scale=rs3[b][:, 2, t:t + 1]).then_inc(s["h_d"], 1)

            def hT_evac(b):
                act.wait_ge(s["hT_p"], b + 1)
                nc.scalar.activation(hT3[b][:, :, :], tiles(LC[b]), ACT.Copy).then_inc(s["hT_d"], 1)

            def rb6_evac(b):
                act.wait_ge(s["rb6_p"], b + 1)
                nc.scalar.activation(rb4[b][:, :], LB[b][:, 0:N], ACT.Copy).then_inc(s["rb6_d"], 1)

            between = {11: rb2_evac, 15: shift_left_edge, 16: k1x1_evac}
            for u in range(STEPS + 2):
                if u < STEPS:
                    head_exps(u)
                if u >= 2 and u % 2:
                    head_evac(u - 2)
                if u in between:
                    between[u](0)
            for stage, b in ((rb2_evac, 1), (q_exp, 0), (k_exp, 0), (v3_evac, 0), (ekT_evac, 0), (shift_left_edge, 1), (k1x1_evac, 1),
                             (qT_evac, 0), (o3_tanh, 0), (q_exp, 1), (k_exp, 1), (yc_evac, 0),
                             (ekT_evac, 1), (v3_evac, 1), (qT_evac, 1), (o3_tanh, 1), (gelu, 0), (yc_evac, 1),
                             (hT_evac, 0), (rb6_evac, 0), (gelu, 1), (hT_evac, 1), (rb6_evac, 1)):
                stage(b)

        @block.vector
        def _(dve):
            counts = {}

            def vec_done(name):
                counts.setdefault(name, []).append(sum(len(c) for c in counts.values()) + 1)

            def vec_at(name, nth):
                return counts[name][nth - 1]

            def vec_last(name):
                return counts[name][-1]

            def norm_stats(b, n, src, ready, ve_d, count):
                dve.wait_ge(ready, count)
                for t in range(NT):
                    nc.vector.bn_stats(st3[b][:, n, t, :], src(t)).then_inc(s["vec"], 1)
                    vec_done("st")
                dve.wait_ge(s["vec"], vec_last("st"))
                for t in range(NT):
                    nc.vector.bn_aggr(mv3[b][:, n, t, :], st3[b][:, n, t, :]).then_inc(s["vec"], 1)
                    vec_done("mv")
                dve.wait_ge(s["vec"], vec_last("mv"))
                nc.vector.tensor_scalar_add(ve3[b][:, n, :], mv3[b][:, n, :, 1], EPS_LN).then_inc(ve_d, 1)

            def row_max(b, scores, ready, nm, max_d):
                dve.wait_ge(ready, b + 1)
                nc.vector.tensor_reduce(nm, tiles(scores), AX.X, ALU.max, negate=True).then_inc(max_d, 1)

            nc.vector.memset(warm[:, :], 0.0).then_inc(s["warm_set"], 1)
            for b in range(NB):
                dve.wait_ge(s["x_in"], 32)
                nc.vector.bn_stats(st0[b][:, :], x0[b][:, :]).then_inc(s["vec"], 1)
                vec_done("st0")
            for b in range(NB):
                dve.wait_ge(s["vec"], vec_at("st0", b + 1))
                nc.vector.bn_aggr(mv0[b][:, :], st0[b][:, :]).then_inc(s["vec"], 1)
                vec_done("mv0")
            for b in range(NB):
                dve.wait_ge(s["vec"], vec_at("mv0", b + 1))
                nc.vector.scalar_tensor_tensor(mv0[b][:, 1:2], mv0[b][:, 0:1], mv0[b][:, 0:1], mv0[b][:, 1:2],
                                               ALU.mult, ALU.add).then_inc(s["gin0_d"], 1)
            for b in range(NB):
                dve.wait_ge(s["g0_p"], b + 1)
                nc.vector.tensor_copy(gs0[b][:, :], bank[4 * b][:, 0:2]).then_inc(s["vec"], 1)
                vec_done("g0")
            for b in range(NB):
                dve.wait_ge(s["vec"], vec_at("g0", b + 1))
                nc.vector.scalar_tensor_tensor(sm0[b][:, 0:1], gs0[b][:, 0:1], -1.0, gs0[b][:, 0:1],
                                               ALU.mult, ALU.mult).then_inc(s["vec"], 1)
                vec_done("nm0")
            for b in range(NB):
                dve.wait_ge(s["vec"], vec_at("nm0", b + 1))
                nc.vector.scalar_tensor_tensor(sm0[b][:, 1:2], gs0[b][:, 1:2], EPS_GN, sm0[b][:, 0:1],
                                               ALU.add, ALU.add).then_inc(s["ve0_d"], 1)
            dve.wait_ge(s["wpv_p"], 1)
            nc.vector.tensor_copy(wpvT[:, :], bank[3][:, 0:C]).then_inc(s["wpv_w"], 1)
            nc.vector.tensor_add(bias0[:, :], bank[3][:, C:C + 1], A("bp0")).then_inc(s["bias0_w"], 1)
            for b in range(NB):
                dve.wait_ge(s["rstd0_d"], b + 1)
                nc.vector.tensor_mul(sm0[b][:, 3:4], sm0[b][:, 2:3], A("gamma")).then_inc(s["vec"], 1)
                vec_done("a0")
                dve.wait_ge(s["vec"], vec_at("a0", b + 1))
                nc.vector.tensor_mul(sm0[b][:, 4:5], sm0[b][:, 3:4], gs0[b][:, 0:1]).then_inc(s["vec"], 1)
                vec_done("ma0")
                dve.wait_ge(s["vec"], vec_at("ma0", b + 1))
                nc.vector.tensor_sub(sm0[b][:, 5:6], A("beta"), sm0[b][:, 4:5]).then_inc(s["vec"], 1)
                vec_done("b0")
                dve.wait_ge(s["vec"], vec_at("b0", b + 1))
                nc.vector.tensor_scalar(hn0[b][:, :], x0[b][:, :], sm0[b][:, 3:4], sm0[b][:, 5:6],
                                        ALU.mult, ALU.add).then_inc(s["hn0_d"], 1)
            for b in range(NB):
                dve.wait_ge(s["q0_p"], b + 1)
                nc.vector.tensor_scalar(q0[b][:, :], bank[4 * b][:, 0:N], A("bq0"), float(C) ** -0.5,
                                        ALU.add, ALU.mult).then_inc(s["q0_d"], 1)
            dve.wait_ge(s["bias0_w"], 1)
            for b in range(NB):
                nc.vector.tensor_scalar_add(xb0[b][:, :], x0[b][:, :], bias0[:, :]).then_inc(s["vec"], 1)
                vec_done("xb0")
            for b in range(NB):
                row_max(b, bank[4 * b + 3], s["s0_p"], nmax[b][:, 0:NT], s["max0_d"])
            dve.wait_ge(s["c_in"], 16)
            nc.vector.tensor_scalar_mul(wg[:, :], K("w1x1T"), A("norm_g")).then_inc(s["wg_done"], 1)
            for b in range(NB):
                dve.wait_ge(s["e0_d"], NT * (b + 1))
                nc.vector.reciprocal(rsum[b][:, 0:NT], psum_[b][:, 0:NT]).then_inc(s["rs0_d"], 1)
                dve.wait_ge(s["t0_p"], b + 1)
                nc.vector.tensor_copy(pT0[b][:, :, :], tiles(bank[4 * b])).then_inc(s["pT0_d"], 1)
            nc.vector.tensor_mul(gbv[:, :], A("gpam"), A("bv1")).then_inc(s["gbv_w"], 1)
            for b in range(NB):
                dve.wait_ge(s["pv0_p"], b + 1)
                dve.wait_ge(s["rb0_d"], b + 1)
                nc.vector.tensor_mul(t0[b][:, :], bank[4 * b + 2][:, 0:N], rb0[b][:, :]).then_inc(s["vec"], 1)
                vec_done("n0")
                dve.wait_ge(s["vec"], vec_at("n0", b + 1))
                dve.wait_ge(s["vec"], vec_at("xb0", b + 1))
                nc.vector.tensor_add(x1[b][:, :], t0[b][:, :], xb0[b][:, :]).then_inc(s["x1_d"], 1)

            for b in range(NB):
                dve.wait_ge(s["q1_p"], b + 1)
                nc.vector.tensor_scalar_add(q1[b][:, :], bank[4 * b][:, 0:N], A("bq1")).then_inc(s["q1_d"], 1)
            dve.wait_ge(s["gbv_w"], 1)
            for b in range(NB):
                dve.wait_ge(s["x1_d"], b + 1)
                nc.vector.tensor_scalar_add(xb1[b][:, :], x1[b][:, :], gbv[:, :]).then_inc(s["vec"], 1)
                vec_done("xb1")
            for b in range(NB):
                row_max(b, bank[4 * b + 2], s["s1_p"], nmax[b][:, NT:2 * NT], s["max1_d"])
            nc.vector.tensor_scalar_mul(w1g[:, :], K("w1T"), A("ff_g1")).then_inc(s["w1g_w"], 1)
            for j in range(2):
                nc.vector.tensor_scalar_mul(w2g[:, j, :], tiles(K("w2T"))[:, j, :], A("ff_g2")[:, j:j + 1]).then_inc(s["w2g_w"], 1)
            for b in range(NB):
                dve.wait_ge(s["e1_d"], NT * (b + 1))
                nc.vector.reciprocal(rsum[b][:, NT:2 * NT], psum_[b][:, NT:2 * NT]).then_inc(s["vec"], 1)
                vec_done("rs1")
                dve.wait_ge(s["vec"], vec_at("rs1", b + 1))
                nc.vector.tensor_scalar_mul(rsum[b][:, NT:2 * NT], rsum[b][:, NT:2 * NT], A("gpam")).then_inc(s["rsg1_d"], 1)
                dve.wait_ge(s["t1_p"], b + 1)
                nc.vector.tensor_copy(pT1[b][:, :, :], tiles(bank[4 * b])).then_inc(s["pT1_d"], 1)
            for b in range(NB):
                dve.wait_ge(s["pv1_p"], b + 1)
                dve.wait_ge(s["rb1_d"], b + 1)
                nc.vector.tensor_mul(t1[b][:, :], bank[4 * b + 3][:, 0:N], rb1[b][:, :]).then_inc(s["vec"], 1)
                vec_done("n1")
                dve.wait_ge(s["vec"], vec_at("n1", b + 1))
                dve.wait_ge(s["vec"], vec_at("xb1", b + 1))
                nc.vector.tensor_add(pam[b][:, :], t1[b][:, :], xb1[b][:, :]).then_inc(s["pam_d"], 1)
            for b in range(NB):
                dve.wait_ge(s["pamT_p"], b + 1)
                nc.vector.tensor_copy(pamT[b][:, :, :], tiles(bank[4 * b], 4)[:, 0:NT, :]).then_inc(s["pamT_d"], 1)
            for b in range(NB):
                dve.wait_ge(s["cen_p"], b + 1)
                nc.vector.tensor_reduce(cmin[b][:, :], bank[4 * b + 1][:, 0:C], AX.X, ALU.min).then_inc(s["min_d"], 1)
            for b in range(NB):
                dve.wait_ge(s["ceT_p"], b + 1)
                nc.vector.tensor_copy(ceT[b][:, :], bank[4 * b + 2][:, 0:C]).then_inc(s["ceT_d"], 1)
                nc.vector.reciprocal(cscale[b][:, 0:1], csum[b][:, :]).then_inc(s["vec"], 1)
                vec_done("cr")
                dve.wait_ge(s["vec"], vec_at("cr", b + 1))
                nc.vector.tensor_mul(cscale[b][:, 1:2], cscale[b][:, 0:1], A("gcam")).then_inc(s["vec"], 1)
                vec_done("cs")
            for b in range(NB):
                dve.wait_ge(s["co_p"], b + 1)
                dve.wait_ge(s["vec"], vec_at("cs", b + 1))
                nc.vector.scalar_tensor_tensor(x2[b][:, :], bank[4 * b + 3][:, 0:N], cscale[b][:, 1:2], pam[b][:, :],
                                               ALU.mult, ALU.add).then_inc(s["x2_d"], 1)

            for b in range(NB):
                dve.wait_ge(s["q2_p"], b + 1)
                nc.vector.tensor_scalar(q2[b][:, :], bank[4 * b][:, 0:N], D ** -0.5, None, ALU.mult).then_inc(s["q2_d"], 1)
            for b in range(NB):
                dve.wait_ge(s["x2_d"], b + 1)
                nc.vector.tensor_scalar_add(xb2[b][:, :], x2[b][:, :], A("bout")).then_inc(s["vec"], 1)
                vec_done("xb2")
            nc.vector.tensor_scalar(outwc[:, :], K("outwT"), 0.5, None, ALU.mult).then_inc(s["vec"], 1)
            vec_done("outw_half")
            dve.wait_ge(s["vec"], vec_at("outw_half", 1))
            nc.vector.reduce_sum(outws[:, 0:1], outwc[:, :], AX.X).then_inc(s["vec"], 1)
            vec_done("outw_sum")
            dve.wait_ge(s["vec"], vec_at("outw_sum", 1))
            nc.vector.tensor_scalar(outws[:, 1:2], outws[:, 0:1], -1.0 / C, None, ALU.mult).then_inc(s["vec"], 1)
            vec_done("outw_neg")
            dve.wait_ge(s["vec"], vec_at("outw_neg", 1))
            nc.vector.tensor_scalar_add(outwc[:, :], outwc[:, :], outws[:, 1:2]).then_inc(s["outw_c"], 1)
            dve.wait_ge(s["w2m_p"], 1)
            nc.vector.tensor_sub(w1c[:, :], w1g[:, :], bank[3][:, 0:HID]).then_inc(s["w1c_w"], 1)
            for j in range(2):
                nc.vector.scalar_tensor_tensor(w2c[:, j, :], bank[3][:, HID:HID + C], -0.5, w2g[:, j, :],
                                               ALU.mult, ALU.add).then_inc(s["w2c_w"], 1)

            def head_max(u):
                b, h = head_of(u)
                dve.wait_ge(s["s2_p"], u + 1)
                nc.vector.tensor_reduce(nmax2[b][:, h, :], tiles(bank[u % S2_BANKS]), AX.X, ALU.max, negate=True).then_inc(s["max2_d"], 1)

            def head_evac(u):
                dve.wait_ge(s["t2_p"], u + 1)
                if u >= PT2_RING:
                    dve.wait_ge(s["pv2_p"], (u - PT2_RING) // HG + 1)
                nc.vector.tensor_copy(pT2[u % PT2_RING][:, :, :], tiles(bank[4 + u % T2_BANKS])).then_inc(s["pT2e_d"], 1)

            def head_sums(b):
                dve.wait_ge(s["e2_d"], NT * HEADS * (b + 1))
                nc.vector.reciprocal(rsum2[b][:, :, :], sum2[b][:, :, :]).then_inc(s["rs2_d"], 1)

            def o2_norm(b):
                dve.wait_ge(s["rb2_d"], b + 1)
                dve.wait_ge(s["pv2_p"], NG * (b + 1))
                nc.vector.tensor_mul(o2[b][:, :], bank[4 * b + 3][:, 0:N], rb2[b][:, :]).then_inc(s["o2_d"], 1)

            def x3_sum(b):
                dve.wait_ge(s["w2_p"], b + 1)
                dve.wait_ge(s["vec"], vec_at("xb2", b + 1))
                nc.vector.tensor_add(x3[b][:, :], LC[b][:, 0:N], xb2[b][:, :]).then_inc(s["x3_d"], 1)

            def x3_stats(b):
                norm_stats(b, 0, lambda t: tiles(LA[b], 4)[:, t, :], s["x3T_p"], s["ve3_d"], b + 1)
                dve.wait_ge(s["mean3_p"], b + 1)
                nc.vector.tensor_sub(xc3[b][:, :], x3[b][:, :], LB[b][:, 0:N]).then_inc(s["xc3_d"], 1)

            def f_norm(b):
                dve.wait_ge(s["rb3_p"], b + 1)
                dve.wait_ge(s["xc3_d"], b + 1)
                dve.wait_ge(s["zeroed"], 3 * (b + 1))
                nc.vector.tensor_mul(fsh[1][b][:, 1:H + 1, :], xc3[b][:, :].rearrange("p (h w) -> p h w", h=H),
                                     LC[b][:, 0:N].rearrange("p (h w) -> p h w", h=H)).then_inc(s["f_d"], 1)

            def k_taps(b):
                dve.wait_ge(s["k1x1_d"], b + 1)
                order = [(0, 0), (0, -1)] + [(dy, dx) for dy in (-1, 0, 1) for dx in (-1, 0, 1) if (dy, dx) not in ((0, 0), (0, -1))]
                for n, (dy, dx) in enumerate(order):
                    tap = K("kdw")[:, 3 * (dy + 1) + dx + 1:3 * (dy + 1) + dx + 2]
                    oy, ox = slice(max(0, -dy), H - max(0, dy)), slice(max(0, -dx), W - max(0, dx))
                    iy, ix = slice(max(0, dy), H + min(0, dy)), slice(max(0, dx), W + min(0, dx))
                    if n == 1:
                        dve.wait_ge(s["zeroed"], 3 * NB + b + 1)
                    if n >= 2:
                        dve.wait_ge(s["vec"], vec_at("ktap", TAPS * b + n - 1))
                    if n == 0:
                        nc.vector.tensor_scalar_mul(kacc[b][:, 0, :, :], k1x1[b][:, :, :], tap).then_inc(s["vec"], 1)
                    else:
                        acc = kacc[b][:, n % 2, oy, ox]
                        nc.vector.scalar_tensor_tensor(acc, k1x1[b][:, iy, ix], tap, acc, ALU.mult, ALU.add).then_inc(s["vec"], 1)
                    vec_done("ktap")
                dve.wait_ge(s["vec"], vec_at("ktap", TAPS * (b + 1)))
                nc.vector.tensor_add(kc[b][:, :], kacc[b][:, 0, :, :].rearrange("p h w -> p (h w)"),
                                     kacc[b][:, 1, :, :].rearrange("p h w -> p (h w)")).then_inc(s["vec"], 1)
                vec_done("kc")
                dve.wait_ge(s["vec"], vec_at("kc", b + 1))
                nc.vector.tensor_reduce(nmk[b][:, :], kc[b][:, :], AX.X, ALU.max, negate=True).then_inc(s["k3m_d"], 1)

            def heads(t, b):
                return t[b][:, :, :].unsqueeze(3).broadcast_to([128, NT, HEADS, D])

            def q_max(b):
                dve.wait_ge(s["q3_p"], b + 1)
                q = tiles(LA[b], 4)[:, 0:NT, :].rearrange("p t (h d) -> p t h d", h=HEADS)
                nc.vector.tensor_reduce(mq[b][:, :, :], q, AX.X, ALU.max).then_inc(s["vec"], 1)
                vec_done("mq")
                dve.wait_ge(s["vec"], vec_at("mq", b + 1))
                nc.vector.tensor_tensor(qs[b][:, :, :, :], q, heads(mq, b), ALU.subtract).then_inc(s["qs_d"], 1)

            def q_norm(b):
                dve.wait_ge(s["eq_d"], b + 1)
                nc.vector.reduce_sum(sq[b][:, :, :], eq[b][:, :, :, :], AX.X).then_inc(s["vec"], 1)
                vec_done("sq")
                dve.wait_ge(s["vec"], vec_at("sq", b + 1))
                nc.vector.reciprocal(rq[b][:, :, :], sq[b][:, :, :]).then_inc(s["vec"], 1)
                vec_done("rq")
                dve.wait_ge(s["vec"], vec_at("rq", b + 1))
                nc.vector.tensor_tensor(qn[b][:, :, :, :], eq[b][:, :, :, :], heads(rq, b), ALU.mult).then_inc(s["qn_d"], 1)

            def k_sums(b):
                dve.wait_ge(s["ek_d"], b + 1)
                nc.vector.reciprocal(rsk[b][:, 0:1], sumk[b][:, :]).then_inc(s["vec"], 1)
                vec_done("rkr")
                dve.wait_ge(s["vec"], vec_at("rkr", b + 1))
                nc.vector.tensor_scalar(rsk[b][:, 1:2], rsk[b][:, 0:1], D ** -0.5, None, ALU.mult).then_inc(s["vec"], 1)
                vec_done("rk")

            def context(b):
                dve.wait_ge(s["ctx_p"], b + 1)
                dve.wait_ge(s["vec"], vec_at("rk", b + 1))
                nc.vector.scalar_tensor_tensor(cm[b][:, :], LC[b][:, 0:C], rsk[b][:, 1:2], K("headmask"),
                                               ALU.mult, ALU.mult).then_inc(s["cm_d"], 1)

            def silu(b):
                dve.wait_ge(s["th_d"], b + 1)
                nc.vector.scalar_tensor_tensor(s3[b][:, :], th[b][:, :], 1.0, LA[b][:, 0:N],
                                               ALU.add, ALU.mult).then_inc(s["s3_d"], 1)

            def y_stats(b):
                norm_stats(b, 1, lambda t: tiles(LD[b], 4)[:, t, :], s["yT_p"], s["ve4_d"], b + 1)

            def x4_sum(b):
                dve.wait_ge(s["rb4_p"], b + 1)
                dve.wait_ge(s["ycg_d"], b + 1)
                nc.vector.tensor_mul(x4a[b][:, :], LB[b][:, 0:N], ycg[b][:, :]).then_inc(s["vec"], 1)
                vec_done("x4a")
                dve.wait_ge(s["vec"], vec_at("x4a", b + 1))
                nc.vector.tensor_add(x4[b][:, :], x4a[b][:, :], x3[b][:, :]).then_inc(s["x4_d"], 1)

            def x4_stats(b):
                norm_stats(b, 2, lambda t: tiles(LA[b], 4)[:, t, :], s["x4T_p"], s["ve5_d"], b + 1)

            def h_stats(b):
                norm_stats(b, 3, lambda t: h3[b][:, t, :], s["h_d"], s["ve6_d"], NT * (b + 1))

            def y_sum(b):
                dve.wait_ge(s["ff_p"], b + 1)
                dve.wait_ge(s["rb6_d"], b + 1)
                nc.vector.tensor_mul(fo[b][:, :], LA[b][:, 0:N], rb4[b][:, :]).then_inc(s["vec"], 1)
                vec_done("fo")
                dve.wait_ge(s["vec"], vec_at("fo", b + 1))
                nc.vector.tensor_add(y[b][:, :], fo[b][:, :], x4[b][:, :]).then_inc(s["y_d"], 1)

            between = {8: head_sums, 11: o2_norm, 12: x3_sum, 13: x3_stats, 15: f_norm}
            for u in range(STEPS + 2):
                if u < STEPS:
                    head_max(u)
                if u >= 2 and u % 2 == 0:
                    head_evac(u - 2)
                if u in between:
                    between[u](0)
            for stage, b in ((head_sums, 1), (k_taps, 0), (o2_norm, 1), (q_max, 0), (x3_sum, 1), (x3_stats, 1), (q_norm, 0), (f_norm, 1),
                             (k_sums, 0), (context, 0), (k_taps, 1), (silu, 0), (q_max, 1), (q_norm, 1),
                             (y_stats, 0), (k_sums, 1), (x4_sum, 0), (context, 1), (x4_stats, 0), (silu, 1), (h_stats, 0), (y_stats, 1),
                             (x4_sum, 1), (x4_stats, 1), (y_sum, 0), (h_stats, 1), (y_sum, 1)):
                stage(b)

        @block.tensor
        def _(pe):
            def spread(dst, rows, width=128):
                return nc.tensor.matmul(dst, rows, ident, start=True, stop=True)

            def transposes(dst, src, done):
                for i in range(NT):
                    for t in range(NT):
                        last = nc.tensor.transpose(tiles(dst)[:, i, t * 128:(t + 1) * 128],
                                                   src[:, t, i * 128:(i + 1) * 128], ident)
                last.then_inc(done, 1)

            def keep_clock(n, dst):
                for _ in range(n):
                    nc.tensor.matmul(dst[:, :], warm[:, 0:128], warm[:, :], start=True, stop=True)

            pe.wait_ge(s["warm_set"], 1)
            keep_clock(10, bank[7])
            pe.wait_ge(s["a_in"], 16)
            for b in range(NB):
                pe.wait_ge(s["gin0_d"], b + 1)
                nc.tensor.matmul(bank[4 * b][:, 0:2], A("gmean"), mv0[b][:, :], start=True, stop=True).then_inc(s["g0_p"], 1)
            pe.wait_ge(s["a2_in"], 16)
            nc.tensor.matmul(bank[3][:, 0:C], A("wv0"), A("wpT0"), start=True, stop=True)
            nc.tensor.matmul(bank[3][:, C:C + 1], A("wpT0"), A("bv0"), start=True, stop=True).then_inc(s["wpv_p"], 1)
            keep_clock(3, bank[7])
            for b in range(NB):
                pe.wait_ge(s["hn0_d"], b + 1)
                nc.tensor.matmul(bank[4 * b][:, 0:N], A("wqT0"), hn0[b][:, :], start=True, stop=True).then_inc(s["q0_p"], 1)
                nc.tensor.matmul(bank[4 * b + 1][:, 0:N], A("wkT0"), hn0[b][:, :], start=True, stop=True).then_inc(s["k0_p"], 1)
                pe.wait_ge(s["wpv_w"], 1)
                for t in range(NT):
                    last = nc.tensor.matmul(bank[4 * b + 2][:, t * C:(t + 1) * C], hn0[b][:, t * 128:(t + 1) * 128], wpvT[:, :],
                                            start=True, stop=True)
                last.then_inc(s["v0_p"], 1)
            for b in range(NB):
                pe.wait_ge(s["q0_d"], b + 1)
                pe.wait_ge(s["k0_d"], b + 1)
                pe.wait_ge(s["bias0_w"], 1)
                for t in range(NT):
                    last = nc.tensor.matmul(tiles(bank[4 * b + 3])[:, t, :], q0[b][:, t * 128:(t + 1) * 128], k0[b][:, :],
                                            start=True, stop=True)
                last.then_inc(s["s0_p"], 1)

            def weigh(b, p, e_d, t_p, rs, rs_d, rb_p):
                pe.wait_ge(e_d, NT * (b + 1))
                transposes(bank[4 * b], p[b], t_p)
                pe.wait_ge(rs_d, b + 1)
                for t in range(NT):
                    last = spread(bank[4 * b + 1][:, t * 128:(t + 1) * 128], rs[:, t:t + 1].broadcast_to([128, 128]))
                last.then_inc(rb_p, 1)

            def mix(b, dst, v, pT, v_d, pT_d, done):
                pe.wait_ge(v_d, b + 1)
                pe.wait_ge(pT_d, b + 1)
                for i in range(NT):
                    last = nc.tensor.matmul(dst, v[b][:, i, :], pT[b][:, i, :], start=(i == 0), stop=(i == NT - 1))
                last.then_inc(done, 1)

            for b in range(NB):
                weigh(b, p0, s["e0_d"], s["t0_p"], rsum[b][:, 0:NT], s["rs0_d"], s["rb0_p"])
            for b in range(NB):
                mix(b, bank[4 * b + 2][:, 0:N], v0, pT0, s["v0_d"], s["pT0_d"], s["pv0_p"])

            pe.wait_ge(s["b_in"], 16)
            for b in range(NB):
                pe.wait_ge(s["x1_d"], b + 1)
                nc.tensor.matmul(bank[4 * b][:, 0:N], B("wqT1"), x1[b][:, :], start=True, stop=True).then_inc(s["q1_p"], 1)
                nc.tensor.matmul(bank[4 * b + 1][:, 0:N], B("wkT1"), x1[b][:, :], start=True, stop=True).then_inc(s["k1_p"], 1)
                for t in range(NT):
                    last = nc.tensor.matmul(bank[4 * b + 3][:, t * C:(t + 1) * C], x1[b][:, t * 128:(t + 1) * 128], B("wvT1"),
                                            start=True, stop=True)
                last.then_inc(s["v1_p"], 1)
            for b in range(NB):
                pe.wait_ge(s["q1_d"], b + 1)
                pe.wait_ge(s["k1_d"], b + 1)
                for t in range(NT):
                    last = nc.tensor.matmul(tiles(bank[4 * b + 2])[:, t, :], q1[b][:, t * 128:(t + 1) * 128], k1[b][:, :],
                                            start=True, stop=True)
                last.then_inc(s["s1_p"], 1)
            for b in range(NB):
                weigh(b, p1, s["e1_d"], s["t1_p"], rsum[b][:, NT:2 * NT], s["rsg1_d"], s["rb1_p"])
            for b in range(NB):
                mix(b, bank[4 * b + 3][:, 0:N], v1, pT1, s["v1_d"], s["pT1_d"], s["pv1_p"])
            for b in range(NB):
                pe.wait_ge(s["pam_d"], b + 1)
                for t in range(NT):
                    last = nc.tensor.transpose(bank[4 * b][:, t * C:(t + 1) * C], pam[b][:, t * 128:(t + 1) * 128], ident)
                last.then_inc(s["pamT_p"], 1)
            for b in range(NB):
                pe.wait_ge(s["pamT_d"], b + 1)
                for t in range(NT):
                    last = nc.tensor.matmul(bank[4 * b + 1][:, 0:C], pamT[b][:, t, :], pamT[b][:, t, :],
                                            start=(t == 0), stop=(t == NT - 1))
                last.then_inc(s["cen_p"], 1)
            for b in range(NB):
                nc.tensor.matmul(bank[4 * b][:, 0:N], B("wqe")[0:EMB, :], B("emb")[0:EMB, :], start=True, stop=False)
            for b in range(NB):
                pe.wait_ge(s["ce_d"], b + 1)
                nc.tensor.transpose(bank[4 * b + 2][:, 0:C], ce[b][:, :], ident).then_inc(s["ceT_p"], 1)
                nc.tensor.matmul(bank[4 * b + 1][:, 0:N], B("wke")[0:EMB, :], B("emb")[0:EMB, :], start=True, stop=False)
            for b in range(NB):
                pe.wait_ge(s["ceT_d"], b + 1)
                nc.tensor.matmul(bank[4 * b + 3][:, 0:N], ceT[b][:, :], pam[b][:, :], start=True, stop=True).then_inc(s["co_p"], 1)

            for b in range(NB):
                pe.wait_ge(s["x2_d"], b + 1)
                for n, (wx, done) in enumerate((("wqx", s["q2_p"]), ("wkx", s["k2_p"]))):
                    nc.tensor.matmul(bank[4 * b + n][:, 0:N], B(wx), x2[b][:, :], start=False, stop=True).then_inc(done, 1)
                for t in range(NT):
                    last = nc.tensor.matmul(tiles(bank[4 * b + 2])[:, t, :], x2[b][:, t * 128:(t + 1) * 128], B("wvx"),
                                            start=True, stop=True)
                last.then_inc(s["v2_p"], 1)
            pe.wait_ge(s["c_in"], 16)
            pe.wait_ge(s["w1g_w"], 1)
            pe.wait_ge(s["w2g_w"], 2)
            nc.tensor.matmul(bank[3][:, 0:HID], K("cmean"), w1g[:, :], start=True, stop=True)
            for j in range(2):
                last = nc.tensor.matmul(bank[3][:, HID:HID + C], K("cmean"), w2g[:, j, :], start=(j == 0), stop=(j == 1))
            last.then_inc(s["w2m_p"], 1)
            pe.wait_ge(s["q2_d"], NB)
            pe.wait_ge(s["k2_d"], NB)

            def head_scores(u):
                b, h = head_of(u)
                if u >= S2_BANKS:
                    pe.wait_ge(s["e2_d"], NT * (u - S2_BANKS + 1))
                pe.wait_ge(s["qh2_d"], u + 1)
                for t in range(NT):
                    last = nc.tensor.matmul(tiles(bank[u % S2_BANKS])[:, t, :], qh2[b][:, h, t * 128:(t + 1) * 128], k2[b][:, :],
                                            start=True, stop=True)
                last.then_inc(s["s2_p"], 1)

            def head_transposes(u):
                pe.wait_ge(s["e2_d"], NT * (u + 1))
                if u >= T2_BANKS:
                    pe.wait_ge(s["pT2e_d"] if u % 2 == 0 else s["pT2o_d"], (u - T2_BANKS) // 2 + 1)
                transposes(bank[4 + u % T2_BANKS], p2[u % P2_RING], s["t2_p"])

            def group_mix(grp):
                b, g = divmod(grp, NG)
                pe.wait_ge(s["pT2e_d"], 2 * (grp + 1))
                pe.wait_ge(s["pT2o_d"], 2 * (grp + 1))
                pe.wait_ge(s["v2_d"], b + 1)
                pe.wait_ge(s["w2c_w"], 2)
                for kt in range(NT):
                    for i in range(HG):
                        last = nc.tensor.matmul(bank[4 * b + 3][QUAD * i:QUAD * (i + 1), 0:N],
                                                v2[b][:, kt, g * C + QUAD * i:g * C + QUAD * (i + 1)],
                                                pT2[(grp * HG + i) % PT2_RING][:, kt, :], start=(g == 0 and kt == 0),
                                                stop=(g == NG - 1 and kt == NT - 1), tile_position=(0, QUAD * i), skip_group_check=True)
                last.then_inc(s["pv2_p"], 1)

            def column_spread(dst, rows, done):
                for t in range(NT):
                    last = spread(dst[:, t * 128:(t + 1) * 128], rows(t))
                last.then_inc(done, 1)

            def rb2_spread(b):
                pe.wait_ge(s["rsx2_d"], b + 1)
                pe.wait_ge(s["v2_d"], NB)
                column_spread(LA[b], lambda t: rsx2[b][:, t, :, :].rearrange("p h d -> p (h d)"), s["rb2_p"])

            def w2_out(b):
                pe.wait_ge(s["o2_d"], b + 1)
                nc.tensor.matmul(LC[b][:, 0:N], B("wout"), o2[b][:, :], start=True, stop=True).then_inc(s["w2_p"], 1)

            def x3_transposes(b):
                pe.wait_ge(s["x3_d"], b + 1)
                for t in range(NT):
                    last = nc.tensor.transpose(LA[b][:, t * C:(t + 1) * C], x3[b][:, t * 128:(t + 1) * 128], ident)
                last.then_inc(s["x3T_p"], 1)
                nc.tensor.matmul(LB[b][:, 0:N], K("cmean"), x3[b][:, :], start=True, stop=True).then_inc(s["mean3_p"], 1)

            def rb3_spread(b):
                pe.wait_ge(s["rs3_d"], b + 1)
                column_spread(LC[b], lambda t: rs3[b][:, 0, t:t + 1].broadcast_to([128, 128]), s["rb3_p"])

            def k_1x1(b):
                pe.wait_ge(s["f_d"], b + 1)
                nc.tensor.matmul(LB[b][:, 0:N], wg[:, 0:C], fsh[1][b][:, 1:H + 1, :].rearrange("p h w -> p (h w)"),
                                 start=True, stop=True).then_inc(s["k1x1_p"], 1)

            def conv(dst, b, j, which, done):
                pe.wait_ge(s["conv_w"], TAPS)
                for n, (dx, dy) in enumerate((dx, dy) for dx in (1, 0, 2) for dy in range(3)):
                    if dx == 0 and dy == 0:
                        pe.wait_ge(s["f0_d"], b + 1)
                    if dx == 2 and dy == 0:
                        pe.wait_ge(s["f2_d"], b + 1)
                    row = dy + j * (H // NT)
                    last = nc.tensor.matmul(dst[:, j * C:(j + 1) * C], fsh[dx][b][:, row:row + H // NT, :].rearrange("p h w -> p (h w)"),
                                            convw[:, 3 * dy + dx, which, :], start=(n == 0), stop=(n == TAPS - 1))
                if j == NT - 1:
                    last.then_inc(done, 1)

            def conv_q0(b):
                conv(LA[b], b, 0, 0, s["q3_p"])

            def conv_q1(b):
                conv(LA[b], b, 1, 0, s["q3_p"])

            def conv_v0(b):
                if b == 0:
                    pe.wait_ge(s["pT2o_d"], STEPS // 2)
                conv(LD[b], b, 0, 1, s["v3_p"])

            def conv_v1(b):
                conv(LD[b], b, 1, 1, s["v3_p"])

            def ek_transposes(b):
                pe.wait_ge(s["ek_d"], b + 1)
                for t in range(NT):
                    last = nc.tensor.transpose(LB[b][:, t * C:(t + 1) * C], ek[b][:, t * 128:(t + 1) * 128], ident)
                last.then_inc(s["ekT_p"], 1)

            def ctx_product(b):
                pe.wait_ge(s["ekT_d"], b + 1)
                pe.wait_ge(s["v3_d"], b + 1)
                for t in range(NT):
                    last = nc.tensor.matmul(LC[b][:, 0:C], ekT[b][:, t, :], v3[b][:, t, :], start=(t == 0), stop=(t == NT - 1))
                last.then_inc(s["ctx_p"], 1)

            def q_transposes(b):
                pe.wait_ge(s["qn_d"], b + 1)
                pe.wait_ge(s["ekT_d"], b + 1)
                for t in range(NT):
                    last = nc.tensor.transpose(LB[b][:, t * 128:(t + 1) * 128],
                                               qn[b][:, t, :, :].rearrange("p h d -> p (h d)"), ident)
                last.then_inc(s["qT_p"], 1)

            def o3_product(b):
                pe.wait_ge(s["cm_d"], b + 1)
                pe.wait_ge(s["qT_d"], b + 1)
                nc.tensor.matmul(LA[b][:, 0:N], cm[b][:, :], qT[b][:, :], start=True, stop=True).then_inc(s["o3_p"], 1)

            def y_products(b):
                pe.wait_ge(s["outw_c"], 1)
                pe.wait_ge(s["s3_d"], b + 1)
                for t in range(NT):
                    last = nc.tensor.matmul(LD[b][:, t * C:(t + 1) * C], s3[b][:, t * 128:(t + 1) * 128], outwc[:, :],
                                            start=True, stop=True)
                last.then_inc(s["yT_p"], 1)
                nc.tensor.matmul(LC[b][:, 0:N], outwc[:, :], s3[b][:, :], start=True, stop=True).then_inc(s["yc_p"], 1)

            def rb4_spread(b):
                pe.wait_ge(s["rs4_d"], b + 1)
                column_spread(LB[b], lambda t: rs3[b][:, 1, t:t + 1].broadcast_to([128, 128]), s["rb4_p"])

            def h_products(b):
                pe.wait_ge(s["x4_d"], b + 1)
                pe.wait_ge(s["w1c_w"], 1)
                for t in range(NT):
                    last = nc.tensor.transpose(LA[b][:, t * C:(t + 1) * C], x4[b][:, t * 128:(t + 1) * 128], ident)
                last.then_inc(s["x4T_p"], 1)
                for t in range(NT):
                    last = nc.tensor.matmul(tiles(LD[b])[:, t, :], x4[b][:, t * 128:(t + 1) * 128], w1c[:, :], start=True, stop=True)
                last.then_inc(s["h_p"], 1)

            def h_transposes(b):
                pe.wait_ge(s["h_d"], NT * (b + 1))
                transposes(LC[b], h3[b], s["hT_p"])

            def ff_product(b):
                pe.wait_ge(s["hT_d"], b + 1)
                for j in range(2):
                    last = nc.tensor.matmul(LA[b][:, 0:N], w2c[:, j, :], hT3[b][:, j, :], start=(j == 0), stop=(j == 1))
                last.then_inc(s["ff_p"], 1)

            def rb6_spread(b):
                pe.wait_ge(s["rs6_d"], b + 1)
                column_spread(LB[b], lambda t: rs3[b][:, 3, t:t + 1].broadcast_to([128, 128]), s["rb6_p"])

            between = {10: rb2_spread, 12: w2_out, 13: x3_transposes, 14: rb3_spread, 15: k_1x1, 16: conv_q0, 17: conv_q1}
            for u in range(STEPS + 3):
                if u < STEPS:
                    head_scores(u)
                if 2 <= u < STEPS + 2:
                    head_transposes(u - 2)
                if u >= 3 and (u - 3) % HG == HG - 1:
                    group_mix((u - 3) // HG)
                if u in between:
                    between[u](0)
            for stage, b in ((rb2_spread, 1), (conv_v0, 0), (w2_out, 1), (conv_v1, 0), (x3_transposes, 1), (ek_transposes, 0), (ctx_product, 0), (rb3_spread, 1), (k_1x1, 1),
                             (conv_q0, 1), (q_transposes, 0),
                             (conv_q1, 1), (o3_product, 0), (conv_v0, 1), (y_products, 0),
                             (conv_v1, 1), (rb4_spread, 0), (ek_transposes, 1), (ctx_product, 1), (q_transposes, 1), (h_products, 0),
                             (o3_product, 1), (y_products, 1), (h_transposes, 0), (rb4_spread, 1), (ff_product, 0),
                             (h_products, 1), (rb6_spread, 0), (h_transposes, 1), (ff_product, 1), (rb6_spread, 1)):
                stage(b)



def _embedding():
    import numpy as np
    f = np.float32
    nf = nt = EMB // 4
    ln_x = np.concatenate([np.array([-2.0], f), np.log2(np.arange(1, H * nf, dtype=f))])
    ln_x = ln_x.reshape(H, nf).T * np.arange(1, nf + 1, dtype=f)[:, None]
    freq = np.stack([np.cos(ln_x), np.sin(ln_x)], axis=1).reshape(2 * nf, H).astype(f)
    k = np.arange(0, nt, dtype=f) + f(0.5)
    xs = np.arange(0, nt * W, dtype=f).reshape(W, nt).T
    theta = (k[:, None] * xs / f(W * nt) * f(6.283185307179586)).astype(f)
    time = np.stack([np.cos(theta), np.sin(theta)], axis=1).reshape(2 * nt, W).astype(f)
    freq = np.broadcast_to(freq[:, :, None], (2 * nf, H, W))
    time = np.broadcast_to(time[:, None, :], (2 * nt, H, W))
    return np.concatenate([freq, time], axis=0).reshape(EMB, N)


def _layout(inputs):
    import numpy as np
    g = {k: np.asarray(v) for k, v in inputs.items()}
    f = np.float32

    def pad(w):
        return np.concatenate([w, np.zeros((w.shape[0], C - w.shape[1]), f)], axis=1)

    def head_groups(w):
        o = np.zeros((w.shape[0], NG, HG, NG, D), f)
        for n in range(NG):
            o[:, n, :, n, :] = w.reshape(-1, HG, NG, D)[:, :, n, :]
        return o.reshape(-1, NG * C)

    cols = {
        "ident": np.eye(C, dtype=f),
        "gmean": np.kron(np.eye(C // GN_GROUP, dtype=f), np.full((GN_GROUP, GN_GROUP), 1.0 / GN_GROUP, f)),
        "wqT0": g["L0_conv_wq"].T, "wkT0": g["L0_conv_wk"].T, "wv0": g["L0_conv_wv"], "wpT0": g["L0_conv_wp"].T,
        "gamma": g["L0_conv_gamma"], "beta": g["L0_conv_beta"], "bq0": g["L0_conv_bq"], "bk0": g["L0_conv_bk"],
        "bv0": g["L0_conv_bv"], "bp0": g["L0_conv_bp"], "bq1": g["L1_conv_bq"], "bk1": g["L1_conv_bk"],
        "bv1": g["L1_conv_bv"], "gpam": np.broadcast_to(g["L1_conv_gamma_pam"], (C,)),
        "gcam": np.broadcast_to(g["L1_conv_gamma_cam"], (C,)), "bout": g["L2_conv_bout"],
        "norm_g": g["L3_conv_norm_g"].reshape(C), "out_norm_g": g["L3_conv_out_norm_g"].reshape(C),
        "ff_g1": g["L3_conv_ff_g1"].reshape(C), "ff_g2": g["L3_conv_ff_g2"].reshape(2, C).T,
        "wqT1": pad(g["L1_conv_Wq"].T), "wkT1": pad(g["L1_conv_Wk"].T), "wvT1": g["L1_conv_Wv"].T,
        "wqx": g["L2_conv_Wq"][:C], "wkx": g["L2_conv_Wk"][:C], "wqe": g["L2_conv_Wq"][C:], "wke": g["L2_conv_Wk"][C:],
        "emb": _embedding(), "headcol": np.kron(np.eye(HEADS, dtype=f), np.ones((D, 1), f)),
        "wvx": head_groups(g["L2_conv_Wv"]), "wout": g["L2_conv_Wout"],
        "w1x1T": np.concatenate([g["L3_conv_k_w"].T, g["L3_conv_q_w"].T, g["L3_conv_v_w"].T], axis=1),
        "cmean": np.full((C, C), 1.0 / C, f),
        "headmask": np.kron(np.eye(HEADS, dtype=f), np.ones((D, D), f)),
        "kdw": g["L3_conv_k_dw"].reshape(C, TAPS), "outwT": g["L3_conv_out_w"].T, "w1T": g["L3_conv_ff_w1"].T,
        "w2T": g["L3_conv_ff_w2"].T.reshape(2, C, C).transpose(1, 0, 2).reshape(C, 2 * C),
    }

    def pack(names):
        at, width = places(names)
        o = np.zeros((128, width), f)
        for name, (lo, hi) in at.items():
            a = cols[name].reshape(cols[name].shape[0], hi - lo)
            o[:a.shape[0], lo:hi] = a
        return o

    taps = np.stack([g[f"L3_conv_{n}_dw"].reshape(C, TAPS).T for n in "qv"], axis=1)
    return {"x": g["x"], "pack_a": pack(PACK_A), "pack_b": pack(PACK_B), "pack_c": pack(PACK_C),
            "taps": np.ascontiguousarray(taps.reshape(TAPS * 2 * C))}


def kernel(**inputs):
    import numpy as _np
    import concourse.bacc as _bacc
    from concourse import mybir as _mybir
    from concourse.bass_utils import run_bass_kernel_spmd as _run

    nc = _bacc.Bacc("TRN2", target_bir_lowering=False, num_devices=1)
    arrays, args = {}, []
    for name, a in _layout(inputs).items():
        a = _np.ascontiguousarray(a)
        arrays[f"in_{name}"] = a
        args.append(nc.dram_tensor(f"in_{name}", a.shape, _mybir.dt.from_np(a.dtype), kind="ExternalInput").ap())
    args.append(nc.dram_tensor("out_0", (NB, C, H, W), _mybir.dt.float32, kind="ExternalOutput").ap())
    build(nc, *args)
    return _run(nc, [arrays], core_ids=[0]).results[0]["out_0"]
```

```python
import concourse.bass as bass
from concourse import mybir
from contextlib import ExitStack

NB = 2
C = 128
H = W = 16
N = H * W
NT = N // 128
CQ = C // 8
HEADS, D = 8, 16
QUAD = 32
HG = C // QUAD
NG = HEADS // HG
EMB = 64
HID = 2 * C
TAPS = 9
PARTS = 3
PAIRS = C // D
GN_GROUP = 4
EPS_GN, EPS_LN = 1e-6, 1e-5

PACK_A = [("gmean", C),
          ("gamma", 1), ("beta", 1), ("bq0", 1), ("bk0", 1), ("bv0", 1), ("bp0", 1),
          ("bq1", 1), ("bk1", 1), ("bv1", 1), ("gpam", 1), ("gcam", 1), ("bout", 1),
          ("norm_g", 1), ("out_norm_g", 1), ("ff_g1", 1), ("ff_g2", 2),
          ("wqT0", C), ("wkT0", C), ("wv0", C), ("wpT0", C), ("ident", C)]
FIRST_A = PACK_A[:-5]
PACK_B = [("wqkT1", 2 * QUAD), ("wvT1", C),
          ("wqx", C), ("wkx", C), ("wqe", C), ("wke", C), ("emb", N), ("headcol", HEADS),
          ("wv2", C), ("wout", C)]
PACK_C = [("w1x1T", 3 * C), ("cmean", C), ("headmask", C), ("outwT", C), ("w1T", HID), ("w2T", HID), ("kdw", TAPS), ("vdw", TAPS)]


def places(pack):
    at, out = 0, {}
    for name, width in pack:
        out[name] = (at, at + width)
        at += width
    return out, at


def build(nc, x, pack_a, pack_b, pack_c, taps, out):
    fp32 = mybir.dt.float32
    ALU = mybir.AluOpType
    ACT = mybir.ActivationFunctionType
    AX = mybir.AxisListType

    with ExitStack() as ctx:
        def sb(name, shape):
            return ctx.enter_context(nc.sbuf_tensor(name, shape, fp32))

        def sb16(name, shape):
            return ctx.enter_context(nc.sbuf_tensor(name, shape, mybir.dt.bfloat16))

        def sem(name):
            return ctx.enter_context(nc.semaphore(name))

        at_a, width_a = places(PACK_A)
        at_b, width_b = places(PACK_B)
        at_c, width_c = places(PACK_C)
        wa, wb, wc = sb("wa", [128, width_a]), sb("wb", [128, width_b]), sb("wc", [128, width_c])

        def A(name):
            return wa[:, at_a[name][0]:at_a[name][1]]

        def B(name):
            return wb[:, at_b[name][0]:at_b[name][1]]

        def K(name):
            return wc[:, at_c[name][0]:at_c[name][1]]

        ident = A("ident")
        tapw = sb("tapw", [128, TAPS * C])
        convw = sb("convw", [128, TAPS, C])
        wg = sb("wg", [128, 3 * C])
        wpvT = sb("wpvT", [128, C])
        bias0 = sb("bias0", [128, 1])
        gbv = sb("gbv", [128, 1])
        outwc = sb("outwc", [128, C])
        outws = sb("outws", [128, 2])
        w1c = sb("w1c", [128, HID])
        w1g = sb("w1g", [128, HID])
        w2c = sb("w2c", [128, 2, C])
        w2g = sb("w2g", [128, 2, C])
        warm = sb16("warm", [128, 512])
        gelu_first = sb("gelu_first", [128, 1])
        mhalf = sb("mhalf", [128, 4])

        def per_batch(name, shape):
            return [sb(f"{name}_{b}", shape) for b in range(NB)]

        x0 = per_batch("x0", [128, N])
        st0 = per_batch("st0", [128, 6])
        mv0 = sb("mv0", [128, NB, 2])
        gs0 = sb("gs0", [128, NB, 2])
        nm0, ve0, rstd0, a0, ma0, nb0 = (sb(name, [128, NB]) for name in ("nm0", "ve0", "rstd0", "a0", "ma0", "nb0"))
        hn0 = per_batch("hn0", [128, N])
        xb0 = per_batch("xb0", [128, N])
        q0, k0 = per_batch("q0", [128, N]), per_batch("k0", [128, N])
        v0 = per_batch("v0", [128, NT, C])
        nmax = per_batch("nmax", [128, 2 * NT])
        psums = per_batch("sums", [128, 2 * NT])
        rsum0, rsum1 = per_batch("rsum0", [128, NT]), per_batch("rsum1", [128, NT])
        p0, pT0 = per_batch("p0", [128, NT, N]), per_batch("pT0", [128, NT, N])
        rb0, t0, x1 = per_batch("rb0", [128, N]), per_batch("t0", [128, N]), per_batch("x1", [128, N])
        xb1 = per_batch("xb1", [128, N])
        q1, k1 = per_batch("q1", [QUAD, N]), per_batch("k1", [QUAD, N])
        v1 = per_batch("v1", [128, NT, C])
        p1, pT1 = p0, pT0
        rb1, t1, pam = per_batch("rb1", [128, N]), per_batch("t1", [128, N]), per_batch("pam", [128, N])
        pamT = per_batch("pamT", [128, NT, C])
        cmin, csum, cscale = per_batch("cmin", [128, 1]), per_batch("csum", [128, 1]), per_batch("cscale", [128, 2])
        ce, ceT = per_batch("ce", [128, C]), per_batch("ceT", [128, C])
        x2, xb2 = per_batch("x2", [128, N]), per_batch("xb2", [128, N])
        qe2, ke2 = sb("qe2", [128, N]), sb("ke2", [128, N])
        q2, k2 = per_batch("q2", [128, N]), per_batch("k2", [128, N])
        qh2 = sb("qh2", [128, HEADS, N])
        parts2, rest2 = [sb16(f"parts2_{n}", [128, PARTS, N]) for n in "qk"], [sb(f"rest2_{n}", [128, N]) for n in "qk"]
        stack2 = [sb16(f"stack2_{n}", [128, HEADS, N]) for n in "qk"]
        stacks_dram = [nc.dram_tensor(f"stacks_{n}", (HEADS, D, PAIRS, N), mybir.dt.bfloat16, kind="Internal").ap() for n in "qk"]
        v2 = per_batch("v2", [128, NT, NG * C])
        nmax2 = per_batch("nmax2", [128, HEADS, NT])
        sum2, rsum2 = per_batch("sum2", [128, NT, HEADS]), per_batch("rsum2", [128, NT, HEADS])
        rsx2 = per_batch("rsx2", [128, NT, HEADS, D])
        S2_BANKS, T2_BANKS, P2_RING, PT2_RING = 3, 2, 4, 2 * HG
        LAG = 3
        p2 = [sb(f"p2_{i}", [128, NT, N]) for i in range(P2_RING)]
        pT2 = [sb(f"pT2_{i}", [128, NT, N]) for i in range(PT2_RING)]
        rb2, o2 = per_batch("rb2", [128, N]), per_batch("o2", [128, N])
        x3, xc3 = per_batch("x3", [128, N]), per_batch("xc3", [128, N])
        st3 = per_batch("st3", [128, 4, NT, 6])
        mv3 = per_batch("mv3", [128, 4, NT, 2])
        ve3 = per_batch("ve3", [128, 4, NT])
        rs3 = per_batch("rs3", [128, 4, NT])
        fsh = [per_batch(f"fsh{dx}", [128, H + 2, W]) for dx in range(3)]
        vacc = per_batch("vacc", [128, H, W])
        vprod = [p2[n // NT][:, n % NT, :].rearrange("p (h w) -> p h w", h=H) for n in range(TAPS - 1)]
        kacc = per_batch("kacc", [128, 2, H, W])
        kc = per_batch("kc", [128, N])
        nmk, sumk, rsk = per_batch("nmk", [128, 1]), per_batch("sumk", [128, 1]), per_batch("rsk", [128, 2])
        ek, ekT = per_batch("ek", [128, N]), per_batch("ekT", [128, NT, C])
        v3 = per_batch("v3", [128, NT, C])
        mq, sq, rq = (per_batch(n, [128, NT, HEADS]) for n in ("mq", "sq", "rq"))
        qs, eq, qn = (per_batch(n, [128, NT, HEADS, D]) for n in ("qs", "eq", "qn"))
        qT, cm = per_batch("qT", [128, N]), per_batch("cm", [128, C])
        th, s3 = per_batch("th", [128, N]), per_batch("s3", [128, N])
        ycg, x4a, x4 = per_batch("ycg", [128, N]), per_batch("x4a", [128, N]), per_batch("x4", [128, N])
        h3, hT3 = per_batch("h3", [128, NT, HID]), per_batch("hT3", [128, 2, N])
        rb4, fo, y = per_batch("rb4", [128, N]), per_batch("fo", [128, N]), per_batch("y", [128, N])

        bank = [ctx.enter_context(nc.psum_tensor(f"bank{i}", [128, 512], fp32)) for i in range(8)]

        def tiles(t, n=NT):
            return t[:, :].rearrange("p (t c) -> p t c", t=n)

        LA, LB, LC, LD = (bank[6], bank[4]), (bank[3], bank[7]), (bank[2], bank[0]), (bank[5], bank[1])
        STEPS = NB * HEADS

        def head_of(u):
            b, n = divmod(u, HEADS)
            g, i = divmod(n, HG)
            return b, NG * i + g

        CENTRE_FIRST = [(0, 0), (0, -1)] + [(dy, dx) for dy in (-1, 0, 1) for dx in (-1, 0, 1) if (dy, dx) not in ((0, 0), (0, -1))]

        def tap(name, dy, dx):
            return K(name)[:, 3 * (dy + 1) + dx + 1:3 * (dy + 1) + dx + 2]

        def shifted(dy, dx):
            return ((slice(max(0, -dy), H - max(0, dy)), slice(max(0, -dx), W - max(0, dx))),
                    (slice(max(0, dy), H + min(0, dy)), slice(max(0, dx), W + min(0, dx))))

        NAMES = """a2_in warm_set vec a_in x_in b_in c_in tap_in zeroed mhalf_set wg_done conv_w wpv_p wpv_w bias0_w gbv_w outw_c w1g_w w1c_w
            w2g_w w1m_p w2m_p w2c_w gin0_d g0_p ve0_d rstd0_d hn0_d q0_p k0_p v0_p q0_d k0_d v0_d s0_p max0_d e0_d
            rs0_d t0_p pT0_d rb0_p rb0_d pv0_p x1_d qk1_p v1_p q1_d k1_d v1_d s1_p max1_d e1_d rs1_d t1_p
            pT1_d pT0b_d pT1b_d rb1_p rb1_d pv1_p pam_d pamT_p pamT_d cen_p min_d ce_d ceT_p ceT_d co_p x2_d q2_p k2_p v2_p
            q2_d k2_d v2_d s2_p e2_d t2_p pT2e_d pT2o_d pv2_p rs2_d qh2_d rsx2_d f0_d f2_d rb2_p rb2_d o2_d w2_p
            x3_d x3T_p ve3_d rs3_d mean3_p xc3_d rb3_p f_d k3m_d ek_d ekT_p ekT_d v3_d qs_d eq_d qn_d qT_p qT_d
            ctx_p cm_d o3_p th_d s3_d yc_p yT_p ycg_d ve4_d rs4_d rb4_p x4_d x4T_p ve5_d rs5_d h_p h_d ve6_d
            rs6_d rb6_p rb6_d hT_p hT_d ff_p y_d emb_p emb_d v2_zeroed table_set stored part_d rest_d parts_d spilled
            stacks0_in stacks1_in max2_d k1x1_p v1x1_p vprod_d vsum_d v3_p q3_p""".split()
        s = {n: sem(n) for n in NAMES}
        block = ctx.enter_context(nc.Block())

        @block.sync
        def _(sp):
            sp.dma_start(x0[0][:, :], x[0].rearrange("c h w -> c (h w)")).then_inc(s["x_in"], 16)
            first = at_a[FIRST_A[-1][0]][1]
            sp.dma_start(wa[:, 0:first], pack_a[:, 0:first]).then_inc(s["a_in"], 16)
            sp.dma_start(wa[:, first:width_a], pack_a[:, first:width_a]).then_inc(s["a2_in"], 16)
            sp.dma_start(wb[:, :], pack_b).then_inc(s["b_in"], 16)
            sp.dma_start(wc[:, :], pack_c).then_inc(s["c_in"], 16)
            for part in range(PARTS):
                for n, places in enumerate((slice(PARTS * part, min(PARTS * (part + 1), PAIRS)), slice(part, PAIRS, PARTS))):
                    if part < PARTS - 1:
                        sp.wait_ge(s["part_d"], 2 * part + n + 1)
                    else:
                        sp.wait_ge(s["parts_d"], n + 1)
                    rows = stacks_dram[n].rearrange("h d j n -> (h d) j n")[:, places, :]
                    copies = len(range(PAIRS)[places])
                    sp.dma_start(rows, parts2[n][:, part:part + 1, :].broadcast_to([128, copies, N])).then_inc(s["spilled"], 16)
            sp.wait_ge(s["spilled"], 16 * 2 * PARTS)
            for g in range(NG):
                for n in range(2):
                    sp.dma_start(stack2[n][:, g::NG, :], stacks_dram[n][g::NG].rearrange("h d j n -> (d j) h n")).then_inc(s[f"stacks{g}_in"], 16)
            for b in range(NB):
                sp.wait_ge(s["y_d"], b + 1)
                sp.dma_start(out[b].rearrange("c h w -> c (h w)"), y[b][:, :]).then_inc(s["stored"], 16)
            sp.wait_ge(s["stored"], 16 * NB)

        @block.gpsimd
        def _(pool):
            nc.gpsimd.memset(mhalf[:, :], -0.5).then_inc(s["mhalf_set"], 1)
            for b in range(NB):
                for dx in range(3):
                    nc.gpsimd.memset(fsh[dx][b][:, :, :], 0.0).then_inc(s["zeroed"], 1)
            pool.wait_ge(s["mhalf_set"], 1)

            def inverse_root(dst, src, ready, done, b, width):
                pool.wait_ge(ready, b + 1)
                nc.gpsimd.tensor_tensor(dst, src, mhalf[:, 0:width], ALU.pow).then_inc(done, 1)

            inverse_root(rstd0[:, :], ve0[:, :], s["ve0_d"], s["rstd0_d"], 0, NB)
            for b in range(NB):
                nc.gpsimd.memset(v2[b][:, :, :], 0.0).then_inc(s["v2_zeroed"], 1)
            pool.wait_ge(s["a_in"], 16)
            pool.wait_ge(s["c_in"], 16)
            nc.gpsimd.tensor_scalar(w1g[:, :], K("w1T"), A("ff_g1"), 1.0, ALU.mult, ALU.mult).then_inc(s["w1g_w"], 1)
            for j in range(2):
                nc.gpsimd.tensor_scalar(w2g[:, j, :], tiles(K("w2T"))[:, j, :], A("ff_g2")[:, j:j + 1], 1.0,
                                        ALU.mult, ALU.mult).then_inc(s["w2g_w"], 1)
            nc.gpsimd.tensor_scalar(wg[:, :], K("w1x1T"), A("norm_g"), 1.0, ALU.mult, ALU.mult).then_inc(s["wg_done"], 1)
            pool.wait_ge(s["wg_done"], 1)
            pool.wait_ge(s["tap_in"], 16)
            for t in range(TAPS):
                nc.gpsimd.tensor_tensor(convw[:, t, :], wg[:, C:2 * C], tapw[:, t * C:(t + 1) * C], ALU.mult).then_inc(s["conv_w"], 1)
            for u in range(HEADS):
                b, h = head_of(u)
                pool.wait_ge(s["q2_d"], 1)
                nc.gpsimd.tensor_scalar(qh2[:, h, :], q2[b][:, :], B("headcol")[:, h:h + 1], 1.0,
                                        ALU.mult, ALU.mult).then_inc(s["qh2_d"], 1)
            for b in range(NB):
                nc.gpsimd.memset(kacc[b][:, 1, :, :], 0.0).then_inc(s["zeroed"], 1)

            def root(n, ready, done):
                return lambda b: inverse_root(rs3[b][:, n, :], ve3[b][:, n, :], ready, done, b, NT)

            root3, root4 = root(0, s["ve3_d"], s["rs3_d"]), root(1, s["ve4_d"], s["rs4_d"])
            root5, root6 = root(2, s["ve5_d"], s["rs5_d"]), root(3, s["ve6_d"], s["rs6_d"])

            def v_sums(first, last):
                def stage(b):
                    for n in range(first, last):
                        (oy, ox), (iy, ix) = shifted(*CENTRE_FIRST[n])
                        pool.wait_ge(s["vprod_d"], TAPS * b + n + 1)
                        if n > 1:
                            pool.wait_ge(s["vsum_d"], (TAPS - 1) * b + n - 1)
                        nc.gpsimd.tensor_add(vacc[b][:, oy, ox], vacc[b][:, oy, ox], vprod[n - 1][:, iy, ix]).then_inc(s["vsum_d"], 1)
                return stage

            def rs2_widen(b):
                pool.wait_ge(s["rs2_d"], b + 1)
                nc.gpsimd.tensor_copy(rsx2[b][:, :, :, :], rsum2[b][:, :, :].unsqueeze(3).broadcast_to([128, NT, HEADS, D])).then_inc(s["rsx2_d"], 1)

            for stage, b in ((rs2_widen, 0), (root3, 0), (v_sums(1, 6), 0), (root3, 1), (v_sums(6, TAPS), 0), (v_sums(1, TAPS), 1),
                             (root4, 0), (root4, 1), (root5, 0), (root5, 1), (root6, 0), (root6, 1)):
                stage(b)

        @block.scalar
        def _(act):
            act.dma_start(x0[1][:, :], x[1].rearrange("c h w -> c (h w)")).then_inc(s["x_in"], 16)
            act.dma_start(tapw[:, :], taps.partition_broadcast(128)).then_inc(s["tap_in"], 16)

            def exps(b, src, dst, nm, sums, max_d, e_d):
                act.wait_ge(max_d, b + 1)
                for t in range(NT):
                    nc.scalar.activation(dst[b][:, t, :], tiles(src)[:, t, :], ACT.Exp, bias=nm[:, t:t + 1],
                                         accum_out=sums[:, t:t + 1]).then_inc(e_d, 1)

            def k0_evac(b):
                act.wait_ge(s["k0_p"], b + 1)
                nc.scalar.activation(k0[b][:, :], bank[4 * b + 1][:, 0:N], ACT.Identity, bias=A("bk0")).then_inc(s["k0_d"], 1)

            def v0_evac(b):
                act.wait_ge(s["v0_p"], b + 1)
                nc.scalar.activation(v0[b][:, :, :], tiles(bank[4 * b + 2], 4)[:, 0:NT, :], ACT.Copy).then_inc(s["v0_d"], 1)

            def exps0(b):
                exps(b, bank[4 * b + 3], p0, nmax[b][:, 0:NT], psums[b][:, 0:NT], s["max0_d"], s["e0_d"])

            def p0T_evac(b):
                act.wait_ge(s["t0_p"], b + 1)
                nc.scalar.activation(pT0[b][:, :, :], tiles(bank[4 * b]), ACT.Copy).then_inc(s["pT0b_d"], 1)

            def rb0_evac(b):
                act.wait_ge(s["rb0_p"], b + 1)
                nc.scalar.activation(rb0[b][:, :], bank[4 * b + 1][:, 0:N], ACT.Copy).then_inc(s["rb0_d"], 1)

            def k1_evac(b):
                act.wait_ge(s["qk1_p"], b + 1)
                nc.scalar.activation(k1[b][:, :], bank[4 * b][QUAD:2 * QUAD, 0:N], ACT.Identity, bias=A("bk1")[0:QUAD, :]).then_inc(s["k1_d"], 1)

            def v1_evac(b):
                act.wait_ge(s["v1_p"], b + 1)
                nc.scalar.activation(v1[b][:, :, :], tiles(bank[4 * b + 3], 4)[:, 0:NT, :], ACT.Copy, scale=A("gpam")).then_inc(s["v1_d"], 1)

            def exps1(b):
                exps(b, bank[4 * b + 2], p1, nmax[b][:, NT:2 * NT], psums[b][:, NT:2 * NT], s["max1_d"], s["e1_d"])

            def p1T_evac(b):
                act.wait_ge(s["t1_p"], b + 1)
                nc.scalar.activation(pT1[b][:, :, :], tiles(bank[4 * b]), ACT.Copy).then_inc(s["pT1b_d"], 1)

            def rb1_evac(b):
                act.wait_ge(s["rb1_p"], b + 1)
                nc.scalar.activation(rb1[b][:, :], bank[4 * b + 1][:, 0:N], ACT.Copy).then_inc(s["rb1_d"], 1)

            def pamT_evac(b):
                act.wait_ge(s["pamT_p"], b + 1)
                nc.scalar.activation(pamT[b][:, :, :], tiles(bank[4 * b], 4)[:, 0:NT, :], ACT.Copy).then_inc(s["pamT_d"], 1)

            def energy_exp(b):
                act.wait_ge(s["min_d"], b + 1)
                nc.scalar.activation(ce[b][:, :], bank[4 * b + 1][:, 0:C], ACT.Exp, bias=cmin[b][:, :], scale=-1.0,
                                     accum_out=csum[b][:, :]).then_inc(s["ce_d"], 1)

            for stage, b in ((k0_evac, 0), (k0_evac, 1), (exps0, 0), (exps0, 1), (v0_evac, 0), (rb0_evac, 0), (v0_evac, 1), (p0T_evac, 1),
                             (rb0_evac, 1), (k1_evac, 0), (v1_evac, 0), (k1_evac, 1), (exps1, 0), (exps1, 1), (v1_evac, 1), (rb1_evac, 0),
                             (p1T_evac, 1), (rb1_evac, 1), (pamT_evac, 0), (pamT_evac, 1), (energy_exp, 0), (energy_exp, 1)):
                stage(b)
            def v2_evac(b):
                act.wait_ge(s["v2_p"], b + 1)
                act.wait_ge(s["v2_zeroed"], b + 1)
                heads = tiles(bank[4 * b + 2], 4)[:, 0:NT, :].rearrange("p t (i e d) -> p t i e d", i=HG, e=NG)
                padded = v2[b][:, :, :].rearrange("p t (g i e d) -> p t g i e d", g=NG, i=HG, e=NG)
                for g in range(NG):
                    nc.scalar.activation(padded[:, :, g, :, g, :], heads[:, :, :, g, :], ACT.Copy).then_inc(s["v2_d"], 1)

            def head_exps(u):
                b, h = head_of(u)
                act.wait_ge(s["max2_d"], u + 1)
                if u >= P2_RING:
                    act.wait_ge(s["t2_p"], u - P2_RING + 1)
                for t in range(NT):
                    nc.scalar.activation(p2[u % P2_RING][:, t, :], tiles(bank[u % S2_BANKS])[:, t, :], ACT.Exp,
                                         bias=nmax2[b][:, h, t:t + 1], accum_out=sum2[b][:, t, h:h + 1]).then_inc(s["e2_d"], 1)

            def head_evac(u):
                act.wait_ge(s["t2_p"], u + 1)
                if u >= PT2_RING:
                    act.wait_ge(s["pv2_p"], (u - PT2_RING) // HG + 1)
                nc.scalar.activation(pT2[u % PT2_RING][:, :, :], tiles(bank[4 + u % T2_BANKS]), ACT.Copy).then_inc(s["pT2o_d"], 1)

            def rb2_evac(b):
                act.wait_ge(s["rb2_p"], b + 1)
                nc.scalar.activation(rb2[b][:, :], LA[b][:, 0:N], ACT.Copy).then_inc(s["rb2_d"], 1)

            def rs2_widen(b):
                act.wait_ge(s["rs2_d"], b + 1)
                nc.scalar.activation(rsx2[b][:, :, :, :], rsum2[b][:, :, :].unsqueeze(3).broadcast_to([128, NT, HEADS, D]),
                                     ACT.Copy).then_inc(s["rsx2_d"], 1)

            def shift_edges(b):
                act.wait_ge(s["f_d"], b + 1)
                act.wait_ge(s["zeroed"], 3 * NB)
                nc.scalar.activation(fsh[0][b][:, 1:H + 1, 1:W], fsh[1][b][:, 1:H + 1, 0:W - 1], ACT.Copy).then_inc(s["f0_d"], 1)
                nc.scalar.activation(fsh[2][b][:, 1:H + 1, 0:W - 1], fsh[1][b][:, 1:H + 1, 1:W], ACT.Copy).then_inc(s["f2_d"], 1)

            def v_products(first, last):
                def stage(b):
                    act.wait_ge(s["v1x1_p"], b + 1)
                    act.wait_ge(s["t2_p"], STEPS)
                    for n in range(first, last):
                        if b and n:
                            act.wait_ge(s["vsum_d"], n)
                        dst = vprod[n - 1] if n else vacc[b][:, :, :]
                        nc.scalar.activation(dst, LC[b][:, 0:N].rearrange("p (h w) -> p h w", h=H), ACT.Copy,
                                             scale=tap("vdw", *CENTRE_FIRST[n])).then_inc(s["vprod_d"], 1)
                return stage

            def q_exp(b):
                act.wait_ge(s["qs_d"], b + 1)
                nc.scalar.activation(eq[b][:, :, :, :], qs[b][:, :, :, :], ACT.Exp).then_inc(s["eq_d"], 1)

            def k_exp(b):
                act.wait_ge(s["k3m_d"], b + 1)
                nc.scalar.activation(ek[b][:, :], kc[b][:, :], ACT.Exp, bias=nmk[b][:, :],
                                     accum_out=sumk[b][:, :]).then_inc(s["ek_d"], 1)

            def ekT_evac(b):
                act.wait_ge(s["ekT_p"], b + 1)
                nc.scalar.activation(ekT[b][:, :, :], tiles(LB[b], 4)[:, 0:NT, :], ACT.Copy).then_inc(s["ekT_d"], 1)

            def v3_evac(b):
                act.wait_ge(s["v3_p"], b + 1)
                nc.scalar.activation(v3[b][:, :, :], tiles(LD[b], 4)[:, 0:NT, :], ACT.Copy).then_inc(s["v3_d"], 1)

            def qT_evac(b):
                act.wait_ge(s["qT_p"], b + 1)
                nc.scalar.activation(qT[b][:, :], LB[b][:, 0:N], ACT.Copy).then_inc(s["qT_d"], 1)

            def o3_tanh(b):
                act.wait_ge(s["o3_p"], b + 1)
                nc.scalar.activation(th[b][:, :], LA[b][:, 0:N], ACT.Tanh, scale=0.5).then_inc(s["th_d"], 1)

            def yc_evac(b):
                act.wait_ge(s["yc_p"], b + 1)
                nc.scalar.activation(ycg[b][:, :], LC[b][:, 0:N], ACT.Copy, scale=A("out_norm_g")).then_inc(s["ycg_d"], 1)

            def gelu_table(b):
                act.wait_ge(s["mhalf_set"], 1)
                nc.scalar.activation(gelu_first[:, :], mhalf[:, 0:1], ACT.Gelu).then_inc(s["table_set"], 1)

            def gelu(b):
                act.wait_ge(s["rs5_d"], b + 1)
                act.wait_ge(s["h_p"], b + 1)
                for t in range(NT):
                    nc.scalar.activation(h3[b][:, t, :], tiles(LD[b])[:, t, :], ACT.Gelu,
                                         scale=rs3[b][:, 2, t:t + 1]).then_inc(s["h_d"], 1)

            def hT_evac(b):
                act.wait_ge(s["hT_p"], b + 1)
                nc.scalar.activation(hT3[b][:, :, :], tiles(LC[b]), ACT.Copy).then_inc(s["hT_d"], 1)

            def rb6_evac(b):
                act.wait_ge(s["rb6_p"], b + 1)
                nc.scalar.activation(rb4[b][:, :], LB[b][:, 0:N], ACT.Copy).then_inc(s["rb6_d"], 1)

            def first_parts(b):
                act.wait_ge(s["q2_d"], NB)
                act.wait_ge(s["k2_d"], NB)
                for n, src in enumerate((q2[1], k2[1])):
                    nc.scalar.activation(parts2[n][:, 0, :], src[:, :], ACT.Copy).then_inc(s["part_d"], 1)

            def second_parts(b):
                for n in range(2):
                    act.wait_ge(s["rest_d"], n + 1)
                    nc.scalar.activation(parts2[n][:, 1, :], rest2[n][:, :], ACT.Copy).then_inc(s["part_d"], 1)

            between = {11: rb2_evac, 17: shift_edges}
            v2_evac(0)
            first_parts(1)
            second_parts(1)
            for u in range(STEPS + LAG):
                if u >= LAG and (u - LAG) % 2:
                    head_evac(u - LAG)
                if u < STEPS:
                    head_exps(u)
                if u == 0:
                    v2_evac(1)
                if u in between:
                    between[u](0)
            for stage, b in ((rs2_widen, 1), (v_products(0, 4), 0), (rb2_evac, 1), (v_products(4, TAPS), 0), (k_exp, 0),
                             (shift_edges, 1), (v_products(0, 2), 1), (q_exp, 0), (v_products(2, TAPS), 1), (ekT_evac, 0),
                             (qT_evac, 0), (v3_evac, 0),
                             (k_exp, 1), (q_exp, 1), (ekT_evac, 1), (v3_evac, 1), (qT_evac, 1), (o3_tanh, 0),
                             (o3_tanh, 1), (gelu_table, 1), (yc_evac, 0), (yc_evac, 1), (gelu, 0), (gelu, 1), (hT_evac, 0),
                             (hT_evac, 1), (rb6_evac, 0), (rb6_evac, 1)):
                stage(b)

        @block.vector
        def _(dve):
            counts = {}

            def vec_done(name):
                counts.setdefault(name, []).append(sum(len(c) for c in counts.values()) + 1)

            def vec_at(name, nth):
                return counts[name][nth - 1]

            def vec_last(name):
                return counts[name][-1]

            def norm_stats(b, n, src, ready, ve_d, count):
                for t in range(NT):
                    dve.wait_ge(ready, count(t))
                    nc.vector.bn_stats(st3[b][:, n, t, :], src(t)).then_inc(s["vec"], 1)
                    vec_done("st")
                dve.wait_ge(s["vec"], vec_last("st"))
                for t in range(NT):
                    nc.vector.bn_aggr(mv3[b][:, n, t, :], st3[b][:, n, t, :]).then_inc(s["vec"], 1)
                    vec_done("mv")
                dve.wait_ge(s["vec"], vec_last("mv"))
                nc.vector.tensor_scalar_add(ve3[b][:, n, :], mv3[b][:, n, :, 1], EPS_LN).then_inc(ve_d, 1)

            def row_max(b, scores, ready, nm, max_d):
                dve.wait_ge(ready, b + 1)
                nc.vector.tensor_reduce(nm, tiles(scores), AX.X, ALU.max, negate=True).then_inc(max_d, 1)

            nc.vector.memset(warm[:, :], 0.0).then_inc(s["warm_set"], 1)
            for b in range(NB):
                dve.wait_ge(s["x_in"], 32)
                nc.vector.bn_stats(st0[b][:, :], x0[b][:, :]).then_inc(s["vec"], 1)
                vec_done("st0")
            for b in range(NB):
                dve.wait_ge(s["vec"], vec_at("st0", b + 1))
                nc.vector.bn_aggr(mv0[:, b, :], st0[b][:, :]).then_inc(s["vec"], 1)
                vec_done("mv0")
            for b in range(NB):
                dve.wait_ge(s["vec"], vec_at("mv0", b + 1))
                nc.vector.scalar_tensor_tensor(mv0[:, b, 1:2], mv0[:, b, 0:1], mv0[:, b, 0:1], mv0[:, b, 1:2],
                                               ALU.mult, ALU.add).then_inc(s["gin0_d"], 1)
            dve.wait_ge(s["g0_p"], 1)
            nc.vector.tensor_copy(gs0[:, :, :].rearrange("p b m -> p (b m)"), bank[0][:, 0:2 * NB]).then_inc(s["vec"], 1)
            vec_done("g0")
            dve.wait_ge(s["vec"], vec_at("g0", 1))
            nc.vector.scalar_tensor_tensor(nm0[:, :], gs0[:, :, 0], -1.0, gs0[:, :, 0], ALU.mult, ALU.mult).then_inc(s["vec"], 1)
            vec_done("nm0")
            dve.wait_ge(s["vec"], vec_at("nm0", 1))
            nc.vector.scalar_tensor_tensor(ve0[:, :], gs0[:, :, 1], EPS_GN, nm0[:, :], ALU.add, ALU.add).then_inc(s["ve0_d"], 1)
            dve.wait_ge(s["rstd0_d"], 1)
            nc.vector.tensor_scalar_mul(a0[:, :], rstd0[:, :], A("gamma")).then_inc(s["vec"], 1)
            vec_done("a0")
            dve.wait_ge(s["vec"], vec_at("a0", 1))
            nc.vector.tensor_mul(ma0[:, :], a0[:, :], gs0[:, :, 0]).then_inc(s["vec"], 1)
            vec_done("ma0")
            dve.wait_ge(s["vec"], vec_at("ma0", 1))
            nc.vector.tensor_scalar(nb0[:, :], ma0[:, :], A("beta"), None, ALU.subtract).then_inc(s["vec"], 1)
            vec_done("b0")
            dve.wait_ge(s["vec"], vec_at("b0", 1))
            for b in range(NB):
                nc.vector.tensor_scalar(hn0[b][:, :], x0[b][:, :], a0[:, b:b + 1], nb0[:, b:b + 1],
                                        ALU.mult, ALU.subtract).then_inc(s["hn0_d"], 1)
            dve.wait_ge(s["wpv_p"], 1)
            nc.vector.tensor_copy(wpvT[:, :], bank[3][:, 0:C]).then_inc(s["wpv_w"], 1)
            nc.vector.tensor_add(bias0[:, :], bank[3][:, C:C + 1], A("bp0")).then_inc(s["bias0_w"], 1)
            def q0_evac(b):
                dve.wait_ge(s["q0_p"], b + 1)
                nc.vector.tensor_scalar(q0[b][:, :], bank[4 * b][:, 0:N], A("bq0"), float(C) ** -0.5,
                                        ALU.add, ALU.mult).then_inc(s["q0_d"], 1)

            def xb0_sum(b):
                dve.wait_ge(s["bias0_w"], 1)
                nc.vector.tensor_scalar_add(xb0[b][:, :], x0[b][:, :], bias0[:, :]).then_inc(s["vec"], 1)
                vec_done("xb0")

            def max0(b):
                row_max(b, bank[4 * b + 3], s["s0_p"], nmax[b][:, 0:NT], s["max0_d"])

            def sums0(b):
                dve.wait_ge(s["e0_d"], NT * (b + 1))
                nc.vector.reciprocal(rsum0[b][:, :], psums[b][:, 0:NT]).then_inc(s["rs0_d"], 1)

            def p0T_evac(b):
                dve.wait_ge(s["t0_p"], b + 1)
                nc.vector.tensor_copy(pT0[b][:, :, :], tiles(bank[4 * b])).then_inc(s["pT0_d"], 1)

            def centre_ff_1(b):
                dve.wait_ge(s["w1m_p"], 1)
                nc.vector.tensor_sub(w1c[:, :], w1g[:, :], bank[6][:, 0:HID]).then_inc(s["w1c_w"], 1)

            def centre_ff_2(b):
                dve.wait_ge(s["w2m_p"], 1)
                for j in range(2):
                    nc.vector.scalar_tensor_tensor(w2c[:, j, :], bank[6][:, HID:HID + C], -0.5, w2g[:, j, :],
                                                   ALU.mult, ALU.add).then_inc(s["w2c_w"], 1)

            def x1_sum(b):
                dve.wait_ge(s["pv0_p"], b + 1)
                dve.wait_ge(s["rb0_d"], b + 1)
                nc.vector.tensor_mul(t0[b][:, :], bank[4 * b + 2][:, 0:N], rb0[b][:, :]).then_inc(s["vec"], 1)
                vec_done("n0")
                dve.wait_ge(s["vec"], vec_at("n0", b + 1))
                dve.wait_ge(s["vec"], vec_at("xb0", b + 1))
                nc.vector.tensor_add(x1[b][:, :], t0[b][:, :], xb0[b][:, :]).then_inc(s["x1_d"], 1)

            def q1_evac(b):
                dve.wait_ge(s["qk1_p"], b + 1)
                nc.vector.tensor_scalar_add(q1[b][:, :], bank[4 * b][0:QUAD, 0:N], A("bq1")[0:QUAD, :]).then_inc(s["q1_d"], 1)

            def xb1_sum(b):
                if b == 0:
                    nc.vector.tensor_mul(gbv[:, :], A("gpam"), A("bv1")).then_inc(s["gbv_w"], 1)
                    dve.wait_ge(s["gbv_w"], 1)
                dve.wait_ge(s["x1_d"], b + 1)
                nc.vector.tensor_scalar_add(xb1[b][:, :], x1[b][:, :], gbv[:, :]).then_inc(s["vec"], 1)
                vec_done("xb1")

            def max1(b):
                row_max(b, bank[4 * b + 2], s["s1_p"], nmax[b][:, NT:2 * NT], s["max1_d"])

            def sums1(b):
                dve.wait_ge(s["e1_d"], NT * (b + 1))
                nc.vector.reciprocal(rsum1[b][:, :], psums[b][:, NT:2 * NT]).then_inc(s["rs1_d"], 1)

            def p1T_evac(b):
                dve.wait_ge(s["t1_p"], b + 1)
                nc.vector.tensor_copy(pT1[b][:, :, :], tiles(bank[4 * b])).then_inc(s["pT1_d"], 1)

            def embedding_evac(b):
                dve.wait_ge(s["emb_p"], 1)
                nc.vector.tensor_scalar(qe2[:, :], bank[5][:, 0:N], D ** -0.5, None, ALU.mult).then_inc(s["vec"], 1)
                vec_done("qe2")
                nc.vector.tensor_copy(ke2[:, :], bank[5][:, N:2 * N]).then_inc(s["emb_d"], 1)

            def pam_sum(b):
                dve.wait_ge(s["pv1_p"], b + 1)
                dve.wait_ge(s["rb1_d"], b + 1)
                nc.vector.tensor_mul(t1[b][:, :], bank[4 * b + 3][:, 0:N], rb1[b][:, :]).then_inc(s["vec"], 1)
                vec_done("n1")
                dve.wait_ge(s["vec"], vec_at("n1", b + 1))
                dve.wait_ge(s["vec"], vec_at("xb1", b + 1))
                nc.vector.tensor_add(pam[b][:, :], t1[b][:, :], xb1[b][:, :]).then_inc(s["pam_d"], 1)

            def centre_outw(b):
                dve.wait_ge(s["c_in"], 16)
                nc.vector.tensor_scalar(outwc[:, :], K("outwT"), 0.5, None, ALU.mult).then_inc(s["vec"], 1)
                vec_done("outw_half")
                dve.wait_ge(s["vec"], vec_at("outw_half", 1))
                nc.vector.reduce_sum(outws[:, 0:1], outwc[:, :], AX.X).then_inc(s["vec"], 1)
                vec_done("outw_sum")
                dve.wait_ge(s["vec"], vec_at("outw_sum", 1))
                nc.vector.tensor_scalar(outws[:, 1:2], outws[:, 0:1], -1.0 / C, None, ALU.mult).then_inc(s["vec"], 1)
                vec_done("outw_neg")
                dve.wait_ge(s["vec"], vec_at("outw_neg", 1))
                nc.vector.tensor_scalar_add(outwc[:, :], outwc[:, :], outws[:, 1:2]).then_inc(s["outw_c"], 1)

            def energy_min(b):
                dve.wait_ge(s["cen_p"], b + 1)
                nc.vector.tensor_reduce(cmin[b][:, :], bank[4 * b + 1][:, 0:C], AX.X, ALU.min).then_inc(s["min_d"], 1)

            def ce_scale(b):
                dve.wait_ge(s["ce_d"], b + 1)
                nc.vector.reciprocal(cscale[b][:, 0:1], csum[b][:, :]).then_inc(s["vec"], 1)
                vec_done("cr")
                dve.wait_ge(s["vec"], vec_at("cr", b + 1))
                nc.vector.tensor_mul(cscale[b][:, 1:2], cscale[b][:, 0:1], A("gcam")).then_inc(s["vec"], 1)
                vec_done("cs")

            def ceT_evac(b):
                dve.wait_ge(s["ceT_p"], b + 1)
                nc.vector.tensor_copy(ceT[b][:, :], bank[4 * b + 2][:, 0:C]).then_inc(s["ceT_d"], 1)

            def x2_sum(b):
                dve.wait_ge(s["co_p"], b + 1)
                dve.wait_ge(s["vec"], vec_at("cs", b + 1))
                nc.vector.scalar_tensor_tensor(x2[b][:, :], bank[4 * b + 3][:, 0:N], cscale[b][:, 1:2], pam[b][:, :],
                                               ALU.mult, ALU.add).then_inc(s["x2_d"], 1)

            for stage, b in ((q0_evac, 0), (q0_evac, 1), (xb0_sum, 0), (xb0_sum, 1), (max0, 0), (max0, 1), (sums0, 0), (p0T_evac, 0),
                             (sums0, 1), (centre_outw, 0), (x1_sum, 0), (x1_sum, 1), (q1_evac, 0), (q1_evac, 1), (max1, 0), (max1, 1),
                             (xb1_sum, 0), (xb1_sum, 1), (sums1, 0), (p1T_evac, 0), (embedding_evac, 0), (sums1, 1),
                             (pam_sum, 0), (pam_sum, 1),
                             (centre_ff_1, 0), (energy_min, 0), (ce_scale, 0), (energy_min, 1), (ceT_evac, 0), (centre_ff_2, 0),
                             (ce_scale, 1), (ceT_evac, 1), (x2_sum, 0), (x2_sum, 1)):
                stage(b)

            for b in range(NB):
                dve.wait_ge(s["q2_p"], b + 1)
                nc.vector.scalar_tensor_tensor(q2[b][:, :], bank[4 * b][:, 0:N], D ** -0.5, qe2[:, :], ALU.mult, ALU.add).then_inc(s["q2_d"], 1)
                dve.wait_ge(s["k2_p"], b + 1)
                dve.wait_ge(s["emb_d"], 1)
                nc.vector.tensor_add(k2[b][:, :], bank[4 * b + 1][:, 0:N], ke2[:, :]).then_inc(s["k2_d"], 1)

            def xb2_sums():
                for b in range(NB):
                    dve.wait_ge(s["x2_d"], b + 1)
                    nc.vector.tensor_scalar_add(xb2[b][:, :], x2[b][:, :], A("bout")).then_inc(s["vec"], 1)
                    vec_done("xb2")
            def head_max(u):
                b, h = head_of(u)
                dve.wait_ge(s["s2_p"], u + 1)
                nc.vector.tensor_reduce(nmax2[b][:, h, :], tiles(bank[u % S2_BANKS]), AX.X, ALU.max, negate=True).then_inc(s["max2_d"], 1)

            def head_evac(u):
                dve.wait_ge(s["t2_p"], u + 1)
                if u >= PT2_RING:
                    dve.wait_ge(s["pv2_p"], (u - PT2_RING) // HG + 1)
                nc.vector.tensor_copy(pT2[u % PT2_RING][:, :, :], tiles(bank[4 + u % T2_BANKS])).then_inc(s["pT2e_d"], 1)

            def head_sums(b):
                dve.wait_ge(s["e2_d"], NT * HEADS * (b + 1))
                nc.vector.reciprocal(rsum2[b][:, :, :], sum2[b][:, :, :]).then_inc(s["rs2_d"], 1)

            def o2_norm(b):
                dve.wait_ge(s["rb2_d"], b + 1)
                dve.wait_ge(s["pv2_p"], NG * (b + 1))
                nc.vector.tensor_mul(o2[b][:, :], bank[4 * b + 3][:, 0:N], rb2[b][:, :]).then_inc(s["o2_d"], 1)

            def x3_sum(b):
                dve.wait_ge(s["w2_p"], b + 1)
                dve.wait_ge(s["vec"], vec_at("xb2", b + 1))
                nc.vector.tensor_add(x3[b][:, :], LA[b][:, 0:N], xb2[b][:, :]).then_inc(s["x3_d"], 1)

            def x3_stats(b):
                norm_stats(b, 0, lambda t: tiles(LA[b], 4)[:, t, :], s["x3T_p"], s["ve3_d"], lambda t: b + 1)
                dve.wait_ge(s["mean3_p"], b + 1)
                nc.vector.tensor_sub(xc3[b][:, :], x3[b][:, :], LB[b][:, 0:N]).then_inc(s["xc3_d"], 1)

            def f_norm(b):
                dve.wait_ge(s["rb3_p"], b + 1)
                dve.wait_ge(s["xc3_d"], b + 1)
                dve.wait_ge(s["zeroed"], 3 * (b + 1))
                nc.vector.tensor_mul(fsh[1][b][:, 1:H + 1, :], xc3[b][:, :].rearrange("p (h w) -> p h w", h=H),
                                     LA[b][:, 0:N].rearrange("p (h w) -> p h w", h=H)).then_inc(s["f_d"], 1)

            def k_taps(b, first=0, last=TAPS):
                dve.wait_ge(s["k1x1_p"], b + 1)
                k1x1 = LB[b][:, 0:N].rearrange("p (h w) -> p h w", h=H)
                for n in range(first, last):
                    dy, dx = CENTRE_FIRST[n]
                    (oy, ox), (iy, ix) = shifted(dy, dx)
                    if n == 1:
                        dve.wait_ge(s["zeroed"], 3 * NB + b + 1)
                    if n >= 2:
                        dve.wait_ge(s["vec"], vec_at("ktap", TAPS * b + n - 1))
                    if n == 0:
                        nc.vector.tensor_scalar_mul(kacc[b][:, 0, :, :], k1x1, tap("kdw", dy, dx)).then_inc(s["vec"], 1)
                    else:
                        acc = kacc[b][:, n % 2, oy, ox]
                        nc.vector.scalar_tensor_tensor(acc, k1x1[:, iy, ix], tap("kdw", dy, dx), acc, ALU.mult, ALU.add).then_inc(s["vec"], 1)
                    vec_done("ktap")
                if last < TAPS:
                    return
                dve.wait_ge(s["vec"], vec_at("ktap", TAPS * (b + 1)))
                nc.vector.tensor_add(kc[b][:, :], kacc[b][:, 0, :, :].rearrange("p h w -> p (h w)"),
                                     kacc[b][:, 1, :, :].rearrange("p h w -> p (h w)")).then_inc(s["vec"], 1)
                vec_done("kc")
                dve.wait_ge(s["vec"], vec_at("kc", b + 1))
                nc.vector.tensor_reduce(nmk[b][:, :], kc[b][:, :], AX.X, ALU.max, negate=True).then_inc(s["k3m_d"], 1)

            def k_taps_0(b):
                k_taps(b, 0, 3)

            def k_taps_3(b):
                k_taps(b, 3, 6)

            def k_taps_6(b):
                k_taps(b, 6, 8)

            def k_taps_8(b):
                k_taps(b, 8, TAPS)

            def heads(t, b):
                return t[b][:, :, :].unsqueeze(3).broadcast_to([128, NT, HEADS, D])

            def q_max(b):
                dve.wait_ge(s["q3_p"], b + 1)
                q = tiles(LA[b], 4)[:, 0:NT, :].rearrange("p t (h d) -> p t h d", h=HEADS)
                nc.vector.tensor_reduce(mq[b][:, :, :], q, AX.X, ALU.max).then_inc(s["vec"], 1)
                vec_done("mq")
                dve.wait_ge(s["vec"], vec_at("mq", b + 1))
                nc.vector.tensor_tensor(qs[b][:, :, :, :], q, heads(mq, b), ALU.subtract).then_inc(s["qs_d"], 1)

            def q_norm(b):
                dve.wait_ge(s["eq_d"], b + 1)
                nc.vector.reduce_sum(sq[b][:, :, :], eq[b][:, :, :, :], AX.X).then_inc(s["vec"], 1)
                vec_done("sq")
                dve.wait_ge(s["vec"], vec_at("sq", b + 1))
                nc.vector.reciprocal(rq[b][:, :, :], sq[b][:, :, :]).then_inc(s["vec"], 1)
                vec_done("rq")
                dve.wait_ge(s["vec"], vec_at("rq", b + 1))
                nc.vector.tensor_tensor(qn[b][:, :, :, :], eq[b][:, :, :, :], heads(rq, b), ALU.mult).then_inc(s["qn_d"], 1)

            def k_sums(b):
                dve.wait_ge(s["ek_d"], b + 1)
                nc.vector.reciprocal(rsk[b][:, 0:1], sumk[b][:, :]).then_inc(s["vec"], 1)
                vec_done("rkr")
                dve.wait_ge(s["vec"], vec_at("rkr", b + 1))
                nc.vector.tensor_scalar(rsk[b][:, 1:2], rsk[b][:, 0:1], D ** -0.5, None, ALU.mult).then_inc(s["vec"], 1)
                vec_done("rk")

            def context(b):
                dve.wait_ge(s["ctx_p"], b + 1)
                dve.wait_ge(s["vec"], vec_at("rk", b + 1))
                nc.vector.scalar_tensor_tensor(cm[b][:, :], LC[b][:, 0:C], rsk[b][:, 1:2], K("headmask"),
                                               ALU.mult, ALU.mult).then_inc(s["cm_d"], 1)

            def silu(b):
                dve.wait_ge(s["th_d"], b + 1)
                nc.vector.scalar_tensor_tensor(s3[b][:, :], th[b][:, :], 1.0, LA[b][:, 0:N],
                                               ALU.add, ALU.mult).then_inc(s["s3_d"], 1)

            def y_stats(b):
                norm_stats(b, 1, lambda t: tiles(LD[b], 4)[:, t, :], s["yT_p"], s["ve4_d"], lambda t: b + 1)

            def x4_sum(b):
                dve.wait_ge(s["rb4_p"], b + 1)
                dve.wait_ge(s["ycg_d"], b + 1)
                nc.vector.tensor_mul(x4a[b][:, :], LB[b][:, 0:N], ycg[b][:, :]).then_inc(s["vec"], 1)
                vec_done("x4a")
                dve.wait_ge(s["vec"], vec_at("x4a", b + 1))
                nc.vector.tensor_add(x4[b][:, :], x4a[b][:, :], x3[b][:, :]).then_inc(s["x4_d"], 1)

            def x4_stats(b):
                norm_stats(b, 2, lambda t: tiles(LA[b], 4)[:, t, :], s["x4T_p"], s["ve5_d"], lambda t: b + 1)

            def h_stats(b):
                norm_stats(b, 3, lambda t: h3[b][:, t, :], s["h_d"], s["ve6_d"], lambda t: NT * b + t + 1)

            def y_sum(b):
                dve.wait_ge(s["ff_p"], b + 1)
                dve.wait_ge(s["rb6_d"], b + 1)
                nc.vector.tensor_mul(fo[b][:, :], LA[b][:, 0:N], rb4[b][:, :]).then_inc(s["vec"], 1)
                vec_done("fo")
                dve.wait_ge(s["vec"], vec_at("fo", b + 1))
                nc.vector.tensor_add(y[b][:, :], fo[b][:, :], x4[b][:, :]).then_inc(s["y_d"], 1)

            def rests(b):
                for n, src in enumerate((q2[1], k2[1])):
                    dve.wait_ge(s["part_d"], n + 1)
                    nc.vector.tensor_sub(rest2[n][:, :], src[:, :], parts2[n][:, 0, :]).then_inc(s["rest_d"], 1)

            def third_parts(b):
                for n in range(2):
                    dve.wait_ge(s["part_d"], n + 3)
                    nc.vector.tensor_sub(parts2[n][:, 2, :], rest2[n][:, :], parts2[n][:, 1, :]).then_inc(s["parts_d"], 1)

            between = {8: head_sums, 12: o2_norm, 13: x3_sum, 14: x3_stats, 16: f_norm}
            for u in range(STEPS + LAG):
                if u == 0:
                    rests(1)
                if u < STEPS:
                    head_max(u)
                if u == 0:
                    third_parts(1)
                if u == 1:
                    xb2_sums()
                if u >= LAG and (u - LAG) % 2 == 0:
                    head_evac(u - LAG)
                if u in between:
                    between[u](0)
            for stage, b in ((head_sums, 1), (k_taps_0, 0), (k_taps_3, 0), (o2_norm, 1), (k_taps_6, 0), (x3_sum, 1), (x3_stats, 1),
                             (k_taps_8, 0), (f_norm, 1), (q_max, 0), (k_sums, 0), (k_taps_0, 1), (q_norm, 0), (k_taps_3, 1),
                             (k_taps_6, 1), (k_taps_8, 1),
                             (q_max, 1), (context, 0), (k_sums, 1), (q_norm, 1), (context, 1), (silu, 0), (silu, 1),
                             (y_stats, 0), (y_stats, 1),
                             (x4_sum, 0), (x4_sum, 1), (x4_stats, 0), (x4_stats, 1), (h_stats, 0), (h_stats, 1), (y_sum, 0), (y_sum, 1)):
                stage(b)

        @block.tensor
        def _(pe):
            def spread(dst, rows, width=128):
                return nc.tensor.transpose(dst, rows, ident)

            def transposes(dst, src, done, ready=None, count=0):
                for t in range(NT):
                    if ready is not None:
                        pe.wait_ge(ready, count + t + 1)
                    for i in range(NT):
                        last = nc.tensor.transpose(tiles(dst)[:, i, t * 128:(t + 1) * 128],
                                                   src[:, t, i * 128:(i + 1) * 128], ident)
                last.then_inc(done, 1)

            def keep_clock(n, dst):
                for _ in range(n):
                    nc.tensor.matmul(dst[:, :], warm[:, 0:128], warm[:, :], start=True, stop=True)

            pe.wait_ge(s["warm_set"], 1)
            keep_clock(9, bank[7])
            pe.wait_ge(s["a_in"], 16)
            pe.wait_ge(s["gin0_d"], NB)
            nc.tensor.matmul(bank[0][:, 0:2 * NB], A("gmean"), mv0[:, :, :].rearrange("p b m -> p (b m)"),
                             start=True, stop=True).then_inc(s["g0_p"], 1)
            keep_clock(4, bank[7])
            pe.wait_ge(s["a2_in"], 16)
            nc.tensor.matmul(bank[3][:, 0:C], A("wv0"), A("wpT0"), start=True, stop=True)
            nc.tensor.matmul(bank[3][:, C:C + 1], A("wpT0"), A("bv0"), start=True, stop=True).then_inc(s["wpv_p"], 1)

            def q0_product(b):
                pe.wait_ge(s["hn0_d"], b + 1)
                nc.tensor.matmul(bank[4 * b][:, 0:N], A("wqT0"), hn0[b][:, :], start=True, stop=True).then_inc(s["q0_p"], 1)

            def k0_product(b):
                nc.tensor.matmul(bank[4 * b + 1][:, 0:N], A("wkT0"), hn0[b][:, :], start=True, stop=True).then_inc(s["k0_p"], 1)

            def v0_product(b):
                pe.wait_ge(s["wpv_w"], 1)
                for t in range(NT):
                    last = nc.tensor.matmul(bank[4 * b + 2][:, t * C:(t + 1) * C], hn0[b][:, t * 128:(t + 1) * 128], wpvT[:, :],
                                            start=True, stop=True)
                last.then_inc(s["v0_p"], 1)

            def scores0(b):
                pe.wait_ge(s["q0_d"], b + 1)
                pe.wait_ge(s["k0_d"], b + 1)
                pe.wait_ge(s["bias0_w"], 1)
                for t in range(NT):
                    last = nc.tensor.matmul(tiles(bank[4 * b + 3])[:, t, :], q0[b][:, t * 128:(t + 1) * 128], k0[b][:, :],
                                            start=True, stop=True)
                last.then_inc(s["s0_p"], 1)

            def ff_mean_1(b):
                pe.wait_ge(s["c_in"], 16)
                pe.wait_ge(s["w1g_w"], 1)
                pe.wait_ge(s["e1_d"], NT * NB)
                nc.tensor.matmul(bank[6][:, 0:HID], K("cmean"), w1g[:, :], start=True, stop=True).then_inc(s["w1m_p"], 1)

            def ff_mean_2(b):
                pe.wait_ge(s["w2g_w"], 2)
                pe.wait_ge(s["w1c_w"], 1)
                for j in range(2):
                    last = nc.tensor.matmul(bank[6][:, HID:HID + C], K("cmean"), w2g[:, j, :], start=(j == 0), stop=(j == 1))
                last.then_inc(s["w2m_p"], 1)

            def p0_transposes(b):
                transposes(bank[4 * b], p0[b], s["t0_p"], s["e0_d"], NT * b)

            def row_scale(b, rs, rb_p):
                for t in range(NT):
                    last = spread(bank[4 * b + 1][:, t * 128:(t + 1) * 128], rs[b][:, t:t + 1].broadcast_to([128, 128]))
                last.then_inc(rb_p, 1)

            def scale0(b):
                pe.wait_ge(s["rs0_d"], b + 1)
                row_scale(b, rsum0, s["rb0_p"])

            def mix0(b):
                pe.wait_ge(s["v0_d"], b + 1)
                pe.wait_ge(s["pT0b_d"] if b else s["pT0_d"], 1)
                for i in range(NT):
                    last = nc.tensor.matmul(bank[4 * b + 2][:, 0:N], v0[b][:, i, :], pT0[b][:, i, :], start=(i == 0), stop=(i == NT - 1))
                last.then_inc(s["pv0_p"], 1)

            def qk1_product(b):
                pe.wait_ge(s["b_in"], 16)
                pe.wait_ge(s["x1_d"], b + 1)
                nc.tensor.matmul(bank[4 * b][0:2 * QUAD, 0:N], B("wqkT1"), x1[b][:, :], start=True, stop=True).then_inc(s["qk1_p"], 1)

            def v1_product(b):
                for t in range(NT):
                    last = nc.tensor.matmul(bank[4 * b + 3][:, t * C:(t + 1) * C], x1[b][:, t * 128:(t + 1) * 128], B("wvT1"),
                                            start=True, stop=True)
                last.then_inc(s["v1_p"], 1)

            def scores1(b):
                pe.wait_ge(s["q1_d"], b + 1)
                pe.wait_ge(s["k1_d"], b + 1)
                for t in range(NT):
                    last = nc.tensor.matmul(tiles(bank[4 * b + 2])[:, t, :], q1[b][:, t * 128:(t + 1) * 128], k1[b][:, :],
                                            start=True, stop=True)
                last.then_inc(s["s1_p"], 1)

            def embedding(b):
                for n, we in enumerate(("wqe", "wke")):
                    last = nc.tensor.matmul(bank[5][:, n * N:(n + 1) * N], B(we)[0:EMB, :], B("emb")[0:EMB, :], start=True, stop=True)
                last.then_inc(s["emb_p"], 1)

            def p1_transposes(b):
                transposes(bank[4 * b], p1[b], s["t1_p"], s["e1_d"], NT * b)

            def scale1(b):
                pe.wait_ge(s["rs1_d"], b + 1)
                if b == 1:
                    pe.wait_ge(s["emb_d"], 1)
                row_scale(b, rsum1, s["rb1_p"])

            def mix1(b):
                pe.wait_ge(s["v1_d"], b + 1)
                pe.wait_ge(s["pT1b_d"] if b else s["pT1_d"], 1)
                for i in range(NT):
                    last = nc.tensor.matmul(bank[4 * b + 3][:, 0:N], v1[b][:, i, :], pT1[b][:, i, :], start=(i == 0), stop=(i == NT - 1))
                last.then_inc(s["pv1_p"], 1)

            def pam_transposes(b):
                pe.wait_ge(s["pam_d"], b + 1)
                for t in range(NT):
                    last = nc.tensor.transpose(bank[4 * b][:, t * C:(t + 1) * C], pam[b][:, t * 128:(t + 1) * 128], ident)
                last.then_inc(s["pamT_p"], 1)

            def energy(b):
                pe.wait_ge(s["pamT_d"], b + 1)
                for t in range(NT):
                    last = nc.tensor.matmul(bank[4 * b + 1][:, 0:C], pamT[b][:, t, :], pamT[b][:, t, :],
                                            start=(t == 0), stop=(t == NT - 1))
                last.then_inc(s["cen_p"], 1)

            def ce_transpose(b):
                pe.wait_ge(s["ce_d"], b + 1)
                if b == 1:
                    pe.wait_ge(s["w2c_w"], 2)
                nc.tensor.transpose(bank[4 * b + 2][:, 0:C], ce[b][:, :], ident).then_inc(s["ceT_p"], 1)

            def co_product(b):
                pe.wait_ge(s["ceT_d"], b + 1)
                nc.tensor.matmul(bank[4 * b + 3][:, 0:N], ceT[b][:, :], pam[b][:, :], start=True, stop=True).then_inc(s["co_p"], 1)

            def qk2(b):
                pe.wait_ge(s["x2_d"], b + 1)
                for n, (wx, done) in enumerate((("wqx", s["q2_p"]), ("wkx", s["k2_p"]))):
                    nc.tensor.matmul(bank[4 * b + n][:, 0:N], B(wx), x2[b][:, :], start=True, stop=True).then_inc(done, 1)

            def v2_product(b):
                for t in range(NT):
                    last = nc.tensor.matmul(bank[4 * b + 2][:, t * C:(t + 1) * C], x2[b][:, t * 128:(t + 1) * 128], B("wv2"),
                                            start=True, stop=True)
                last.then_inc(s["v2_p"], 1)

            for stage, b in ((q0_product, 0), (k0_product, 0), (q0_product, 1), (k0_product, 1), (scores0, 0), (scores0, 1),
                             (v0_product, 0), (v0_product, 1), (p0_transposes, 0), (scale0, 0), (p0_transposes, 1), (scale0, 1), (mix0, 0),
                             (mix0, 1),
                             (qk1_product, 0), (v1_product, 0), (qk1_product, 1), (scores1, 0), (scores1, 1), (v1_product, 1),
                             (embedding, 0),
                             (p1_transposes, 0), (scale1, 0), (p1_transposes, 1), (mix1, 0), (scale1, 1), (mix1, 1),
                             (pam_transposes, 0), (ff_mean_1, 0), (energy, 0), (pam_transposes, 1), (ff_mean_2, 0), (energy, 1),
                             (ce_transpose, 0), (co_product, 0),
                             (ce_transpose, 1), (co_product, 1), (qk2, 0), (v2_product, 0), (qk2, 1)):
                stage(b)

            def head_scores(u):
                b, h = head_of(u)
                if u < S2_BANKS:
                    pe.wait_ge((s["q2_d"], s["k2_d"], s["v2_d"])[u], (1, 1, NG)[u])
                else:
                    pe.wait_ge(s["e2_d"], NT * (u - S2_BANKS + 1))
                if b == 0:
                    pe.wait_ge(s["k2_d"], 1)
                    pe.wait_ge(s["qh2_d"], u + 1)
                    queries, keys = qh2, k2[b][:, :]
                else:
                    pe.wait_ge(s[f"stacks{h % NG}_in"], 16 * 2)
                    queries, keys = stack2[0], stack2[1][:, h, :]
                for t in range(NT):
                    last = nc.tensor.matmul(tiles(bank[u % S2_BANKS])[:, t, :], queries[:, h, t * 128:(t + 1) * 128], keys,
                                            start=True, stop=True)
                last.then_inc(s["s2_p"], 1)

            def head_transposes(u):
                pe.wait_ge(s["e2_d"], NT * (u + 1))
                if u < T2_BANKS:
                    pe.wait_ge((s["q2_d"], s["k2_d"])[u], NB)
                else:
                    pe.wait_ge(s["pT2e_d"] if u % 2 == 0 else s["pT2o_d"], (u - T2_BANKS) // 2 + 1)
                transposes(bank[4 + u % T2_BANKS], p2[u % P2_RING], s["t2_p"])

            def group_mix(grp):
                b, g = divmod(grp, NG)
                pe.wait_ge(s["pT2e_d"], 2 * (grp + 1))
                pe.wait_ge(s["pT2o_d"], 2 * (grp + 1))
                pe.wait_ge(s["v2_d"], NG * (b + 1))
                for kt in range(NT):
                    for i in range(HG):
                        last = nc.tensor.matmul(bank[4 * b + 3][QUAD * i:QUAD * (i + 1), 0:N],
                                                v2[b][:, kt, g * C + QUAD * i:g * C + QUAD * (i + 1)],
                                                pT2[(grp * HG + i) % PT2_RING][:, kt, :], start=(g == 0 and kt == 0),
                                                stop=(g == NG - 1 and kt == NT - 1), tile_position=(0, QUAD * i), skip_group_check=True)
                last.then_inc(s["pv2_p"], 1)

            def keep_before_v(b):
                keep_clock(2, LD[b][:, :])

            def keep_before_rb4(b):
                keep_clock(3, LB[b][:, :])

            def keep_before_rb6(b):
                keep_clock(3, LB[b][:, :])

            def last_mix(b):
                group_mix(NG * (b + 1) - 1)

            def column_spread(dst, rows, done):
                for t in range(NT):
                    last = spread(dst[:, t * 128:(t + 1) * 128], rows(t))
                last.then_inc(done, 1)

            def rb2_spread(b):
                pe.wait_ge(s["rsx2_d"], b + 1)
                pe.wait_ge(s["v2_d"], NG * NB)
                column_spread(LA[b], lambda t: rsx2[b][:, t, :, :].rearrange("p h d -> p (h d)"), s["rb2_p"])

            def w2_out(b):
                pe.wait_ge(s["o2_d"], b + 1)
                nc.tensor.matmul(LA[b][:, 0:N], B("wout"), o2[b][:, :], start=True, stop=True).then_inc(s["w2_p"], 1)

            def x3_transposes(b):
                pe.wait_ge(s["x3_d"], b + 1)
                for t in range(NT):
                    last = nc.tensor.transpose(LA[b][:, t * C:(t + 1) * C], x3[b][:, t * 128:(t + 1) * 128], ident)
                last.then_inc(s["x3T_p"], 1)
                nc.tensor.matmul(LB[b][:, 0:N], K("cmean"), x3[b][:, :], start=True, stop=True).then_inc(s["mean3_p"], 1)

            def rb3_spread(b):
                pe.wait_ge(s["rs3_d"], b + 1)
                column_spread(LA[b], lambda t: rs3[b][:, 0, t:t + 1].broadcast_to([128, 128]), s["rb3_p"])

            def k_1x1(b):
                pe.wait_ge(s["f_d"], b + 1)
                nc.tensor.matmul(LB[b][:, 0:N], wg[:, 0:C], fsh[1][b][:, 1:H + 1, :].rearrange("p h w -> p (h w)"),
                                 start=True, stop=True).then_inc(s["k1x1_p"], 1)

            def conv(j, first, last):
                def stage(b):
                    pe.wait_ge(s["conv_w"], TAPS)
                    for n, (dx, dy) in enumerate((dx, dy) for dx in (1, 0, 2) for dy in range(3)):
                        if not first <= n < last:
                            continue
                        if dx == 0:
                            pe.wait_ge(s["f0_d"], b + 1)
                        if dx == 2:
                            pe.wait_ge(s["f2_d"], b + 1)
                        row = dy + j * (H // NT)
                        product = nc.tensor.matmul(LA[b][:, j * C:(j + 1) * C],
                                                   fsh[dx][b][:, row:row + H // NT, :].rearrange("p h w -> p (h w)"),
                                                   convw[:, 3 * dy + dx, :], start=(n == 0), stop=(n == TAPS - 1))
                    if j == NT - 1 and last == TAPS:
                        product.then_inc(s["q3_p"], 1)
                return stage

            def v_1x1(b):
                pe.wait_ge(s["f_d"], b + 1)
                nc.tensor.matmul(LC[b][:, 0:N], wg[:, 2 * C:3 * C], fsh[1][b][:, 1:H + 1, :].rearrange("p h w -> p (h w)"),
                                 start=True, stop=True).then_inc(s["v1x1_p"], 1)

            def v_transposes(b):
                pe.wait_ge(s["vsum_d"], (TAPS - 1) * (b + 1))
                pe.wait_ge(s["pT2o_d"], STEPS // 2)
                for t in range(NT):
                    last = nc.tensor.transpose(LD[b][:, t * C:(t + 1) * C],
                                               vacc[b][:, t * (H // NT):(t + 1) * (H // NT), :].rearrange("p h w -> p (h w)"), ident)
                last.then_inc(s["v3_p"], 1)

            def ek_transposes(b):
                pe.wait_ge(s["ek_d"], b + 1)
                for t in range(NT):
                    last = nc.tensor.transpose(LB[b][:, t * C:(t + 1) * C], ek[b][:, t * 128:(t + 1) * 128], ident)
                last.then_inc(s["ekT_p"], 1)

            def ctx_product(b):
                pe.wait_ge(s["ekT_d"], b + 1)
                pe.wait_ge(s["v3_d"], b + 1)
                for t in range(NT):
                    last = nc.tensor.matmul(LC[b][:, 0:C], ekT[b][:, t, :], v3[b][:, t, :], start=(t == 0), stop=(t == NT - 1))
                last.then_inc(s["ctx_p"], 1)

            def q_transposes(b):
                pe.wait_ge(s["qn_d"], b + 1)
                pe.wait_ge(s["ekT_d"], b + 1)
                for t in range(NT):
                    last = nc.tensor.transpose(LB[b][:, t * 128:(t + 1) * 128],
                                               qn[b][:, t, :, :].rearrange("p h d -> p (h d)"), ident)
                last.then_inc(s["qT_p"], 1)

            def o3_product(b):
                pe.wait_ge(s["cm_d"], b + 1)
                pe.wait_ge(s["qT_d"], b + 1)
                nc.tensor.matmul(LA[b][:, 0:N], cm[b][:, :], qT[b][:, :], start=True, stop=True).then_inc(s["o3_p"], 1)

            def y_products(b):
                pe.wait_ge(s["outw_c"], 1)
                pe.wait_ge(s["s3_d"], b + 1)
                for t in range(NT):
                    last = nc.tensor.matmul(LD[b][:, t * C:(t + 1) * C], s3[b][:, t * 128:(t + 1) * 128], outwc[:, :],
                                            start=True, stop=True)
                last.then_inc(s["yT_p"], 1)
                nc.tensor.matmul(LC[b][:, 0:N], outwc[:, :], s3[b][:, :], start=True, stop=True).then_inc(s["yc_p"], 1)

            def rb4_spread(b):
                pe.wait_ge(s["rs4_d"], b + 1)
                column_spread(LB[b], lambda t: rs3[b][:, 1, t:t + 1].broadcast_to([128, 128]), s["rb4_p"])

            def h_products(b):
                pe.wait_ge(s["x4_d"], b + 1)
                pe.wait_ge(s["w1c_w"], 1)
                for t in range(NT):
                    last = nc.tensor.transpose(LA[b][:, t * C:(t + 1) * C], x4[b][:, t * 128:(t + 1) * 128], ident)
                last.then_inc(s["x4T_p"], 1)
                for t in range(NT):
                    last = nc.tensor.matmul(tiles(LD[b])[:, t, :], x4[b][:, t * 128:(t + 1) * 128], w1c[:, :], start=True, stop=True)
                last.then_inc(s["h_p"], 1)

            def h_transposes(b):
                transposes(LC[b], h3[b], s["hT_p"], s["h_d"], NT * b)

            def ff_product_0(b):
                pe.wait_ge(s["hT_d"], b + 1)
                nc.tensor.matmul(LA[b][:, 0:N], w2c[:, 0, :], hT3[b][:, 0, :], start=True, stop=False)

            def ff_product_1(b):
                nc.tensor.matmul(LA[b][:, 0:N], w2c[:, 1, :], hT3[b][:, 1, :], start=False, stop=True).then_inc(s["ff_p"], 1)

            def rb6_spread(b):
                pe.wait_ge(s["rs6_d"], b + 1)
                column_spread(LB[b], lambda t: rs3[b][:, 3, t:t + 1].broadcast_to([128, 128]), s["rb6_p"])

            keep_in_heads = {10: 2, 11: 3}
            between = {11: rb2_spread, 13: w2_out, 14: x3_transposes, 16: rb3_spread}
            for u in range(STEPS + LAG):
                if u < STEPS:
                    head_scores(u)
                if u == 0:
                    v2_product(1)
                if u in keep_in_heads:
                    keep_clock(keep_in_heads[u], bank[6])
                if u >= LAG:
                    head_transposes(u - LAG)
                if u > LAG and (u - LAG - 1) % HG == HG - 1:
                    group_mix((u - LAG - 1) // HG)
                if u in between:
                    between[u](0)
            for stage, b in ((k_1x1, 0), (v_1x1, 0), (last_mix, 1), (rb2_spread, 1), (conv(0, 0, 5), 0), (w2_out, 1),
                             (conv(0, 5, 8), 0), (x3_transposes, 1), (conv(0, 8, TAPS), 0), (conv(1, 0, 7), 0),
                             (rb3_spread, 1), (conv(1, 7, TAPS), 0), (v_1x1, 1), (k_1x1, 1), (conv(0, 0, TAPS), 1),
                             (ek_transposes, 0), (conv(1, 0, TAPS), 1), (v_transposes, 0), (q_transposes, 0),
                             (keep_before_v, 1), (ctx_product, 0), (ek_transposes, 1), (keep_before_v, 1), (v_transposes, 1),
                             (ctx_product, 1), (q_transposes, 1), (o3_product, 0),
                             (o3_product, 1), (y_products, 0), (y_products, 1), (keep_before_rb4, 1),
                             (rb4_spread, 0), (rb4_spread, 1), (h_products, 0), (h_products, 1), (keep_before_rb6, 1),
                             (h_transposes, 0), (h_transposes, 1),
                             (ff_product_0, 0), (rb6_spread, 0), (ff_product_1, 0), (ff_product_0, 1), (rb6_spread, 1), (ff_product_1, 1)):
                stage(b)



def _embedding():
    import numpy as np
    f = np.float32
    nf = nt = EMB // 4
    ln_x = np.concatenate([np.array([-2.0], f), np.log2(np.arange(1, H * nf, dtype=f))])
    ln_x = ln_x.reshape(H, nf).T * np.arange(1, nf + 1, dtype=f)[:, None]
    freq = np.stack([np.cos(ln_x), np.sin(ln_x)], axis=1).reshape(2 * nf, H).astype(f)
    k = np.arange(0, nt, dtype=f) + f(0.5)
    xs = np.arange(0, nt * W, dtype=f).reshape(W, nt).T
    theta = (k[:, None] * xs / f(W * nt) * f(6.283185307179586)).astype(f)
    time = np.stack([np.cos(theta), np.sin(theta)], axis=1).reshape(2 * nt, W).astype(f)
    freq = np.broadcast_to(freq[:, :, None], (2 * nf, H, W))
    time = np.broadcast_to(time[:, None, :], (2 * nt, H, W))
    return np.concatenate([freq, time], axis=0).reshape(EMB, N)


def _layout(inputs):
    import numpy as np
    g = {k: np.asarray(v) for k, v in inputs.items()}
    f = np.float32

    def pad(w):
        return np.concatenate([w, np.zeros((w.shape[0], QUAD - w.shape[1]), f)], axis=1)

    cols = {
        "ident": np.eye(C, dtype=f),
        "gmean": np.kron(np.eye(C // GN_GROUP, dtype=f), np.full((GN_GROUP, GN_GROUP), 1.0 / GN_GROUP, f)),
        "wqT0": g["L0_conv_wq"].T, "wkT0": g["L0_conv_wk"].T, "wv0": g["L0_conv_wv"], "wpT0": g["L0_conv_wp"].T,
        "gamma": g["L0_conv_gamma"], "beta": g["L0_conv_beta"], "bq0": g["L0_conv_bq"], "bk0": g["L0_conv_bk"],
        "bv0": g["L0_conv_bv"], "bp0": g["L0_conv_bp"], "bq1": g["L1_conv_bq"], "bk1": g["L1_conv_bk"],
        "bv1": g["L1_conv_bv"], "gpam": np.broadcast_to(g["L1_conv_gamma_pam"], (C,)),
        "gcam": np.broadcast_to(g["L1_conv_gamma_cam"], (C,)), "bout": g["L2_conv_bout"],
        "norm_g": g["L3_conv_norm_g"].reshape(C), "out_norm_g": g["L3_conv_out_norm_g"].reshape(C),
        "ff_g1": g["L3_conv_ff_g1"].reshape(C), "ff_g2": g["L3_conv_ff_g2"].reshape(2, C).T,
        "wqkT1": np.concatenate([pad(g["L1_conv_Wq"].T), pad(g["L1_conv_Wk"].T)], axis=1), "wvT1": g["L1_conv_Wv"].T,
        "wqx": g["L2_conv_Wq"][:C], "wkx": g["L2_conv_Wk"][:C], "wqe": g["L2_conv_Wq"][C:], "wke": g["L2_conv_Wk"][C:],
        "emb": _embedding(), "headcol": np.kron(np.eye(HEADS, dtype=f), np.ones((D, 1), f)),
        "wv2": g["L2_conv_Wv"], "wout": g["L2_conv_Wout"],
        "w1x1T": np.concatenate([g["L3_conv_k_w"].T, g["L3_conv_q_w"].T, g["L3_conv_v_w"].T], axis=1),
        "cmean": np.full((C, C), 1.0 / C, f),
        "headmask": np.kron(np.eye(HEADS, dtype=f), np.ones((D, D), f)),
        "kdw": g["L3_conv_k_dw"].reshape(C, TAPS), "vdw": g["L3_conv_v_dw"].reshape(C, TAPS),
        "outwT": g["L3_conv_out_w"].T, "w1T": g["L3_conv_ff_w1"].T,
        "w2T": g["L3_conv_ff_w2"].T.reshape(2, C, C).transpose(1, 0, 2).reshape(C, 2 * C),
    }

    def pack(names):
        at, width = places(names)
        o = np.zeros((128, width), f)
        for name, (lo, hi) in at.items():
            a = cols[name].reshape(cols[name].shape[0], hi - lo)
            o[:a.shape[0], lo:hi] = a
        return o

    taps = g["L3_conv_q_dw"].reshape(C, TAPS).T
    return {"x": g["x"], "pack_a": pack(PACK_A), "pack_b": pack(PACK_B), "pack_c": pack(PACK_C),
            "taps": np.ascontiguousarray(taps.reshape(TAPS * C))}


def kernel(**inputs):
    import numpy as _np
    import concourse.bacc as _bacc
    from concourse import mybir as _mybir
    from concourse.bass_utils import run_bass_kernel_spmd as _run

    nc = _bacc.Bacc("TRN2", target_bir_lowering=False, num_devices=1)
    arrays, args = {}, []
    for name, a in _layout(inputs).items():
        a = _np.ascontiguousarray(a)
        arrays[f"in_{name}"] = a
        args.append(nc.dram_tensor(f"in_{name}", a.shape, _mybir.dt.from_np(a.dtype), kind="ExternalInput").ap())
    args.append(nc.dram_tensor("out_0", (NB, C, H, W), _mybir.dt.float32, kind="ExternalOutput").ap())
    build(nc, *args)
    return _run(nc, [arrays], core_ids=[0]).results[0]["out_0"]
```
